# Optimizing a Trainium2 kernel written in Bass

```python
import numpy as np
import jax
import jax.numpy as jnp

def _softmax(x, axis=-1):
    return jax.nn.softmax(x, axis=axis)

def _gelu(x):
    return jax.nn.gelu(x, approximate=True)

def _silu(x):
    return jax.nn.silu(x)

def _sigmoid(x):
    return jax.nn.sigmoid(x)

def _layernorm(x, axis=-1, eps=1e-05):
    m = jnp.mean(x, axis=axis, keepdims=True)
    v = jnp.var(x, axis=axis, keepdims=True)
    return (x - m) / jnp.sqrt(v + eps)

def _scatter_add(tgt, idx, src, axis=0):
    return tgt.at[idx].add(src)

def _segment_sum(src, seg, n):
    return jax.ops.segment_sum(src, seg, n)
kernel_name = 'mk_audio_tower_d2_tok_audfeat512_r4_4fab04'

def setup_inputs(seed: int=0):
    np.random.seed(seed)
    _w = jnp.asarray

    def _rec_inputs():
        import jax
        import jax.numpy as jnp
        _rk = jax.random.key(seed)
        x = 7.22013e-05 + 1.00017 * jax.random.normal(jax.random.fold_in(_rk, 1), (4, 750, 128), jnp.float32)
        return x
    x = _rec_inputs()

    def _L0_tok_setup():
        import jax, jax.numpy as jnp
        import numpy as np
        B, T, D, H, K = (16, 256, 128, 128, 2)
        key = jax.random.key(seed)
        ks = jax.random.split(key, 7)
        scale = 1.0 / np.sqrt(D * K)
        x = jax.random.normal(ks[0], (B, T, D), dtype=jnp.float32)
        W_z = jax.random.uniform(ks[1], (H, D, K), jnp.float32, -scale, scale)
        b_z = jax.random.uniform(ks[2], (H,), jnp.float32, -scale, scale)
        W_f = jax.random.uniform(ks[3], (H, D, K), jnp.float32, -scale, scale)
        b_f = jax.random.uniform(ks[4], (H,), jnp.float32, -scale, scale)
        W_o = jax.random.uniform(ks[5], (H, D, K), jnp.float32, -scale, scale)
        b_o = jax.random.uniform(ks[6], (H,), jnp.float32, -scale, scale)
        return {'x': x, 'W_z': W_z, 'b_z': b_z, 'W_f': W_f, 'b_f': b_f, 'W_o': W_o, 'b_o': b_o}
    _L0_tok_all = _L0_tok_setup()
    _L0_tok_in = {k: v for k, v in _L0_tok_all.items() if k in ('W_z', 'b_z', 'W_f', 'b_f', 'W_o', 'b_o')}
    del _L0_tok_all

    def _L0_attn_setup():
        import jax, jax.numpy as jnp
        import numpy as np
        import math
        key = jax.random.key(seed)
        ks = jax.random.split(key, 6)
        B, L, D, H, R = (4, 512, 128, 8, 4)
        hd = D // H
        x = jax.random.normal(ks[0], (B, L, D), jnp.float32)
        Wqk = jax.random.normal(ks[1], (D, 2 * D), jnp.float32) * 0.02
        bqk = jnp.zeros((2 * D,), jnp.float32)
        Wv = jax.random.normal(ks[2], (D, D), jnp.float32) * 0.02
        bv = jnp.zeros((D,), jnp.float32)
        Wo = jax.random.normal(ks[3], (D, D), jnp.float32) * 0.02
        bo = jnp.zeros((D,), jnp.float32)
        rotations = jax.random.normal(ks[4], (H, R, hd), jnp.float32) * 0.02
        return {'x': x, 'Wqk': Wqk, 'bqk': bqk, 'Wv': Wv, 'bv': bv, 'Wo': Wo, 'bo': bo, 'rotations': rotations}
    _L0_attn_all = _L0_attn_setup()
    _L0_attn_in = {k: v for k, v in _L0_attn_all.items() if k in ('Wqk', 'bqk', 'Wv', 'bv', 'Wo', 'bo', 'rotations')}
    del _L0_attn_all

    def _L0_ffn_setup():
        import jax, jax.numpy as jnp
        import numpy as np
        from jax import lax
        B, S, IN, D, E, NH = (8, 128, 128, 256, 4, 16)
        DH = D // NH
        EPS = 1e-05
        SCALE = np.float32(1.0 / np.sqrt(DH))

        def _ln(x, g, b):
            m = x.mean(-1, keepdims=True)
            v = ((x - m) ** 2).mean(-1, keepdims=True)
            return (x - m) * lax.rsqrt(v + EPS) * g + b

        def _lstm_dir(x, Wi, Wh, b):
            bsz = x.shape[0]
            h0 = jnp.zeros((bsz, Wh.shape[0]), x.dtype)

            def step(carry, xt):
                h, c = carry
                zg = xt @ Wi + h @ Wh + b
                i, f, g, o = jnp.split(zg, 4, axis=-1)
                c = jax.nn.sigmoid(f) * c + jax.nn.sigmoid(i) * jnp.tanh(g)
                h = jax.nn.sigmoid(o) * jnp.tanh(c)
                return ((h, c), h)
            _, hs = lax.scan(step, (h0, h0), jnp.swapaxes(x, 0, 1))
            return jnp.swapaxes(hs, 0, 1)

        def _expert(x, p):
            ew1, eb1, ew2, eb2, eg, ebeta, aiw, aib, aow, aob, wif, whf, bf, wibk, whbk, bbk, sw1, sb1, sw2, sb2, tw1, tb1, tw2, tb2, dw1, db1, dw2, db2, dg, dbeta = p
            h = _ln(jax.nn.relu(x @ ew1 + eb1) @ ew2 + eb2, eg, ebeta)
            qkv = h @ aiw + aib
            q, k, v = jnp.split(qkv, 3, axis=-1)

            def heads(t):
                return t.reshape(t.shape[0], t.shape[1], NH, DH).transpose(0, 2, 1, 3)
            q, k, v = (heads(q), heads(k), heads(v))
            attn = jax.nn.softmax(jnp.einsum('bhqd,bhkd->bhqk', q, k) * SCALE, axis=-1)
            o = jnp.einsum('bhqk,bhkd->bhqd', attn, v).transpose(0, 2, 1, 3).reshape(h.shape)
            h = o @ aow + aob
            hf = _lstm_dir(h, wif, whf, bf)
            hb = _lstm_dir(h[:, ::-1], wibk, whbk, bbk)[:, ::-1]
            mem = jnp.concatenate([hf, hb], axis=-1)
            gate_s = jax.nn.sigmoid(jax.nn.relu(mem @ sw1 + sb1) @ sw2 + sb2)
            gate_t = jnp.tanh(jax.nn.relu(mem @ tw1 + tb1) @ tw2 + tb2)
            g = gate_s * gate_t
            return _ln(jax.nn.relu(g @ dw1 + db1) @ dw2 + db2, dg, dbeta)

        def _forward(x, router_w, router_b, *p):
            outs = jax.vmap(lambda pe: _expert(x, pe))(tuple(p))
            w = jax.nn.softmax(x @ router_w + router_b, axis=-1)
            return jnp.einsum('ebsd,bse->bsd', outs, w)
        key = jax.random.key(seed)
        ks = iter(jax.random.split(key, 64))

        def rn(shape, scale=0.02):
            return jax.random.normal(next(ks), shape, dtype=jnp.float32) * scale
        z = lambda shape: jnp.zeros(shape, dtype=jnp.float32)
        return {'x': jax.random.normal(next(ks), (B, S, IN), dtype=jnp.float32), 'router_w': rn((IN, E)), 'router_b': z((E,)), 'enc_w1': rn((E, IN, D)), 'enc_b1': z((E, D)), 'enc_w2': rn((E, D, D)), 'enc_b2': z((E, D)), 'enc_g': jnp.ones((E, D), jnp.float32), 'enc_beta': z((E, D)), 'attn_in_w': rn((E, D, 3 * D)), 'attn_in_b': z((E, 3 * D)), 'attn_out_w': rn((E, D, D)), 'attn_out_b': z((E, D)), 'lstm_wi_f': rn((E, D, 4 * D)), 'lstm_wh_f': rn((E, D, 4 * D)), 'lstm_b_f': z((E, 4 * D)), 'lstm_wi_b': rn((E, D, 4 * D)), 'lstm_wh_b': rn((E, D, 4 * D)), 'lstm_b_b': z((E, 4 * D)), 'sig_w1': rn((E, 2 * D, D)), 'sig_b1': z((E, D)), 'sig_w2': rn((E, D, D)), 'sig_b2': z((E, D)), 'tan_w1': rn((E, 2 * D, D)), 'tan_b1': z((E, D)), 'tan_w2': rn((E, D, D)), 'tan_b2': z((E, D)), 'dec_w1': rn((E, D, D)), 'dec_b1': z((E, D)), 'dec_w2': rn((E, D, IN)), 'dec_b2': z((E, IN)), 'dec_g': jnp.ones((E, IN), jnp.float32), 'dec_beta': z((E, IN))}
    _L0_ffn_all = _L0_ffn_setup()
    _L0_ffn_in = {k: v for k, v in _L0_ffn_all.items() if k in ('router_w', 'router_b', 'enc_w1', 'enc_b1', 'enc_w2', 'enc_b2', 'enc_g', 'enc_beta', 'attn_in_w', 'attn_in_b', 'attn_out_w', 'attn_out_b', 'lstm_wi_f', 'lstm_wh_f', 'lstm_b_f', 'lstm_wi_b', 'lstm_wh_b', 'lstm_b_b', 'sig_w1', 'sig_b1', 'sig_w2', 'sig_b2', 'tan_w1', 'tan_b1', 'tan_w2', 'tan_b2', 'dec_w1', 'dec_b1', 'dec_w2', 'dec_b2', 'dec_g', 'dec_beta')}
    del _L0_ffn_all

    def _L1_attn_setup():
        import jax, jax.numpy as jnp
        import numpy as np
        GAMMA = 0.96875
        HIDDEN = 128
        key = jax.random.key(seed)
        kx, kq, kk, kv = jax.random.split(key, 4)
        B, S, H = (8, 512, HIDDEN)
        X = jax.random.normal(kx, (B, S, H), dtype=jnp.float32)
        W_Q = jax.random.normal(kq, (H, H), dtype=jnp.float32) / H
        W_K = jax.random.normal(kk, (H, H), dtype=jnp.float32) / H
        W_V = jax.random.normal(kv, (H, H), dtype=jnp.float32) / H
        return {'X': X, 'W_Q': W_Q, 'W_K': W_K, 'W_V': W_V}
    _L1_attn_all = _L1_attn_setup()
    _L1_attn_in = {k: v for k, v in _L1_attn_all.items() if k in ('W_Q', 'W_K', 'W_V')}
    del _L1_attn_all

    def _L1_ffn_setup():
        import jax, jax.numpy as jnp
        import numpy as np
        from jax import lax
        N, M, DIM, HEADS, TOPK = (4, 512, 128, 8, 16)

        def _split_heads(t, h):
            n, m, c = t.shape
            return t.reshape(n, m, h, c // h).transpose(0, 2, 1, 3).reshape(n * h, m, c // h)
        key = jax.random.key(seed)
        ks = jax.random.split(key, 7)
        f = lambda k, s, sc=1.0: jax.random.normal(k, s, dtype=jnp.float32) * sc
        return {'x': f(ks[0], (N, M, DIM)), 'pos_w': f(ks[1], (DIM, 1, 3), 0.1), 'pos_b': f(ks[2], (DIM,), 0.02), 'qkv_w': f(ks[3], (3 * DIM, DIM), 0.02), 'qkv_b': f(ks[4], (3 * DIM,), 0.02), 'wo_w': f(ks[5], (DIM, DIM), 0.02), 'wo_b': f(ks[6], (DIM,), 0.02)}
    _L1_ffn_all = _L1_ffn_setup()
    _L1_ffn_in = {k: v for k, v in _L1_ffn_all.items() if k in ('pos_w', 'pos_b', 'qkv_w', 'qkv_b', 'wo_w', 'wo_b')}
    del _L1_ffn_all
    return {'x': x, 'L0_tok_W_z': _L0_tok_in['W_z'], 'L0_tok_b_z': _L0_tok_in['b_z'], 'L0_tok_W_f': _L0_tok_in['W_f'], 'L0_tok_b_f': _L0_tok_in['b_f'], 'L0_tok_W_o': _L0_tok_in['W_o'], 'L0_tok_b_o': _L0_tok_in['b_o'], 'L0_attn_Wqk': _L0_attn_in['Wqk'], 'L0_attn_bqk': _L0_attn_in['bqk'], 'L0_attn_Wv': _L0_attn_in['Wv'], 'L0_attn_bv': _L0_attn_in['bv'], 'L0_attn_Wo': _L0_attn_in['Wo'], 'L0_attn_bo': _L0_attn_in['bo'], 'L0_attn_rotations': _L0_attn_in['rotations'], 'L0_ffn_router_w': _L0_ffn_in['router_w'], 'L0_ffn_router_b': _L0_ffn_in['router_b'], 'L0_ffn_enc_w1': _L0_ffn_in['enc_w1'], 'L0_ffn_enc_b1': _L0_ffn_in['enc_b1'], 'L0_ffn_enc_w2': _L0_ffn_in['enc_w2'], 'L0_ffn_enc_b2': _L0_ffn_in['enc_b2'], 'L0_ffn_enc_g': _L0_ffn_in['enc_g'], 'L0_ffn_enc_beta': _L0_ffn_in['enc_beta'], 'L0_ffn_attn_in_w': _L0_ffn_in['attn_in_w'], 'L0_ffn_attn_in_b': _L0_ffn_in['attn_in_b'], 'L0_ffn_attn_out_w': _L0_ffn_in['attn_out_w'], 'L0_ffn_attn_out_b': _L0_ffn_in['attn_out_b'], 'L0_ffn_lstm_wi_f': _L0_ffn_in['lstm_wi_f'], 'L0_ffn_lstm_wh_f': _L0_ffn_in['lstm_wh_f'], 'L0_ffn_lstm_b_f': _L0_ffn_in['lstm_b_f'], 'L0_ffn_lstm_wi_b': _L0_ffn_in['lstm_wi_b'], 'L0_ffn_lstm_wh_b': _L0_ffn_in['lstm_wh_b'], 'L0_ffn_lstm_b_b': _L0_ffn_in['lstm_b_b'], 'L0_ffn_sig_w1': _L0_ffn_in['sig_w1'], 'L0_ffn_sig_b1': _L0_ffn_in['sig_b1'], 'L0_ffn_sig_w2': _L0_ffn_in['sig_w2'], 'L0_ffn_sig_b2': _L0_ffn_in['sig_b2'], 'L0_ffn_tan_w1': _L0_ffn_in['tan_w1'], 'L0_ffn_tan_b1': _L0_ffn_in['tan_b1'], 'L0_ffn_tan_w2': _L0_ffn_in['tan_w2'], 'L0_ffn_tan_b2': _L0_ffn_in['tan_b2'], 'L0_ffn_dec_w1': _L0_ffn_in['dec_w1'], 'L0_ffn_dec_b1': _L0_ffn_in['dec_b1'], 'L0_ffn_dec_w2': _L0_ffn_in['dec_w2'], 'L0_ffn_dec_b2': _L0_ffn_in['dec_b2'], 'L0_ffn_dec_g': _L0_ffn_in['dec_g'], 'L0_ffn_dec_beta': _L0_ffn_in['dec_beta'], 'L1_attn_W_Q': _L1_attn_in['W_Q'], 'L1_attn_W_K': _L1_attn_in['W_K'], 'L1_attn_W_V': _L1_attn_in['W_V'], 'L1_ffn_pos_w': _L1_ffn_in['pos_w'], 'L1_ffn_pos_b': _L1_ffn_in['pos_b'], 'L1_ffn_qkv_w': _L1_ffn_in['qkv_w'], 'L1_ffn_qkv_b': _L1_ffn_in['qkv_b'], 'L1_ffn_wo_w': _L1_ffn_in['wo_w'], 'L1_ffn_wo_b': _L1_ffn_in['wo_b']}

def reference(x, L0_tok_W_z, L0_tok_b_z, L0_tok_W_f, L0_tok_b_f, L0_tok_W_o, L0_tok_b_o, L0_attn_Wqk, L0_attn_bqk, L0_attn_Wv, L0_attn_bv, L0_attn_Wo, L0_attn_bo, L0_attn_rotations, L0_ffn_router_w, L0_ffn_router_b, L0_ffn_enc_w1, L0_ffn_enc_b1, L0_ffn_enc_w2, L0_ffn_enc_b2, L0_ffn_enc_g, L0_ffn_enc_beta, L0_ffn_attn_in_w, L0_ffn_attn_in_b, L0_ffn_attn_out_w, L0_ffn_attn_out_b, L0_ffn_lstm_wi_f, L0_ffn_lstm_wh_f, L0_ffn_lstm_b_f, L0_ffn_lstm_wi_b, L0_ffn_lstm_wh_b, L0_ffn_lstm_b_b, L0_ffn_sig_w1, L0_ffn_sig_b1, L0_ffn_sig_w2, L0_ffn_sig_b2, L0_ffn_tan_w1, L0_ffn_tan_b1, L0_ffn_tan_w2, L0_ffn_tan_b2, L0_ffn_dec_w1, L0_ffn_dec_b1, L0_ffn_dec_w2, L0_ffn_dec_b2, L0_ffn_dec_g, L0_ffn_dec_beta, L1_attn_W_Q, L1_attn_W_K, L1_attn_W_V, L1_ffn_pos_w, L1_ffn_pos_b, L1_ffn_qkv_w, L1_ffn_qkv_b, L1_ffn_wo_w, L1_ffn_wo_b):
    import jax
    import jax.numpy as jnp

    def _L0_tok_ref(x, W_z, b_z, W_f, b_f, W_o, b_o):
        import jax, jax.numpy as jnp
        import numpy as np
        B, T, D, H, K = (16, 256, 128, 128, 2)

        def conv(W, b):
            return jnp.einsum('btd,hd->bth', x[:, :-1, :], W[:, :, 0]) + jnp.einsum('btd,hd->bth', x[:, 1:, :], W[:, :, 1]) + b
        z = jnp.tanh(conv(W_z, b_z))
        f = jax.nn.sigmoid(conv(W_f, b_f))
        o = jax.nn.sigmoid(conv(W_o, b_o))

        def step(c, zfo):
            zt, ft, ot = zfo
            c = ft * c + (1.0 - ft) * zt
            return (c, ot * c)
        c0 = jnp.zeros_like(z[:, 0, :])
        zT = jnp.swapaxes(z, 0, 1)
        fT = jnp.swapaxes(f, 0, 1)
        oT = jnp.swapaxes(o, 0, 1)
        _, h = jax.lax.scan(step, c0, (zT, fT, oT))
        return jnp.swapaxes(h, 0, 1)

    def _L0_attn_ref(x, Wqk, bqk, Wv, bv, Wo, bo, rotations):
        import jax, jax.numpy as jnp
        import numpy as np
        import math
        B, L, D = x.shape
        H = rotations.shape[0]
        hd = D // H
        qk = x @ Wqk + bqk
        q, k = jnp.split(qk, 2, axis=-1)
        v = x @ Wv + bv

        def heads(t):
            return t.reshape(B, L, H, hd).transpose(0, 2, 1, 3)
        q, k, v = (heads(q), heads(k), heads(v))
        rotated = jnp.einsum('bhld,hrd->bhlr', q, rotations)
        buckets = jnp.argmax(jnp.concatenate([rotated, -rotated], axis=-1), axis=-1)
        idx = jnp.argsort(buckets, axis=-1)
        gather = lambda t: jnp.take_along_axis(t, idx[..., None], axis=2)
        sq, sk, sv = (gather(q), gather(k), gather(v))
        dots = jnp.einsum('bhid,bhjd->bhij', sq, sk) / math.sqrt(hd)
        attn = jax.nn.softmax(dots, axis=-1)
        out = jnp.einsum('bhij,bhjd->bhid', attn, sv)
        restore = jnp.argsort(idx, axis=-1)
        out = jnp.take_along_axis(out, restore[..., None], axis=2)
        out = out.transpose(0, 2, 1, 3).reshape(B, L, D)
        return out @ Wo + bo

    def _L0_ffn_ref(x, router_w, router_b, enc_w1, enc_b1, enc_w2, enc_b2, enc_g, enc_beta, attn_in_w, attn_in_b, attn_out_w, attn_out_b, lstm_wi_f, lstm_wh_f, lstm_b_f, lstm_wi_b, lstm_wh_b, lstm_b_b, sig_w1, sig_b1, sig_w2, sig_b2, tan_w1, tan_b1, tan_w2, tan_b2, dec_w1, dec_b1, dec_w2, dec_b2, dec_g, dec_beta):
        import jax, jax.numpy as jnp
        import numpy as np
        from jax import lax
        B, S, IN, D, E, NH = (8, 128, 128, 256, 4, 16)
        DH = D // NH
        EPS = 1e-05
        SCALE = np.float32(1.0 / np.sqrt(DH))

        def _ln(x, g, b):
            m = x.mean(-1, keepdims=True)
            v = ((x - m) ** 2).mean(-1, keepdims=True)
            return (x - m) * lax.rsqrt(v + EPS) * g + b

        def _lstm_dir(x, Wi, Wh, b):
            bsz = x.shape[0]
            h0 = jnp.zeros((bsz, Wh.shape[0]), x.dtype)

            def step(carry, xt):
                h, c = carry
                zg = xt @ Wi + h @ Wh + b
                i, f, g, o = jnp.split(zg, 4, axis=-1)
                c = jax.nn.sigmoid(f) * c + jax.nn.sigmoid(i) * jnp.tanh(g)
                h = jax.nn.sigmoid(o) * jnp.tanh(c)
                return ((h, c), h)
            _, hs = lax.scan(step, (h0, h0), jnp.swapaxes(x, 0, 1))
            return jnp.swapaxes(hs, 0, 1)

        def _expert(x, p):
            ew1, eb1, ew2, eb2, eg, ebeta, aiw, aib, aow, aob, wif, whf, bf, wibk, whbk, bbk, sw1, sb1, sw2, sb2, tw1, tb1, tw2, tb2, dw1, db1, dw2, db2, dg, dbeta = p
            h = _ln(jax.nn.relu(x @ ew1 + eb1) @ ew2 + eb2, eg, ebeta)
            qkv = h @ aiw + aib
            q, k, v = jnp.split(qkv, 3, axis=-1)

            def heads(t):
                return t.reshape(t.shape[0], t.shape[1], NH, DH).transpose(0, 2, 1, 3)
            q, k, v = (heads(q), heads(k), heads(v))
            attn = jax.nn.softmax(jnp.einsum('bhqd,bhkd->bhqk', q, k) * SCALE, axis=-1)
            o = jnp.einsum('bhqk,bhkd->bhqd', attn, v).transpose(0, 2, 1, 3).reshape(h.shape)
            h = o @ aow + aob
            hf = _lstm_dir(h, wif, whf, bf)
            hb = _lstm_dir(h[:, ::-1], wibk, whbk, bbk)[:, ::-1]
            mem = jnp.concatenate([hf, hb], axis=-1)
            gate_s = jax.nn.sigmoid(jax.nn.relu(mem @ sw1 + sb1) @ sw2 + sb2)
            gate_t = jnp.tanh(jax.nn.relu(mem @ tw1 + tb1) @ tw2 + tb2)
            g = gate_s * gate_t
            return _ln(jax.nn.relu(g @ dw1 + db1) @ dw2 + db2, dg, dbeta)

        def _forward(x, router_w, router_b, *p):
            outs = jax.vmap(lambda pe: _expert(x, pe))(tuple(p))
            w = jax.nn.softmax(x @ router_w + router_b, axis=-1)
            return jnp.einsum('ebsd,bse->bsd', outs, w)
        return _forward(x, router_w, router_b, enc_w1, enc_b1, enc_w2, enc_b2, enc_g, enc_beta, attn_in_w, attn_in_b, attn_out_w, attn_out_b, lstm_wi_f, lstm_wh_f, lstm_b_f, lstm_wi_b, lstm_wh_b, lstm_b_b, sig_w1, sig_b1, sig_w2, sig_b2, tan_w1, tan_b1, tan_w2, tan_b2, dec_w1, dec_b1, dec_w2, dec_b2, dec_g, dec_beta)

    def _L1_attn_ref(X, W_Q, W_K, W_V):
        import jax, jax.numpy as jnp
        import numpy as np
        GAMMA = 0.96875
        HIDDEN = 128
        Q = X @ W_Q
        K = X @ W_K
        V = X @ W_V
        S_len = X.shape[1]
        idx = jnp.arange(S_len)
        D = GAMMA ** jnp.abs(idx[None, :] - idx[:, None]).astype(X.dtype)
        scores = jnp.einsum('bsh,bth->bst', Q, K) * D
        ret = jnp.einsum('bst,bth->bsh', scores * jax.nn.sigmoid(scores), V)
        return ret

    def _L1_ffn_ref(x, pos_w, pos_b, qkv_w, qkv_b, wo_w, wo_b):
        import jax, jax.numpy as jnp
        import numpy as np
        from jax import lax
        N, M, DIM, HEADS, TOPK = (4, 512, 128, 8, 16)

        def _split_heads(t, h):
            n, m, c = t.shape
            return t.reshape(n, m, h, c // h).transpose(0, 2, 1, 3).reshape(n * h, m, c // h)
        n, m, c = x.shape
        h = HEADS
        scale = c ** (-0.5)
        pos = lax.conv_general_dilated(x.transpose(0, 2, 1), pos_w, window_strides=(1,), padding=[(1, 1)], feature_group_count=c, dimension_numbers=('NCH', 'OIH', 'NCH'))
        x = x + (pos + pos_b[None, :, None]).transpose(0, 2, 1)
        qkv = x @ qkv_w.T + qkv_b
        q, k, v = jnp.split(qkv, [c, 2 * c], axis=-1)
        q = _split_heads(q, h)
        k = _split_heads(k, h)
        v = _split_heads(v, h)
        qd = lax.stop_gradient(q)
        kd = lax.stop_gradient(k)
        logits = jnp.einsum('bmd,bpd->bmp', qd * scale, kd)
        _, idx = lax.top_k(logits, TOPK)
        gather = jax.vmap(lambda t, i: t[i])
        k_sel = gather(k, idx)
        v_sel = gather(v, idx)
        attn = jax.nn.softmax(jnp.einsum('bmd,bmkd->bmk', q * scale, k_sel), axis=-1)
        out = jnp.einsum('bmk,bmkd->bmd', attn, v_sel)
        d = c // h
        out = out.reshape(n, h, m, d).transpose(0, 2, 1, 3).reshape(n, m, c)
        return out @ wo_w.T + wo_b
    h = _L0_tok_ref(x, L0_tok_W_z, L0_tok_b_z, L0_tok_W_f, L0_tok_b_f, L0_tok_W_o, L0_tok_b_o)
    h = h + _L0_attn_ref(_layernorm(h, axis=-1), L0_attn_Wqk, L0_attn_bqk, L0_attn_Wv, L0_attn_bv, L0_attn_Wo, L0_attn_bo, L0_attn_rotations)
    h = h + _L0_ffn_ref(_layernorm(h, axis=-1), L0_ffn_router_w, L0_ffn_router_b, L0_ffn_enc_w1, L0_ffn_enc_b1, L0_ffn_enc_w2, L0_ffn_enc_b2, L0_ffn_enc_g, L0_ffn_enc_beta, L0_ffn_attn_in_w, L0_ffn_attn_in_b, L0_ffn_attn_out_w, L0_ffn_attn_out_b, L0_ffn_lstm_wi_f, L0_ffn_lstm_wh_f, L0_ffn_lstm_b_f, L0_ffn_lstm_wi_b, L0_ffn_lstm_wh_b, L0_ffn_lstm_b_b, L0_ffn_sig_w1, L0_ffn_sig_b1, L0_ffn_sig_w2, L0_ffn_sig_b2, L0_ffn_tan_w1, L0_ffn_tan_b1, L0_ffn_tan_w2, L0_ffn_tan_b2, L0_ffn_dec_w1, L0_ffn_dec_b1, L0_ffn_dec_w2, L0_ffn_dec_b2, L0_ffn_dec_g, L0_ffn_dec_beta)
    h = h + _L1_attn_ref(_layernorm(h, axis=-1), L1_attn_W_Q, L1_attn_W_K, L1_attn_W_V)
    h = h + _L1_ffn_ref(_layernorm(h, axis=-1), L1_ffn_pos_w, L1_ffn_pos_b, L1_ffn_qkv_w, L1_ffn_qkv_b, L1_ffn_wo_w, L1_ffn_wo_b)
    return h

_drawn_inputs = setup_inputs


def setup_inputs(seed=0):
    import zlib

    import numpy as np

    out = dict(_drawn_inputs(seed))
    spreads = {'L0_attn_bqk': (0.0, 0.8),
     'L0_attn_bv': (0.0, 0.1),
     'L0_attn_bo': (0.0, 0.1),
     'L0_ffn_router_b': (0.0, 0.1),
     'L0_ffn_enc_b1': (0.0, 0.8),
     'L0_ffn_enc_b2': (0.0, 0.8),
     'L0_ffn_enc_g': (1.0, 0.6),
     'L0_ffn_enc_beta': (0.0, 0.8),
     'L0_ffn_attn_in_b': (0.0, 0.8),
     'L0_ffn_attn_out_b': (0.0, 0.8),
     'L0_ffn_lstm_b_f': (0.0, 0.8),
     'L0_ffn_lstm_b_b': (0.0, 0.8),
     'L0_ffn_sig_b1': (0.0, 0.8),
     'L0_ffn_sig_b2': (0.0, 0.8),
     'L0_ffn_tan_b1': (0.0, 0.8),
     'L0_ffn_tan_b2': (0.0, 0.473),
     'L0_ffn_dec_b1': (0.0, 0.1),
     'L0_ffn_dec_b2': (0.0, 0.1),
     'L0_ffn_dec_g': (1.0, 0.2),
     'L0_ffn_dec_beta': (0.0, 0.1)}
    factors = {'L0_tok_b_f': 8.0,
     'L0_tok_b_o': 8.0,
     'L0_attn_Wqk': 8.0,
     'L0_attn_Wv': 3.287,
     'L0_attn_rotations': 64.0,
     'L0_ffn_enc_w1': 8.0,
     'L0_ffn_enc_w2': 8.0,
     'L0_ffn_attn_in_w': 8.0,
     'L0_ffn_attn_out_w': 8.0,
     'L0_ffn_lstm_wi_f': 8.0,
     'L0_ffn_lstm_wh_f': 8.0,
     'L0_ffn_lstm_wi_b': 8.0,
     'L0_ffn_lstm_wh_b': 8.0,
     'L0_ffn_sig_w1': 8.0,
     'L0_ffn_sig_w2': 8.0,
     'L0_ffn_tan_w1': 8.0,
     'L0_ffn_tan_w2': 7.366,
     'L1_ffn_pos_w': 4.144,
     'L1_ffn_pos_b': 33.594,
     'L1_ffn_qkv_b': 7.51}
    for name, (base, spread) in spreads.items():
        noise = np.random.default_rng([zlib.crc32(name.encode()), seed]).standard_normal(out[name].shape)
        drawn = base * np.exp(spread * noise) if base else spread * noise
        out[name] = jnp.asarray(drawn.astype(out[name].dtype))
    for name, factor in factors.items():
        out[name] = (out[name] * factor).astype(out[name].dtype)
    return out
```

```python
from contextlib import ExitStack

import concourse.bass as bass
from concourse import mybir

ALU = mybir.AluOpType
ACT = mybir.ActivationFunctionType
F32 = mybir.dt.float32
F16 = mybir.dt.float16
BF16 = mybir.dt.bfloat16
AX = mybir.AxisListType.X

P = 128
B, T, E = 4, 749, 4
D_EXPERT = 2 * P
BANK = 512
HD = 16
EPS = 1e-5
COLS_OF = ((0, BANK), (BANK, T))

QUAD = 4
TILES = -(-T // P)
Q_START = [min(P * t, T - P) for t in range(TILES)]
K_SIZE = [min(P, T - P * t) for t in range(TILES)]
HALF = 3 * P
Q_PARTS = (0, 0, 0, 1, 1, 2)
K_PARTS = (0, 1, 2, 0, 1, 0)
STACK = HD * len(Q_PARTS)
TAKEN = -2.0 ** 126

S = 7
GC = 32
COLS = (0, 1, 2, 3, 6, 7, 4, 5)
PIECES = ((0, 4), (4, 7))
CT = 107
CW = CT * B


def start_from_one(nc, sems):
    for s in sems:
        for each in s if isinstance(s, list) else (s,):
            for one in each if isinstance(each, list) else (each,):
                nc.gpsimd.sem_inc(one, 1)
    nc.all_engine_barrier()


def end_stage(nc, sems):
    nc.clear_and_free_semaphores(sems)
    nc.all_engine_barrier()


def stage_tok(nc, x, w_tok, b_tok, h_out):
    with ExitStack() as ctx:
        sems = []
        ctx.callback(end_stage, nc, sems)
        sb = lambda n, shape, dt=F32: ctx.enter_context(nc.sbuf_tensor(f"tok_{n}", shape, dt))

        def sem(n):
            sems.append(nc.alloc_semaphore(f"tok_{n}"))
            return sems[-1]

        x_sb = sb("x", [P, B, T + 1])
        w_sb = sb("w", [P, 3, 2, P])
        b_sb = sb("b", [P, 3])
        gate = sb("gate", [P, 2, 3, T])
        fz = sb("fz", [P, 2, T])
        inp = sb("inp", [P, 2, T])
        cell = sb("cell", [P, 2, T])
        h_sb = sb("h", [P, 2, T])
        g_ps = [ctx.enter_context(nc.psum_tensor(f"tok_g_ps{g}", [P, 2 * BANK], F32)) for g in range(3)]
        w_loaded = sem("w_loaded")
        x_loaded = [sem(f"x_loaded{b}") for b in range(B)]
        gate_mm = sem("gate_mm")
        gate_out = sem("gate_out")
        step = sem("step")
        stored = [sem(f"stored{k}") for k in range(2)]
        block = ctx.enter_context(nc.Block())

        @block.sync
        def _(sp):
            sp.dma_start(w_sb[:], w_tok).then_inc(w_loaded, 16)
            sp.dma_start(b_sb[:], b_tok).then_inc(w_loaded, 16)
            for b in range(B):
                sp.dma_start(x_sb[:, b], x[:, b]).then_inc(x_loaded[b], 16)
            for b in range(B):
                sp.wait_ge(step, 4 * b + 4)
                sp.dma_start(h_out[:, b], h_sb[:, b % 2]).then_inc(stored[b % 2], 16)
            for k in range(2):
                sp.wait_ge(stored[k], 16 * (B // 2))

        @block.tensor
        def _(pe):
            pe.wait_ge(w_loaded, 32)
            for b in range(B):
                pe.wait_ge(x_loaded[b], 16)
                for g in range(3):
                    if b:
                        pe.wait_ge(gate_out, 3 * (b - 1) + g + 1)
                    for lo, hi in COLS_OF:
                        for tap in range(2):
                            mm = nc.tensor.matmul(g_ps[g][:, lo:hi], w_sb[:, g, tap], x_sb[:, b, lo + tap:hi + tap],
                                                  start=(tap == 0), stop=(tap == 1))
                    mm.then_inc(gate_mm, 1)

        @block.scalar
        def _(act):
            for b in range(B):
                for g in range(3):
                    act.wait_ge(gate_mm, 3 * b + g + 1)
                    if b >= 2 and g == 0:
                        act.wait_ge(step, 4 * (b - 2) + 4)
                    nc.scalar.activation(gate[:, b % 2, g], g_ps[g][:, 0:T], ACT.Tanh if g == 0 else ACT.Sigmoid,
                                         bias=b_sb[:, g:g + 1]).then_inc(gate_out, 1)

        @block.vector
        def _(dve):
            for b in range(B):
                k = b % 2
                dve.wait_ge(gate_out, 3 * b + 3)
                nc.vector.tensor_tensor(fz[:, k], gate[:, k, 1], gate[:, k, 0], ALU.mult).then_inc(step, 1)
                dve.wait_ge(step, 4 * b + 1)
                nc.vector.tensor_tensor(inp[:, k], gate[:, k, 0], fz[:, k], ALU.subtract).then_inc(step, 1)
                dve.wait_ge(step, 4 * b + 2)
                nc.vector.tensor_tensor_scan(cell[:, k], gate[:, k, 1], inp[:, k], 0.0, ALU.mult, ALU.add).then_inc(step, 1)
                dve.wait_ge(step, 4 * b + 3)
                if b >= 2:
                    dve.wait_ge(stored[k], 16 * (b // 2))
                nc.vector.tensor_tensor(h_sb[:, k], gate[:, k, 2], cell[:, k], ALU.mult).then_inc(step, 1)


def stage_norm(nc, name, h_in, n_out, o_in=None, w_o=None, cols=None, h_out=None, conv=False):
    with ExitStack() as ctx:
        sems = []
        ctx.callback(end_stage, nc, sems)
        sb = lambda n, shape, dt=F32: ctx.enter_context(nc.sbuf_tensor(f"{name}_{n}", shape, dt))

        def sem(n):
            sems.append(nc.alloc_semaphore(f"{name}_{n}"))
            return sems[-1]

        norm = n_out is not None
        h_sb = sb("h", [P, B, T])
        col_sb = sb("cols", [P, 5])
        avg = sb("avg", [P, P])
        eps_sb = sb("eps", [P, 1])
        d_sb = sb("d", [P, 2, T])
        sq = sb("sq", [P, 2, T])
        r_sb = sb("r", [P, 2, T])
        n_sb = sb("n", [P, 2, T + 2])
        y_sb = sb("y", [P, 2, T])
        o_sb = sb("o", [P, B, T])
        w_sb = sb("w", [P, P])
        o_ps = [ctx.enter_context(nc.psum_tensor(f"{name}_o_ps{k}", [P, 2 * BANK], F32)) for k in range(2)]
        m_ps = ctx.enter_context(nc.psum_tensor(f"{name}_m_ps", [P, 2 * BANK], F32))
        v_ps = ctx.enter_context(nc.psum_tensor(f"{name}_v_ps", [P, 2 * BANK], F32))
        w_loaded = sem("w_loaded")
        loaded = [sem(f"loaded{b}") for b in range(B)]
        o_mm = sem("o_mm")
        h_done = sem("h_done")
        mean_mm = sem("mean_mm")
        d_done = sem("d_done")
        sq_done = sem("sq_done")
        var_mm = sem("var_mm")
        root_done = sem("root_done")
        r_done = sem("r_done")
        n_done = sem("n_done")
        conv_step = sem("conv_step")
        ready = sem("ready")
        edge_done = sem("edge_done")
        h_stored = sem("h_stored")
        n_stored = [sem(f"n_stored{k}") for k in range(2)]
        LOADS = 32 if o_in is not None else 16
        block = ctx.enter_context(nc.Block())

        @block.sync
        def _(sp):
            if cols is not None:
                sp.dma_start(col_sb[:], cols).then_inc(w_loaded, 16)
            if o_in is not None:
                sp.dma_start(w_sb[:], w_o).then_inc(w_loaded, 16)
            for b in range(B):
                sp.dma_start(h_sb[:, b], h_in[:, b]).then_inc(loaded[b], 16)
                if o_in is not None:
                    sp.dma_start(o_sb[:, b], o_in[b]).then_inc(loaded[b], 16)
            for b in range(B):
                if h_out is not None:
                    sp.wait_ge(h_done, b + 1)
                    sp.dma_start(h_out[:, b], h_sb[:, b]).then_inc(h_stored, 16)
                if norm:
                    sp.wait_ge(ready, b + 1)
                    sp.dma_start(n_out[:, b], (y_sb if conv else n_sb)[:, b % 2, 0:T] if conv else n_sb[:, b % 2, 1:T + 1]
                                 ).then_inc(n_stored[b % 2], 16)
            if h_out is not None:
                sp.wait_ge(h_stored, 16 * B)
            if norm:
                for k in range(2):
                    sp.wait_ge(n_stored[k], 16 * (B // 2))

        @block.tensor
        def _(pe):
            def project(b):
                if b == 0:
                    pe.wait_ge(w_loaded, 32)
                pe.wait_ge(loaded[b], LOADS)
                if b >= 2:
                    pe.wait_ge(h_done, b - 1)
                for lo, hi in COLS_OF:
                    mm = nc.tensor.matmul(o_ps[b % 2][:, lo:hi], w_sb[:], o_sb[:, b, lo:hi], start=True, stop=True)
                mm.then_inc(o_mm, 1)
            if o_in is not None:
                project(0)
            if norm:
                pe.wait_ge(edge_done, 1)
            for b in range(B):
                if o_in is not None and b + 1 < B:
                    project(b + 1)
                if not norm:
                    continue
                if o_in is not None:
                    pe.wait_ge(h_done, b + 1)
                else:
                    pe.wait_ge(loaded[b], LOADS)
                if b:
                    pe.wait_ge(d_done, b)
                for lo, hi in COLS_OF:
                    mm = nc.tensor.matmul(m_ps[:, lo:hi], avg[:], h_sb[:, b, lo:hi], start=True, stop=True)
                mm.then_inc(mean_mm, 1)
                pe.wait_ge(sq_done, b + 1)
                if b:
                    pe.wait_ge(root_done, b)
                for lo, hi in COLS_OF:
                    mm = nc.tensor.matmul(v_ps[:, lo:hi], avg[:], sq[:, b % 2, lo:hi], start=True, stop=True)
                mm.then_inc(var_mm, 1)

        @block.scalar
        def _(act):
            if norm:
                act.wait_ge(edge_done, 1)
            for b in range(B if norm else 0):
                act.wait_ge(d_done, b + 1)
                if b >= 2:
                    act.wait_ge(var_mm, b - 1)
                nc.scalar.activation(sq[:, b % 2], d_sb[:, b % 2], ACT.Square).then_inc(sq_done, 1)
                act.wait_ge(var_mm, b + 1)
                if b >= 2:
                    act.wait_ge(ready, b - 1)
                nc.scalar.activation(r_sb[:, b % 2], v_ps[:, 0:T], ACT.Sqrt, bias=eps_sb[:]).then_inc(root_done, 1)

        @block.vector
        def _(dve):
            nc.vector.memset(avg[:], 1.0 / P)
            nc.vector.memset(eps_sb[:], EPS)
            nc.vector.memset(n_sb[:], 0.0).then_inc(edge_done, 1)
            dve.wait_ge(edge_done, 1)
            if cols is not None:
                dve.wait_ge(w_loaded, LOADS)
            for b in range(B):
                k = b % 2
                if o_in is not None:
                    dve.wait_ge(o_mm, b + 1)
                    dve.wait_ge(loaded[b], LOADS)
                    nc.vector.scalar_tensor_tensor(h_sb[:, b], o_ps[k][:, 0:T], col_sb[:, 0:1], h_sb[:, b],
                                                   ALU.add, ALU.add).then_inc(h_done, 1)
                if not norm:
                    continue
                dve.wait_ge(mean_mm, b + 1)
                nc.vector.tensor_tensor(d_sb[:, k], h_sb[:, b], m_ps[:, 0:T], ALU.subtract).then_inc(d_done, 1)
                dve.wait_ge(root_done, b + 1)
                nc.vector.reciprocal(r_sb[:, k], r_sb[:, k]).then_inc(r_done, 1)
                dve.wait_ge(r_done, b + 1)
                if b >= 2:
                    dve.wait_ge(n_stored[k], 16 * (b // 2))
                done = n_done if conv else ready
                nc.vector.tensor_tensor(n_sb[:, k, 1:T + 1], d_sb[:, k], r_sb[:, k], ALU.mult).then_inc(done, 1)
                if conv:
                    dve.wait_ge(n_done, b + 1)
                    nc.vector.tensor_scalar(y_sb[:, k], n_sb[:, k, 0:T], col_sb[:, 2:3], col_sb[:, 1:2],
                                            ALU.mult, ALU.add).then_inc(conv_step, 1)
                    for tap in (1, 2):
                        dve.wait_ge(conv_step, 3 * b + tap)
                        nc.vector.scalar_tensor_tensor(y_sb[:, k], n_sb[:, k, tap:T + tap], col_sb[:, 2 + tap:3 + tap],
                                                       y_sb[:, k], ALU.mult, ALU.add).then_inc(conv_step, 1)
                    dve.wait_ge(conv_step, 3 * b + 3)
                    nc.vector.tensor_tensor(y_sb[:, k], n_sb[:, k, 1:T + 1], y_sb[:, k], ALU.add).then_inc(ready, 1)


def stage_qkv(nc, name, src, w_qkv, cols, v_bias, q_parts, k_parts, v_aug, experts, heads, scale):
    KC = src.shape[1]
    F = heads * HD
    MC = F // P
    G = heads // 4
    TT = [(lo, min(lo + P, T)) for lo in range(0, T, P)]
    NT = len(TT)
    U = B * G
    with ExitStack() as ctx:
        sems = []
        ctx.callback(end_stage, nc, sems)
        sb = lambda n, shape, dt=F32: ctx.enter_context(nc.sbuf_tensor(f"{name}_{n}", shape, dt))

        def sem(n):
            sems.append(nc.alloc_semaphore(f"{name}_{n}"))
            return sems[-1]

        w_sb = sb("w", [P, experts, KC, 3 * F])
        col_sb = sb("cols", [P, experts, 2 * MC])
        vb_sb = sb("vb", [P, experts, F])
        s_sb = sb("s", [P, 2, KC, T])
        whole = sb("whole", [P, 2, T])
        rest = sb("rest", [P, 2, T])
        part = sb("part", [P, 2, 3, T], BF16)
        v_sb = sb("v", [P, 2, G, 4, 2 * HD])
        qk_ps = [ctx.enter_context(nc.psum_tensor(f"{name}_qk_ps{k}", [P, 2 * BANK], F32)) for k in range(2)]
        v_ps = [ctx.enter_context(nc.psum_tensor(f"{name}_v_ps{k}", [P, BANK], F32)) for k in range(2)]
        w_loaded = sem("w_loaded")
        s_loaded = [sem(f"s_loaded{k}") for k in range(2)]
        qk_mm = sem("qk_mm")
        whole_done = sem("whole_done")
        part_done = [sem(f"part{p}_done") for p in range(3)]
        rest_done = sem("rest_done")
        part_stored = [sem(f"part_stored{k}") for k in range(2)]
        v_mm = sem("v_mm")
        v_done = sem("v_done")
        v_stored = [sem(f"v_stored{k}") for k in range(2)]
        ones_done = sem("ones_done")
        QK = 2 * MC
        start_from_one(nc, (part_stored, v_done, v_stored, whole_done,))
        block = ctx.enter_context(nc.Block())
        JOBS = 2 * experts
        trips = B // 2

        def put_source(sp, n, i):
            bb, e = divmod(n, experts)
            sp.dma_start(s_sb[:, n % 2], src[e].rearrange("k p b t -> p k b t")[:, :, bass.ds(2 * i + bb, 1), :]
                         .rearrange("p k o t -> p k (o t)")).then_inc(s_loaded[n % 2], 16)

        @block.sync
        def _(sp):
            for e in range(experts):
                sp.dma_start(w_sb[:, e], w_qkv[e].rearrange("(k p) n -> p k n", p=P)).then_inc(w_loaded, 16)
                sp.dma_start(col_sb[:, e], cols[e]).then_inc(w_loaded, 16)
                sp.dma_start(vb_sb[:, e], v_bias[e:e + 1].partition_broadcast(P)).then_inc(w_loaded, 16)
            put_source(sp, 0, 0)
            put_source(sp, 1, 0)

            def trip(i, last):
                for n in range(JOBS):
                    job = i * JOBS + n
                    bb, e = divmod(n, experts)
                    u = (2 * i + bb) * G + e * U
                    u = u if last else sp.snap(u)
                    for m in range(max(QK, NT)):
                        if m < QK:
                            dst = q_parts if m < MC else k_parts
                            g = 2 * (m % MC)
                            sp.wait_ge(part_done[2], QK * job + m + 1)
                            for half in range(2):
                                sp.dma_start(dst[bass.ds(u + g + half, 1)].rearrange("o s r t -> r (o s) t"),
                                               part[half * 64:half * 64 + 64, m % 2]).then_inc(part_stored[m % 2], 16)
                        if m < NT:
                            lo, hi = TT[m]
                            sp.wait_ge(v_done, NT * job + m + 2)
                            sp.dma_start(v_aug[bass.ds(u, G), lo:hi].rearrange("g t n -> t g n"),
                                         v_sb[0:hi - lo, m % 2].rearrange("p g h d -> p g (h d)")).then_inc(v_stored[m % 2], 16)
                    if n + 2 < JOBS:
                        put_source(sp, n + 2, i)
                    elif not last:
                        put_source(sp, n + 2 - JOBS, i + 1)
            if trips > 1:
                with sp.Fori(0, trips - 1) as i:
                    trip(i, False)
            trip(trips - 1, True)
            for k in range(2):
                sp.wait_ge(part_stored[k], 32 * (QK // 2) * JOBS * trips + 1)
                sp.wait_ge(v_stored[k], 16 * (NT // 2) * JOBS * trips + 1)

        @block.tensor
        def _(pe):
            pe.wait_ge(w_loaded, 48 * experts)
            with pe.Fori(0, trips) as i:
                for n in range(JOBS):
                    bb, e = divmod(n, experts)
                    job = i * JOBS + n
                    pe.wait_ge(s_loaded[n % 2], i * (16 * (JOBS // 2)) + 16 * (n // 2 + 1))
                    for m in range(max(QK, NT)):
                        if m < QK:
                            if n or m >= 2:
                                pe.wait_ge(whole_done, QK * job + m)
                            else:
                                pe.wait_ge(whole_done, QK * job + 1)
                            for lo, hi in COLS_OF:
                                for c in range(KC):
                                    mm = nc.tensor.matmul(qk_ps[m % 2][:, lo:hi], w_sb[:, e, c, m * P:(m + 1) * P],
                                                          s_sb[:, n % 2, c, lo:hi], start=(c == 0), stop=(c == KC - 1))
                            mm.then_inc(qk_mm, 1)
                        if m < NT:
                            lo, hi = TT[m]
                            if n or m >= 2:
                                pe.wait_ge(v_done, NT * job + m)
                            else:
                                pe.wait_ge(v_done, NT * job + 1)
                            for c in range(KC):
                                mm = nc.tensor.matmul(v_ps[m % 2][0:hi - lo, 0:F], s_sb[:, n % 2, c, lo:hi],
                                                      w_sb[:, e, c, 2 * F:3 * F], start=(c == 0), stop=(c == KC - 1))
                            mm.then_inc(v_mm, 1)

        @block.scalar
        def _(act):
            with act.Fori(0, trips) as i:
                for n in range(JOBS):
                    job = i * JOBS + n
                    for m in range(QK):
                        count = QK * job + m + 1
                        k = m % 2
                        act.wait_ge(whole_done, count + 1)
                        act.wait_ge(part_stored[k], 32 * ((QK // 2) * job + m // 2) + 1)
                        nc.scalar.activation(part[:, k, 0], whole[:, k], ACT.Copy).then_inc(part_done[0], 1)
                        act.wait_ge(rest_done, count)
                        nc.scalar.activation(part[:, k, 1], rest[:, k], ACT.Copy).then_inc(part_done[1], 1)

        @block.vector
        def _(dve):
            nc.vector.memset(v_sb[:], 1.0).then_inc(ones_done, 1)
            dve.wait_ge(ones_done, 1)
            dve.wait_ge(w_loaded, 48 * experts)
            with dve.Fori(0, trips) as i:
                for n in range(JOBS):
                    bb, e = divmod(n, experts)
                    job = i * JOBS + n

                    def last_part(m):
                        k = m % 2
                        dve.wait_ge(part_done[1], QK * job + m + 1)
                        nc.vector.tensor_tensor(part[:, k, 2], rest[:, k], part[:, k, 1], ALU.subtract
                                                ).then_inc(part_done[2], 1)

                    for m in range(max(QK, NT)):
                        if m < QK:
                            k = m % 2
                            dve.wait_ge(qk_mm, QK * job + m + 1)
                            nc.vector.tensor_scalar(whole[:, k], qk_ps[k][:, 0:T], col_sb[:, e, m:m + 1],
                                                    scale if m < MC else 1.0, ALU.add, ALU.mult).then_inc(whole_done, 1)
                        if m < NT:
                            lo, hi = TT[m]
                            dve.wait_ge(v_mm, NT * job + m + 1)
                            dve.wait_ge(v_stored[m % 2], 16 * ((NT // 2) * job + m // 2) + 1)
                            nc.vector.tensor_tensor(v_sb[0:hi - lo, m % 2, :, :, 0:HD],
                                                    v_ps[m % 2][0:hi - lo, 0:F].rearrange("p (g h d) -> p g h d", g=G, h=4),
                                                    vb_sb[0:hi - lo, e].rearrange("p (g h d) -> p g h d", g=G, h=4), ALU.add
                                                    ).then_inc(v_done, 1)
                        if m < QK:
                            dve.wait_ge(part_done[0], QK * job + m + 1)
                            nc.vector.tensor_tensor(rest[:, k], whole[:, k], part[:, k, 0], ALU.subtract).then_inc(rest_done, 1)
                            last_part(m)


def stage_encode(nc, n_in, w1, w2, cols, e_out):
    D = D_EXPERT
    with ExitStack() as ctx:
        sems = []
        ctx.callback(end_stage, nc, sems)
        sb = lambda n, shape, dt=F32: ctx.enter_context(nc.sbuf_tensor(f"enc_{n}", shape, dt))

        def sem(n):
            sems.append(nc.alloc_semaphore(f"enc_{n}"))
            return sems[-1]

        w1_sb = sb("w1", [P, E, D])
        w2_sb = sb("w2", [P, E, 2, D])
        col_sb = sb("cols", [P, E, 8])
        avg = sb("avg", [P, P])
        eps_sb = sb("eps", [P, 1])
        n_sb = sb("n", [P, T])
        a_sb = sb("a", [P, 2, 2, T])
        x_sb = sb("x", [P, 2, 2, T])
        sq = sb("sq", [P, 2, T])
        r_sb = sb("r", [P, T])
        h_sb = sb("h", [P, 2, 2, T])
        a_ps = [ctx.enter_context(nc.psum_tensor(f"enc_a_ps{k}", [P, 2 * BANK], F32)) for k in range(2)]
        m_ps = ctx.enter_context(nc.psum_tensor("enc_m_ps", [P, 2 * BANK], F32))
        w_loaded = sem("w_loaded")
        n_loaded = sem("n_loaded")
        const_done = sem("const_done")
        a_mm, a_out, x_mm, x_out = sem("a_mm"), sem("a_out"), sem("x_mm"), sem("x_out")
        mean_mm, var_mm = sem("mean_mm"), sem("var_mm")
        d_done, sq_done, y_done, h_done = sem("d_done"), sem("sq_done"), sem("y_done"), sem("h_done")
        root_done, r_done = sem("root_done"), sem("r_done")
        stored = [sem(f"stored{k}") for k in range(2)]
        start_from_one(nc, (a_mm, root_done, stored, var_mm, x_out, y_done,))
        block = ctx.enter_context(nc.Block())

        @block.sync
        def _(sp):
            for e in range(E):
                sp.dma_start(w1_sb[:, e], w1[e]).then_inc(w_loaded, 16)
                sp.dma_start(w2_sb[:, e], w2[e].rearrange("(k p) n -> p k n", p=P)).then_inc(w_loaded, 16)
                sp.dma_start(col_sb[:, e], cols[e]).then_inc(w_loaded, 16)
            with sp.Fori(0, B) as i:
                sp.wait_ge(a_mm, i * (2 * E) + 1)
                sp.dma_start(n_sb[:], n_in[:, bass.ds(i, 1)].rearrange("p o t -> p (o t)")).then_inc(n_loaded, 16)
                for e in range(E):
                    sp.wait_ge(h_done, (i * E + e) * 2 + 2)
                    sp.dma_start(e_out[e].rearrange("c p b t -> p c b t")[:, :, bass.ds(i, 1)].rearrange("p c o t -> p c (o t)"),
                                 h_sb[:, e % 2]).then_inc(stored[e % 2], 16)
            for k in range(2):
                sp.wait_ge(stored[k], 16 * (E // 2) * B + 1)

        @block.tensor
        def _(pe):
            pe.wait_ge(w_loaded, 48 * E)
            pe.wait_ge(const_done, 1)
            with pe.Fori(0, B) as i:
                def first(e):
                    for m in range(2):
                        pe.wait_ge(x_out, ((i * E + e - 1) * 2 + m + 1 if e else i * (E * 2)) + 1)
                        for lo, hi in COLS_OF:
                            mm = nc.tensor.matmul(a_ps[m][:, lo:hi], w1_sb[:, e, m * P:(m + 1) * P], n_sb[:, lo:hi],
                                                  start=True, stop=True)
                        mm.then_inc(a_mm, 1)

                def second(e):
                    for m in range(2):
                        pe.wait_ge(a_out, (i * E + e) * 2 + 2)
                        for lo, hi in COLS_OF:
                            for c in range(2):
                                mm = nc.tensor.matmul(a_ps[m][:, lo:hi], w2_sb[:, e, c, m * P:(m + 1) * P],
                                                      a_sb[:, e % 2, c, lo:hi], start=(c == 0), stop=(c == 1))
                        mm.then_inc(x_mm, 1)

                def mean(e):
                    pe.wait_ge(x_out, (i * E + e) * 2 + 3)
                    pe.wait_ge(root_done, i * E + e + 1)
                    for lo, hi in COLS_OF:
                        for c in range(2):
                            mm = nc.tensor.matmul(m_ps[:, lo:hi], avg[:], x_sb[:, e % 2, c, lo:hi], start=(c == 0), stop=(c == 1))
                    mm.then_inc(mean_mm, 1)

                def variance(e):
                    pe.wait_ge(sq_done, (i * E + e) * 2 + 2)
                    for lo, hi in COLS_OF:
                        for c in range(2):
                            mm = nc.tensor.matmul(m_ps[:, lo:hi], avg[:], sq[:, c, lo:hi], start=(c == 0), stop=(c == 1))
                    mm.then_inc(var_mm, 1)

                pe.wait_ge(n_loaded, i * 16 + 16)
                first(0)
                second(0)
                first(1)
                for e in range(E):
                    mean(e)
                    if e + 1 < E:
                        second(e + 1)
                    variance(e)
                    if e + 2 < E:
                        first(e + 2)

        @block.scalar
        def _(act):
            act.wait_ge(const_done, 1)
            act.wait_ge(w_loaded, 48 * E)
            with act.Fori(0, B) as i:
                def hidden(e):
                    for m in range(2):
                        act.wait_ge(a_mm, (i * E + e) * 2 + m + 2)
                        nc.scalar.activation(a_sb[:, e % 2, m], a_ps[m][:, 0:T], ACT.Relu, bias=col_sb[:, e, m:m + 1]
                                             ).then_inc(a_out, 1)

                hidden(0)
                for e in range(E):
                    for m in range(2):
                        act.wait_ge(x_mm, (i * E + e) * 2 + m + 1)
                        if e >= 2:
                            act.wait_ge(y_done, (i * E + e - 2) * 2 + 3)
                        nc.scalar.activation(x_sb[:, e % 2, m], a_ps[m][:, 0:T], ACT.Identity, bias=col_sb[:, e, 2 + m:3 + m]
                                             ).then_inc(x_out, 1)
                    if e + 1 < E:
                        hidden(e + 1)
                    for m in range(2):
                        act.wait_ge(d_done, (i * E + e) * 2 + m + 1)
                        act.wait_ge(var_mm, i * E + e + 1)
                        nc.scalar.activation(sq[:, m], x_sb[:, e % 2, m], ACT.Square).then_inc(sq_done, 1)
                    act.wait_ge(var_mm, i * E + e + 2)
                    act.wait_ge(y_done, (i * E + e) * 2 + 1)
                    nc.scalar.activation(r_sb[:], m_ps[:, 0:T], ACT.Sqrt, bias=eps_sb[:]).then_inc(root_done, 1)
                    for m in range(2):
                        act.wait_ge(y_done, (i * E + e) * 2 + m + 2)
                        act.wait_ge(stored[e % 2], i * (16 * E // 2) + 16 * (e // 2) + 1)
                        nc.scalar.activation(h_sb[:, e % 2, m], x_sb[:, e % 2, m], ACT.Identity, bias=col_sb[:, e, 6 + m:7 + m],
                                             scale=col_sb[:, e, 4 + m:5 + m]).then_inc(h_done, 1)

        @block.vector
        def _(dve):
            nc.vector.memset(eps_sb[:], EPS)
            nc.vector.memset(avg[:], 1.0 / D).then_inc(const_done, 1)
            with dve.Fori(0, B) as i:
                for e in range(E):
                    dve.wait_ge(mean_mm, i * E + e + 1)
                    for m in range(2):
                        nc.vector.tensor_tensor(x_sb[:, e % 2, m], x_sb[:, e % 2, m], m_ps[:, 0:T], ALU.subtract
                                                ).then_inc(d_done, 1)
                    dve.wait_ge(root_done, i * E + e + 2)
                    nc.vector.reciprocal(r_sb[:], r_sb[:]).then_inc(r_done, 1)
                    dve.wait_ge(r_done, i * E + e + 1)
                    dve.wait_ge(sq_done, (i * E + e) * 2 + 2)
                    for m in range(2):
                        nc.vector.tensor_tensor(x_sb[:, e % 2, m], x_sb[:, e % 2, m], r_sb[:], ALU.mult).then_inc(y_done, 1)




def stage_lstm_inputs(nc, o_in, w_o, w_i, cols, xw):
    D = D_EXPERT
    with ExitStack() as ctx:
        sems = []
        ctx.callback(end_stage, nc, sems)
        sb = lambda n, shape, dt=F32: ctx.enter_context(nc.sbuf_tensor(f"xw_{n}", shape, dt))

        def sem(n):
            sems.append(nc.alloc_semaphore(f"xw_{n}"))
            return sems[-1]

        wo_sb = sb("wo", [P, E, 2, D])
        wi_sb = sb("wi", [P, E, 2, 2, 4 * D])
        col_sb = sb("cols", [P, E, 18])
        o_sb = sb("o", [P, 2, 2, B, CT])
        a_sb = sb("a", [P, 2, 2, CW])
        x_sb = sb("x", [P, 2, 2, CT, 8, B])
        a_ps = [ctx.enter_context(nc.psum_tensor(f"xw_a_ps{k}", [P, BANK], F32)) for k in range(2)]
        x_ps = [ctx.enter_context(nc.psum_tensor(f"xw_x_ps{k}", [P, BANK], F32)) for k in range(4)]
        w_loaded = sem("w_loaded")
        o_loaded = [sem(f"o_loaded{k}") for k in range(2)]
        a_mm, a_out = sem("a_mm"), sem("a_out")
        x_mm = sem("x_mm")
        x_out = [sem("x_out_act"), sem("x_out_dve")]
        stored = [sem(f"stored{k}") for k in range(2)]
        start_from_one(nc, (a_out, stored, x_out,))
        block = ctx.enter_context(nc.Block())
        trips = T // CT
        half = E // 2

        def put_o(sp, i, e):
            for c in range(2):
                sp.dma_start(o_sb[:, e % 2, c], o_in[e].rearrange("b (c p) t -> c p b t", p=P)[c][:, :, bass.ds(i * CT, CT)]
                             ).then_inc(o_loaded[e % 2], 16)

        @block.sync
        def _(sp):
            for e in range(E):
                sp.dma_start(wo_sb[:, e], w_o[e].rearrange("(k p) n -> p k n", p=P)).then_inc(w_loaded, 16)
                sp.dma_start(col_sb[:, e], cols[e]).then_inc(w_loaded, 16)
                for d in range(2):
                    sp.dma_start(wi_sb[:, e, d], w_i[d][e].rearrange("(k p) n -> p k n", p=P)).then_inc(w_loaded, 16)
            put_o(sp, 0, 0)
            put_o(sp, 0, 1)

            def trip(i, last):
                for e in range(E):
                    job = i * E + e
                    sp.wait_ge(a_mm, job * 2 + 2)
                    if e + 2 < E:
                        put_o(sp, i, e + 2)
                    elif not last:
                        put_o(sp, i + 1, e + 2 - E)
                    for d in range(2):
                        for k in range(2):
                            sp.wait_ge(x_out[k], job * 8 + 4 * d + 4 + 1)
                        sp.dma_start(xw[d, e][:, bass.ds(i * CT, CT)].rearrange("p t g -> p (t g)"),
                                     x_sb[:, e % 2, d].rearrange("p t m b -> p (t m b)")).then_inc(stored[e % 2], 16)
            with sp.Fori(0, trips - 1) as i:
                trip(i, False)
            trip(trips - 1, True)
            for k in range(2):
                sp.wait_ge(stored[k], 32 * half * trips + 1)

        @block.tensor
        def _(pe):
            pe.wait_ge(w_loaded, 64 * E)
            with pe.Fori(0, trips) as i:
                def attend(e):
                    pe.wait_ge(o_loaded[e % 2], i * (32 * half) + 32 * (e // 2 + 1))
                    for m in range(2):
                        pe.wait_ge(a_out, ((i * E + e - 1) * 2 + m + 1 if e else i * (E * 2)) + 1)
                        for c in range(2):
                            mm = nc.tensor.matmul(a_ps[m][:, 0:CW], wo_sb[:, e, c, m * P:(m + 1) * P],
                                                  o_sb[:, e % 2, c].rearrange("p b t -> p t b"), start=(c == 0), stop=(c == 1))
                        mm.then_inc(a_mm, 1)
                attend(0)
                for e in range(E):
                    job = i * E + e
                    for n in range(16):
                        d, m = divmod(n, 8)
                        if n == 0:
                            pe.wait_ge(a_out, job * 2 + 3)
                        if e or n >= 4:
                            pe.wait_ge(x_out[n % 2], job * 8 + n // 2)
                        else:
                            pe.wait_ge(x_out[n % 2], job * 8 + 1)
                        for c in range(2):
                            mm = nc.tensor.matmul(x_ps[n % 4][:, 0:CW], wi_sb[:, e, d, c, COLS[m] * P:(COLS[m] + 1) * P],
                                                  a_sb[:, e % 2, c], start=(c == 0), stop=(c == 1))
                        mm.then_inc(x_mm, 1)
                        if n == 7 and e + 1 < E:
                            attend(e + 1)

        def put_x(eng, i, e, n):
            d, m = divmod(n, 8)
            job = i * E + e
            eng.wait_ge(x_mm, job * 16 + n + 1)
            if n < 2:
                eng.wait_ge(stored[e % 2], i * (32 * half) + 32 * (e // 2) + 1)
            out = x_sb[:, e % 2, d, :, m]
            src = x_ps[n % 4][:, 0:CW].rearrange("p (t b) -> p t b", b=B)
            return out, src, col_sb[:, e, 2 + 8 * d + COLS[m]:3 + 8 * d + COLS[m]]

        @block.scalar
        def _(act):
            act.wait_ge(w_loaded, 64 * E)
            with act.Fori(0, trips) as i:
                def attended(e):
                    for m in range(2):
                        act.wait_ge(a_mm, (i * E + e) * 2 + m + 1)
                        if e >= 2:
                            act.wait_ge(x_mm, (i * E + e - 1) * 16)
                        nc.scalar.activation(a_sb[:, e % 2, m], a_ps[m][:, 0:CW], ACT.Identity, bias=col_sb[:, e, m:m + 1]
                                             ).then_inc(a_out, 1)
                attended(0)
                for e in range(E):
                    for n in range(0, 16, 2):
                        out, src, bias = put_x(act, i, e, n)
                        nc.scalar.activation(out, src, ACT.Identity, bias=bias).then_inc(x_out[0], 1)
                        if n == 8 and e + 1 < E:
                            attended(e + 1)

        @block.vector
        def _(dve):
            dve.wait_ge(w_loaded, 64 * E)
            with dve.Fori(0, trips) as i:
                for e in range(E):
                    for n in range(1, 16, 2):
                        out, src, bias = put_x(dve, i, e, n)
                        nc.vector.tensor_scalar(out, src, bias, None, ALU.add).then_inc(x_out[1], 1)


def stage_decode(nc, mem, n_in, h_in, w_s1, w_s2, w_t1, w_t2, w_d1, w_d2, w_r, cols, h_out):
    D = D_EXPERT
    S1, S2, T1, T2, D1, D2, GG, BETA, RB = 0, 2, 4, 6, 8, 10, 11, 12, 13
    with ExitStack() as ctx:
        sems = []
        ctx.callback(end_stage, nc, sems)
        sb = lambda n, shape, dt=F32: ctx.enter_context(nc.sbuf_tensor(f"dec_{n}", shape, dt))

        def sem(n):
            sems.append(nc.alloc_semaphore(f"dec_{n}"))
            return sems[-1]

        s1, t1 = sb("s1", [P, E, 4, D]), sb("t1", [P, E, 4, D])
        s2, t2, d1 = sb("s2", [P, E, 2, D]), sb("t2", [P, E, 2, D]), sb("d1", [P, E, 2, D])
        d2 = sb("d2", [P, E, 2, P])
        wr_sb = sb("wr", [P, E])
        wr_rep = sb("wr_rep", [P, E, P])
        col_sb = sb("cols", [P, E, 14])
        avg = sb("avg", [P, P])
        eps_sb = sb("eps", [P, 1])
        m_sb = sb("m", [P, 2, 4, CW])
        n_sb = sb("n", [P, B, CT])
        h_sb = sb("h", [P, B, CT])
        log = sb("log", [P, E, CW])
        top = sb("top", [P, 2, CW])
        hid = sb("hid", [P, 4, CW])
        gate = sb("gate", [P, 4, CW])
        g_sb = sb("g", [P, 2, CW])
        dh = sb("dh", [P, 2, CW])
        x_sb = sb("x", [P, 2, CW])
        sq = sb("sq", [P, CW])
        r_sb = sb("r", [P, CW])
        acc = sb("acc", [P, CW])
        u_ps = [ctx.enter_context(nc.psum_tensor(f"dec_u_ps{k}", [P, BANK], F32)) for k in range(4)]
        d_ps = [ctx.enter_context(nc.psum_tensor(f"dec_d_ps{k}", [P, BANK], F32)) for k in range(2)]
        y_ps = ctx.enter_context(nc.psum_tensor("dec_y_ps", [P, BANK], F32))
        m_ps = ctx.enter_context(nc.psum_tensor("dec_m_ps", [P, BANK], F32))
        w_loaded, const_done = sem("w_loaded"), sem("const_done")
        rep_done = sem("rep_done")
        m_loaded = [sem(f"m_loaded{k}") for k in range(2)]
        n_loaded, h_loaded = sem("n_loaded"), sem("h_loaded")
        log_mm, log_out = sem("log_mm"), sem("log_out")
        soft = sem("soft")
        exp_done = sem("exp_done")
        u_mm, hid_out = sem("u_mm"), sem("hid_out")
        v_mm, gate_out = sem("v_mm"), sem("gate_out")
        g_done, d_mm, dh_out = sem("g_done"), sem("d_mm"), sem("dh_out")
        y_mm, x_out, mean_mm, sub_done, sq_done, var_mm, root_done = (
            sem(n) for n in ("y_mm", "x_out", "mean_mm", "sub_done", "sq_done", "var_mm", "root_done"))
        fin = sem("fin")
        ready = sem("ready")
        stored = sem("stored")
        SOFT, FIN = 15, 5
        start_from_one(nc, (d_mm, dh_out, fin, g_done, gate_out, hid_out, log_mm, root_done, stored, v_mm, var_mm, x_out, y_mm,))
        block = ctx.enter_context(nc.Block())
        trips = T // CT
        half = E // 2

        def put_mem(sp, i, e):
            for k in range(4):
                sp.dma_start(m_sb[:, e % 2, k], mem[k // 2, e, k % 2][:, bass.ds(i * CT, CT)].rearrange("p t b -> p (t b)")
                             ).then_inc(m_loaded[e % 2], 16)

        @block.sync
        def _(sp):
            loads = 0
            for e in range(E):
                for dst, src in ((s1, w_s1), (s2, w_s2), (t1, w_t1), (t2, w_t2), (d1, w_d1), (d2, w_d2)):
                    sp.dma_start(dst[:, e], src[e].rearrange("(k p) n -> p k n", p=P)).then_inc(w_loaded, 16)
                sp.dma_start(col_sb[:, e], cols[e]).then_inc(w_loaded, 16)
            sp.dma_start(wr_sb[:], w_r).then_inc(w_loaded, 16)
            put_mem(sp, 0, 0)
            put_mem(sp, 0, 1)

            def trip(i, last):
                sp.wait_ge(log_mm, i * E + 1)
                sp.dma_start(n_sb[:], n_in[:, :, bass.ds(i * CT, CT)]).then_inc(n_loaded, 16)
                sp.wait_ge(stored, i * 16 + 1)
                sp.dma_start(h_sb[:], h_in[:, :, bass.ds(i * CT, CT)]).then_inc(h_loaded, 16)
                for e in range(E):
                    sp.wait_ge(u_mm, (i * E + e) * 4 + 4)
                    if e + 2 < E:
                        put_mem(sp, i, e + 2)
                    elif not last:
                        put_mem(sp, i + 1, e + 2 - E)
                sp.wait_ge(ready, i + 1)
                sp.dma_start(h_out[:, :, bass.ds(i * CT, CT)], h_sb[:]).then_inc(stored, 16)
            with sp.Fori(0, trips - 1) as i:
                trip(i, False)
            trip(trips - 1, True)
            sp.wait_ge(stored, 16 * trips + 1)
        WL = 16 * (7 * E + 1)

        @block.tensor
        def _(pe):
            pe.wait_ge(w_loaded, WL)
            pe.wait_ge(rep_done, E)
            with pe.Fori(0, trips) as i:
                pe.wait_ge(n_loaded, i * 16 + 16)
                pe.wait_ge(hid_out, i * (E * 4) + 1)
                for e in range(E):
                    pe.wait_ge(gate_out, i * (E * 4) + 1)
                    nc.tensor.matmul(u_ps[e][:, 0:CW], wr_rep[:, e], n_sb[:].rearrange("p b t -> p t b"),
                                     start=True, stop=True).then_inc(log_mm, 1)

                def mean(e):
                    pe.wait_ge(x_out, i * E + e + 2)
                    pe.wait_ge(root_done, i * E + e + 1)
                    nc.tensor.matmul(m_ps[:, 0:CW], avg[:], x_sb[:, e % 2], start=True, stop=True).then_inc(mean_mm, 1)

                def variance(e):
                    pe.wait_ge(sq_done, i * E + e + 1)
                    nc.tensor.matmul(m_ps[:, 0:CW], avg[:], sq[:], start=True, stop=True).then_inc(var_mm, 1)

                for e in range(E):
                    job = i * E + e
                    pe.wait_ge(m_loaded[e % 2], i * (64 * half) + 64 * (e // 2 + 1))
                    for n in range(4):
                        w, m = (s1, t1)[n // 2], n % 2
                        if e:
                            pe.wait_ge(gate_out, (job - 1) * 4 + n + 2)
                        else:
                            pe.wait_ge(log_out, i * E + n + 1)
                        for c in range(4):
                            mm = nc.tensor.matmul(u_ps[n][:, 0:CW], w[:, e, c, m * P:(m + 1) * P], m_sb[:, e % 2, c],
                                                  start=(c == 0), stop=(c == 3))
                        mm.then_inc(u_mm, 1)
                    if e:
                        mean(e - 1)
                    for n in range(4):
                        w, m = (s2, t2)[n // 2], n % 2
                        pe.wait_ge(hid_out, job * 4 + max(n + 1, 2 * (n // 2) + 2) + 1)
                        for c in range(2):
                            mm = nc.tensor.matmul(u_ps[n][:, 0:CW], w[:, e, c, m * P:(m + 1) * P], hid[:, 2 * (n // 2) + c],
                                                  start=(c == 0), stop=(c == 1))
                        mm.then_inc(v_mm, 1)
                    if e:
                        variance(e - 1)
                    pe.wait_ge(g_done, job * 2 + 3)
                    for m in range(2):
                        pe.wait_ge(dh_out, job * 2 + 1)
                        for c in range(2):
                            mm = nc.tensor.matmul(d_ps[m][:, 0:CW], d1[:, e, c, m * P:(m + 1) * P], g_sb[:, c],
                                                  start=(c == 0), stop=(c == 1))
                        mm.then_inc(d_mm, 1)
                    pe.wait_ge(dh_out, job * 2 + 3)
                    pe.wait_ge(x_out, job + 1)
                    for c in range(2):
                        mm = nc.tensor.matmul(y_ps[:, 0:CW], d2[:, e, c], dh[:, c], start=(c == 0), stop=(c == 1))
                    mm.then_inc(y_mm, 1)
                mean(E - 1)
                variance(E - 1)

        @block.scalar
        def _(act):
            act.wait_ge(w_loaded, WL)
            act.wait_ge(const_done, 1)
            with act.Fori(0, trips) as i:
                act.wait_ge(soft, i * SOFT + 7)
                nc.scalar.activation(log[:].rearrange("p e n -> p (e n)"), log[:].rearrange("p e n -> p (e n)"), ACT.Exp
                                     ).then_inc(exp_done, 1)

                def tail(e):
                    act.wait_ge(sub_done, i * E + e + 1)
                    act.wait_ge(var_mm, i * E + e + 1)
                    nc.scalar.activation(sq[:], x_sb[:, e % 2], ACT.Square).then_inc(sq_done, 1)
                    act.wait_ge(var_mm, i * E + e + 2)
                    act.wait_ge(fin, (i * E + e) * FIN + 1)
                    nc.scalar.activation(r_sb[:], m_ps[:, 0:CW], ACT.Sqrt, bias=eps_sb[:]).then_inc(root_done, 1)

                for e in range(E):
                    job = i * E + e
                    for n in range(4):
                        act.wait_ge(u_mm, job * 4 + n + 1)
                        act.wait_ge(v_mm, job * 4 + 1)
                        at = (S1, T1)[n // 2] + n % 2
                        nc.scalar.activation(hid[:, n], u_ps[n][:, 0:CW], ACT.Relu, bias=col_sb[:, e, at:at + 1]
                                             ).then_inc(hid_out, 1)
                    for n in range(4):
                        act.wait_ge(v_mm, job * 4 + n + 2)
                        act.wait_ge(g_done, job * 2 + 1)
                        at = (S2, T2)[n // 2] + n % 2
                        nc.scalar.activation(gate[:, n], u_ps[n][:, 0:CW], ACT.Sigmoid if n < 2 else ACT.Tanh,
                                             bias=col_sb[:, e, at:at + 1]).then_inc(gate_out, 1)
                    if e:
                        tail(e - 1)
                tail(E - 1)

        @block.vector
        def _(dve):
            nc.vector.memset(eps_sb[:], EPS)
            nc.vector.memset(avg[:], 1.0 / P).then_inc(const_done, 1)
            dve.wait_ge(w_loaded, WL)
            for e in range(E):
                nc.vector.tensor_copy(wr_rep[:, e], wr_sb[:, e:e + 1].to_broadcast([P, P])).then_inc(rep_done, 1)
            with dve.Fori(0, trips) as i:
                at = i * SOFT
                dve.wait_ge(fin, i * (FIN * E) + 1)
                for e in range(E):
                    dve.wait_ge(log_mm, i * E + e + 2)
                    nc.vector.tensor_scalar(log[:, e], u_ps[e][:, 0:CW], col_sb[:, e, RB:RB + 1], None, ALU.add
                                            ).then_inc(log_out, 1)
                dve.wait_ge(log_out, i * E + E)
                for k in range(2):
                    nc.vector.tensor_tensor(top[:, k], log[:, 2 * k], log[:, 2 * k + 1], ALU.max).then_inc(soft, 1)
                dve.wait_ge(soft, at + 2)
                nc.vector.tensor_tensor(top[:, 0], top[:, 0], top[:, 1], ALU.max).then_inc(soft, 1)
                dve.wait_ge(soft, at + 3)
                for e in range(E):
                    nc.vector.tensor_tensor(log[:, e], log[:, e], top[:, 0], ALU.subtract).then_inc(soft, 1)
                dve.wait_ge(exp_done, i + 1)
                for k in range(2):
                    nc.vector.tensor_tensor(top[:, k], log[:, 2 * k], log[:, 2 * k + 1], ALU.add).then_inc(soft, 1)
                dve.wait_ge(soft, at + 9)
                nc.vector.tensor_tensor(top[:, 0], top[:, 0], top[:, 1], ALU.add).then_inc(soft, 1)
                dve.wait_ge(soft, at + 10)
                nc.vector.reciprocal(top[:, 1], top[:, 0]).then_inc(soft, 1)
                dve.wait_ge(soft, at + 11)
                for e in range(E):
                    nc.vector.tensor_tensor(log[:, e], log[:, e], top[:, 1], ALU.mult).then_inc(soft, 1)

                def sub(e):
                    dve.wait_ge(mean_mm, i * E + e + 1)
                    nc.vector.tensor_tensor(x_sb[:, e % 2], x_sb[:, e % 2], m_ps[:, 0:CW], ALU.subtract).then_inc(sub_done, 1)

                def tail(e):
                    f = (i * E + e) * FIN
                    dve.wait_ge(root_done, i * E + e + 2)
                    nc.vector.reciprocal(r_sb[:], r_sb[:]).then_inc(fin, 1)
                    dve.wait_ge(fin, f + 2)
                    dve.wait_ge(sq_done, i * E + e + 1)
                    x = x_sb[:, e % 2]
                    nc.vector.tensor_tensor(x, x, r_sb[:], ALU.mult).then_inc(fin, 1)
                    dve.wait_ge(fin, f + 3)
                    nc.vector.tensor_scalar(x, x, col_sb[:, e, GG:GG + 1], col_sb[:, e, BETA:BETA + 1], ALU.mult, ALU.add
                                            ).then_inc(fin, 1)
                    dve.wait_ge(fin, f + 3 + 1)
                    dve.wait_ge(soft, at + SOFT)
                    dst = x if e else acc[:]
                    nc.vector.tensor_tensor(dst, x, log[:, e], ALU.mult).then_inc(fin, 1)
                    dve.wait_ge(fin, f + 4 + 1)
                    if e:
                        nc.vector.tensor_tensor(acc[:], acc[:], x, ALU.add).then_inc(fin, 1)
                    else:
                        nc.vector.memset(top[:, 0, 0:1], 0.0).then_inc(fin, 1)

                for e in range(E):
                    job = i * E + e
                    if e:
                        sub(e - 1)
                    for m in range(2):
                        dve.wait_ge(gate_out, job * 4 + 3 + m + 1)
                        dve.wait_ge(d_mm, job * 2 + 1)
                        nc.vector.tensor_tensor(g_sb[:, m], gate[:, m], gate[:, 2 + m], ALU.mult).then_inc(g_done, 1)
                    if e:
                        tail(e - 1)
                    for m in range(2):
                        dve.wait_ge(d_mm, job * 2 + m + 2)
                        dve.wait_ge(y_mm, job + 1)
                        nc.vector.tensor_scalar(dh[:, m], d_ps[m][:, 0:CW], col_sb[:, e, D1 + m:D1 + m + 1], 0.0, ALU.add, ALU.max
                                                ).then_inc(dh_out, 1)
                    dve.wait_ge(y_mm, job + 2)
                    nc.vector.tensor_scalar(x_sb[:, e % 2], y_ps[:, 0:CW], col_sb[:, e, D2:D2 + 1], None, ALU.add
                                            ).then_inc(x_out, 1)
                sub(E - 1)
                tail(E - 1)
                dve.wait_ge(fin, (i * E + E) * FIN + 1)
                dve.wait_ge(h_loaded, i * 16 + 16)
                nc.vector.tensor_tensor(h_sb[:], h_sb[:], acc[:].rearrange("p (t b) -> p b t", b=B), ALU.add).then_inc(ready, 1)


def stage_retention(nc, n_in, h_in, w_q, w_k, w_v, decay, h_out):
    TT = [(lo, min(lo + P, T)) for lo in range(0, T, P)]
    NT = len(TT)
    OFF = P * (NT - 1)
    with ExitStack() as ctx:
        sems = []
        ctx.callback(end_stage, nc, sems)
        sb = lambda n, shape, dt=F32: ctx.enter_context(nc.sbuf_tensor(f"ret_{n}", shape, dt))

        def sem(n):
            sems.append(nc.alloc_semaphore(f"ret_{n}"))
            return sems[-1]

        w_sb = sb("w", [P, 3, P])
        dec_sb = sb("dec", [P, OFF + T])
        n_sb = sb("n", [P, B, T])
        h_sb = sb("h", [P, B, T])
        qk = sb("qk", [P, 2, T])
        v_sb = sb("v", [P, NT, P])
        sd = sb("sd", [P, 2, T])
        sg = sb("sg", [P, 2, T])
        a_sb = sb("a", [P, 2, T])
        s_ps = [ctx.enter_context(nc.psum_tensor(f"ret_s_ps{k}", [P, 2 * BANK], F32)) for k in range(2)]
        o_ps = ctx.enter_context(nc.psum_tensor("ret_o_ps", [P, 2 * BANK], F32))
        v_ps = [ctx.enter_context(nc.psum_tensor(f"ret_v_ps{k}", [P, BANK], F32)) for k in range(2)]
        w_loaded = sem("w_loaded")
        loaded = [sem(f"loaded{b}") for b in range(B)]
        qk_mm, qk_out, v_mm, v_out = sem("qk_mm"), sem("qk_out"), sem("v_mm"), sem("v_out")
        s_mm, sd_done, sg_done, a_done, o_mm = sem("s_mm"), sem("sd_done"), sem("sg_done"), sem("a_done"), sem("o_mm")
        ready, stored = sem("ready"), sem("stored")
        block = ctx.enter_context(nc.Block())

        @block.sync
        def _(sp):
            for n, w in enumerate((w_q, w_k, w_v)):
                sp.dma_start(w_sb[:, n], w).then_inc(w_loaded, 16)
            sp.dma_start(dec_sb[:], decay).then_inc(w_loaded, 16)
            for b in range(B):
                sp.dma_start(n_sb[:, b], n_in[:, b]).then_inc(loaded[b], 16)
                sp.dma_start(h_sb[:, b], h_in[:, b]).then_inc(loaded[b], 16)
            for b in range(B):
                sp.wait_ge(ready, b + 1)
                sp.dma_start(h_out[:, b], h_sb[:, b]).then_inc(stored, 16)
            sp.wait_ge(stored, 16 * B)

        @block.tensor
        def _(pe):
            pe.wait_ge(w_loaded, 64)
            for b in range(B):
                pe.wait_ge(loaded[b], 32)
                for n in range(2):
                    if b:
                        pe.wait_ge(sd_done, NT * b)
                    for lo, hi in COLS_OF:
                        mm = nc.tensor.matmul(s_ps[n][:, lo:hi], w_sb[:, n], n_sb[:, b, lo:hi], start=True, stop=True)
                    mm.then_inc(qk_mm, 1)
                for c, (lo, hi) in enumerate(TT):
                    if NT * b + c >= 2:
                        pe.wait_ge(v_out, NT * b + c - 1)
                    nc.tensor.matmul(v_ps[c % 2][0:hi - lo, 0:P], n_sb[:, b, lo:hi], w_sb[:, 2], start=True, stop=True
                                     ).then_inc(v_mm, 1)
                pe.wait_ge(qk_out, 2 * b + 2)

                def scores(c):
                    if c >= 2:
                        pe.wait_ge(sd_done, NT * b + c - 1)
                    k0, k1 = TT[c]
                    for lo, hi in COLS_OF:
                        mm = nc.tensor.matmul(s_ps[c % 2][0:k1 - k0, lo:hi], qk[:, 1, k0:k1], qk[:, 0, lo:hi], start=True, stop=True)
                    mm.then_inc(s_mm, 1)
                scores(0)
                scores(1)
                pe.wait_ge(v_out, NT * b + NT)
                if b:
                    pe.wait_ge(ready, b)
                for c in range(NT):
                    if c + 2 < NT:
                        scores(c + 2)
                    pe.wait_ge(a_done, NT * b + c + 1)
                    k0, k1 = TT[c]
                    for lo, hi in COLS_OF:
                        mm = nc.tensor.matmul(o_ps[:, lo:hi], v_sb[0:k1 - k0, c], a_sb[0:k1 - k0, c % 2, lo:hi],
                                              start=(c == 0), stop=(c == NT - 1))
                    mm.then_inc(o_mm, 1)

        @block.scalar
        def _(act):
            for b in range(B):
                for n in range(2):
                    act.wait_ge(qk_mm, 2 * b + n + 1)
                    nc.scalar.copy(qk[:, n], s_ps[n][:, 0:T]).then_inc(qk_out, 1)
                for c, (k0, k1) in enumerate(TT):
                    act.wait_ge(sd_done, NT * b + c + 1)
                    if NT * b + c >= 2:
                        act.wait_ge(a_done, NT * b + c - 1)
                    nc.scalar.activation(sg[0:k1 - k0, c % 2], sd[0:k1 - k0, c % 2], ACT.Sigmoid).then_inc(sg_done, 1)

        @block.vector
        def _(dve):
            for b in range(B):
                for c, (lo, hi) in enumerate(TT):
                    dve.wait_ge(v_mm, NT * b + c + 1)
                    if b and c == 0:
                        dve.wait_ge(o_mm, NT * b)
                    nc.vector.tensor_copy(v_sb[0:hi - lo, c], v_ps[c % 2][0:hi - lo, 0:P]).then_inc(v_out, 1)

                def weighted(c):
                    k0, k1 = TT[c]
                    dve.wait_ge(s_mm, NT * b + c + 1)
                    if NT * b + c >= 2:
                        dve.wait_ge(a_done, NT * b + c - 1)
                    at = OFF - P * c
                    nc.vector.tensor_tensor(sd[0:k1 - k0, c % 2], s_ps[c % 2][0:k1 - k0, 0:T], dec_sb[0:k1 - k0, at:at + T], ALU.mult
                                            ).then_inc(sd_done, 1)
                weighted(0)
                for c in range(NT):
                    if c + 1 < NT:
                        weighted(c + 1)
                    k0, k1 = TT[c]
                    dve.wait_ge(sg_done, NT * b + c + 1)
                    if NT * b + c >= 2:
                        dve.wait_ge(o_mm, NT * b + c - 1)
                    nc.vector.tensor_tensor(a_sb[0:k1 - k0, c % 2], sd[0:k1 - k0, c % 2], sg[0:k1 - k0, c % 2], ALU.mult
                                            ).then_inc(a_done, 1)
                dve.wait_ge(o_mm, NT * b + NT)
                nc.vector.tensor_tensor(h_sb[:, b], h_sb[:, b], o_ps[:, 0:T], ALU.add).then_inc(ready, 1)


def stage_attention(nc, name, q_parts, k_parts, v_aug, o_out, sel_sum, ident, units, top_k=False):
    with ExitStack() as ctx:
        sems = []
        ctx.callback(end_stage, nc, sems)
        sb = lambda n, shape, dt=F32: ctx.enter_context(nc.sbuf_tensor(f"{name}_{n}", shape, dt))

        def sem(n):
            sems.append(nc.alloc_semaphore(f"{name}_{n}"))
            return sems[-1]

        q_sb = sb("q", [STACK, 2, QUAD, T], BF16)
        k_sb = sb("k", [STACK, 2, QUAD, T], BF16)
        v_sb = sb("v", [P, 2, TILES, P])
        prob = sb("prob", [P, 2, T])
        probT = sb("probT", [P, 2, QUAD, TILES, P])
        negmax = sb("negmax", [P, 2])
        u_sb = sb("u", [P, 2, T])
        rec = sb("rec", [P, 2, T])
        sel_sb = sb("sel", [P, P])
        id_sb = sb("id", [P, P])
        if top_k:
            best = sb("best", [P, 2, 2, 8])
            left = sb("left", [P, 2, T])
            expo = sb("expo", [P, 2, T])
            pause = sb("pause", [P, 1])
        s_ps = [ctx.enter_context(nc.psum_tensor(f"{name}_s_ps{k}", [P, 2 * BANK], F32)) for k in range(2)]
        t_ps = [ctx.enter_context(nc.psum_tensor(f"{name}_t_ps{k}", [P, BANK], F32)) for k in range(2)]
        u_ps = ctx.enter_context(nc.psum_tensor(f"{name}_u_ps", [P, BANK], F32))
        r_ps = ctx.enter_context(nc.psum_tensor(f"{name}_r_ps", [P, BANK], F32))

        const_loaded = sem("const_loaded")
        qkv_loaded = [sem(f"qkv_loaded{k}") for k in range(2)]
        s_ready = sem("s_ready")
        max_ready = sem("max_ready")
        exp_done = sem("exp_done")
        t_ready = [sem(f"t_ready{k}") for k in range(2)]
        t_copied = [sem(f"t_copied{k}") for k in range(2)]
        u_ready = sem("u_ready")
        u_copied = sem("u_copied")
        r_ready = sem("r_ready")
        rec_done = sem("rec_done")
        o_ready = sem("o_ready")
        o_stored = [sem(f"o_stored{k}") for k in range(2)]
        top_step = sem("top_step")
        sel_done = sem("sel_done")

        TPU = QUAD * TILES
        HALVES = ((0, HALF), (HALF, T))

        def put_stack(sp, k, u):
            for parts, src, dst in ((Q_PARTS, q_parts, q_sb), (K_PARTS, k_parts, k_sb)):
                for slot, part in enumerate(parts):
                    sp.dma_start(dst[slot * HD:(slot + 1) * HD, k],
                                 src[bass.ds(u, 1), part].rearrange("o (h r) t -> r (o h) t", r=HD)
                                 ).then_inc(qkv_loaded[k], 16)
            sp.dma_start(v_sb[:, k, 0:TILES - 1], v_aug[bass.ds(u, 1), 0:(TILES - 1) * P].rearrange("o (c p) n -> p (o c) n", p=P)
                         ).then_inc(qkv_loaded[k], 16)
            sp.dma_start(v_sb[0:K_SIZE[-1], k, TILES - 1], v_aug[bass.ds(u, 1), (TILES - 1) * P:T].rearrange("o p n -> (o p) n")
                         ).then_inc(qkv_loaded[k], 16)
        LOADS = 16 * (2 * len(Q_PARTS) + 2)

        def put_out(sp, k, u):
            for h in range(QUAD):
                sp.dma_start(o_out[bass.ds(u, 1), h * HD:(h + 1) * HD].rearrange("o r t -> (o r) t"),
                             u_sb[h * 32:h * 32 + HD, k]).then_inc(o_stored[k], 16)
        STORES = 16 * QUAD

        start_from_one(nc, (o_stored,))
        block = ctx.enter_context(nc.Block())
        pairs = units // 2

        @block.sync
        def _(sp):
            sp.dma_start(sel_sb[:], sel_sum).then_inc(const_loaded, 16)
            sp.dma_start(id_sb[:], ident).then_inc(const_loaded, 16)
            for k in range(2):
                put_stack(sp, k, k)
            with sp.Fori(0, pairs - 1) as i:
                for k in range(2):
                    sp.wait_ge(u_ready, TILES * (2 * i + k + 1))
                    put_stack(sp, k, 2 * i + 2 + k)
                    sp.wait_ge(o_ready, 2 * (2 * i + k + 1))
                    put_out(sp, k, 2 * i + k)
            for k in range(2):
                sp.wait_ge(o_ready, 2 * (units - 2 + k + 1))
                put_out(sp, k, units - 2 + k)
            for k in range(2):
                sp.wait_ge(o_stored[k], STORES * pairs + 1)

        @block.tensor
        def _(pe):
            pe.wait_ge(const_loaded, 32)
            with pe.Fori(0, pairs) as i:
                N = 2 * TPU
                base, ubase = i * N, i * (2 * TILES)

                def logits(n):
                    k, (t, h) = n // TPU, divmod(n % TPU, QUAD)
                    if n % TPU == 0:
                        pe.wait_ge(qkv_loaded[k], LOADS * i + LOADS)
                    if n >= 2:
                        pe.wait_ge(exp_done, base + n - 1)
                    for a, b in ((0, BANK), (BANK, T)):
                        mm = nc.tensor.matmul(s_ps[n % 2][:, a:b], q_sb[:, k, h, Q_START[t]:Q_START[t] + P],
                                              k_sb[:, k, h, a:b], start=True, stop=True)
                    mm.then_inc(s_ready, 1)

                def turn(n):
                    pe.wait_ge(sel_done if top_k else exp_done, base + n + 1)
                    for half in range(2):
                        if n >= 1:
                            pe.wait_ge(t_copied[half], base + n)
                        for c in range(3 * half, 3 * half + 3):
                            mm = nc.tensor.transpose(t_ps[half][0:K_SIZE[c], (c - 3 * half) * P:(c - 3 * half + 1) * P],
                                                     prob[:, n % 2, c * P:c * P + K_SIZE[c]], id_sb[:])
                        mm.then_inc(t_ready[half], 1)

                def weigh(m):
                    k, t = divmod(m, TILES)
                    for half in range(2):
                        pe.wait_ge(t_copied[half], base + QUAD * (m + 1))
                    if m >= 4:
                        pe.wait_ge(u_copied, ubase + m - 3)
                    for c in range(TILES):
                        for h in range(QUAD):
                            mm = nc.tensor.matmul(u_ps[32 * h:32 * h + 32, (m % 4) * P:(m % 4 + 1) * P],
                                                  v_sb[0:K_SIZE[c], k, c, 32 * h:32 * h + 32],
                                                  probT[0:K_SIZE[c], m % 2, h, c], start=(c == 0), stop=(c == TILES - 1))
                    mm.then_inc(u_ready, 1)

                def spread(k, half):
                    pe.wait_ge(u_copied, ubase + TILES * (k + 1))
                    a, b = HALVES[half]
                    if k or half:
                        pe.wait_ge(rec_done, i * 4 + 2 * k + half)
                    nc.tensor.matmul(r_ps[:, 0:b - a], sel_sb[:], u_sb[:, k, a:b], start=True, stop=True).then_inc(r_ready, 1)

                logits(0)
                for n in range(N):
                    if n + 1 < N:
                        logits(n + 1)
                    turn(n)
                    if n % QUAD == 1 and n > QUAD:
                        weigh(n // QUAD - 1)
                    if n % TPU in (6, 9) and n > TPU:
                        spread(n // TPU - 1, int(n % TPU == 9))
                weigh(2 * TILES - 1)
                spread(1, 0)
                spread(1, 1)
                pe.wait_ge(exp_done, base + N)
                for half in range(2):
                    pe.wait_ge(t_copied[half], base + N)
                pe.wait_ge(rec_done, i * 4 + 4)

        @block.scalar
        def _(act):
            with act.Fori(0, pairs) as i:
                N = 2 * TPU
                base, ubase = i * N, i * (2 * TILES)

                def copy_half(n):
                    act.wait_ge(t_ready[0], base + n + 1)
                    t, h = divmod(n, QUAD)
                    if t >= 2:
                        act.wait_ge(u_ready, ubase + t - 1)
                    nc.scalar.activation(probT[:, t % 2, h, 0:3].rearrange("p c q -> p (c q)"), t_ps[0][:, 0:HALF],
                                         ACT.Copy).then_inc(t_copied[0], 1)
                for n in range(N):
                    act.wait_ge(s_ready, base + n + 1)
                    act.wait_ge(max_ready, base + n + 1)
                    if n >= 2:
                        if top_k:
                            act.wait_ge(sel_done, base + n - 1)
                        else:
                            for half in range(2):
                                act.wait_ge(t_ready[half], base + n - 1)
                    dst = expo if top_k else prob
                    nc.scalar.activation(dst[:, n % 2, :], s_ps[n % 2][:, 0:T], ACT.Exp, bias=negmax[:, n % 2:n % 2 + 1]
                                         ).then_inc(exp_done, 1)
                    if n >= 1:
                        copy_half(n - 1)
                copy_half(N - 1)

        @block.vector
        def _(dve):
            with dve.Fori(0, pairs) as i:
                N = 2 * TPU
                base, ubase = i * N, i * (2 * TILES)

                def copy_half(n):
                    dve.wait_ge(t_ready[1], base + n + 1)
                    t, h = divmod(n, QUAD)
                    if t >= 2:
                        dve.wait_ge(u_ready, ubase + t - 1)
                    nc.vector.tensor_copy(probT[:, t % 2, h, 3:5].rearrange("p c q -> p (c q)"), t_ps[1][:, 0:2 * P])
                    nc.vector.tensor_copy(probT[0:K_SIZE[5], t % 2, h, 5], t_ps[1][0:K_SIZE[5], 2 * P:3 * P]
                                          ).then_inc(t_copied[1], 1)

                def copy_sums(m):
                    k, t = divmod(m, TILES)
                    dve.wait_ge(u_ready, ubase + m + 1)
                    if t == 0:
                        dve.wait_ge(o_stored[k], STORES * i + 1)
                    nc.vector.tensor_copy(u_sb[:, k, Q_START[t]:Q_START[t] + P], u_ps[:, (m % 4) * P:(m % 4 + 1) * P]
                                          ).then_inc(u_copied, 1)

                def normalise(k, half):
                    a, b = HALVES[half]
                    dve.wait_ge(r_ready, i * 4 + 2 * k + half + 1)
                    nc.vector.reciprocal(rec[:, k, a:b], r_ps[:, 0:b - a]).then_inc(rec_done, 1)
                    dve.wait_ge(rec_done, i * 4 + 2 * k + half + 1)
                    nc.vector.tensor_tensor(u_sb[:, k, a:b], u_sb[:, k, a:b], rec[:, k, a:b], ALU.mult
                                            ).then_inc(o_ready, 1)

                for n in range(N):
                    dve.wait_ge(s_ready, base + n + 1)
                    if not top_k:
                        if n >= 2:
                            dve.wait_ge(exp_done, base + n - 1)
                        nc.vector.tensor_reduce(negmax[:, n % 2:n % 2 + 1], s_ps[n % 2][:, 0:T], AX, ALU.max, negate=True
                                                ).then_inc(max_ready, 1)
                    else:
                        top = i * (4 * N) + 4 * n
                        if n >= 2:
                            dve.wait_ge(exp_done, base + n - 1)
                        nc.vector.memset(pause[:], 0.0)
                        nc.vector.max(best[:, n % 2, 0], s_ps[n % 2][:, 0:T]).then_inc(top_step, 1)
                        dve.wait_ge(top_step, top + 1)
                        nc.vector.tensor_scalar(negmax[:, n % 2:n % 2 + 1], best[:, n % 2, 0, 0:1], -1.0, None, ALU.mult
                                                ).then_inc(top_step, 1)
                        nc.vector.match_replace(left[:, n % 2], best[:, n % 2, 0], s_ps[n % 2][:, 0:T], TAKEN
                                                ).then_inc(max_ready, 1)
                        dve.wait_ge(max_ready, base + n + 1)
                        nc.vector.memset(pause[:], 0.0)
                        nc.vector.max(best[:, n % 2, 1], left[:, n % 2]).then_inc(top_step, 1)
                        dve.wait_ge(top_step, top + 3)
                        nc.vector.memset(pause[:], 0.0)
                        nc.vector.match_replace(left[:, n % 2], best[:, n % 2, 1], left[:, n % 2], TAKEN
                                                ).then_inc(top_step, 1)
                        dve.wait_ge(top_step, top + 4)
                        dve.wait_ge(exp_done, base + n + 1)
                        if n >= 2:
                            for half in range(2):
                                dve.wait_ge(t_ready[half], base + n - 1)
                        nc.vector.scalar_tensor_tensor(prob[:, n % 2], left[:, n % 2], TAKEN, expo[:, n % 2],
                                                       ALU.is_equal, ALU.mult).then_inc(sel_done, 1)
                    if n >= 1:
                        copy_half(n - 1)
                    if n % QUAD == 2 and n > QUAD:
                        copy_sums(n // QUAD - 1)
                    if n % TPU in (7, 10) and n > TPU:
                        normalise(n // TPU - 1, int(n % TPU == 10))
                copy_half(N - 1)
                copy_sums(2 * TILES - 1)
                normalise(1, 0)
                normalise(1, 1)


def stage_lstm(nc, wh, xw, mem, trips=T // S):
    with ExitStack() as ctx:
        sems = []
        ctx.callback(end_stage, nc, sems)
        sb = lambda name, shape, dt=F32: ctx.enter_context(nc.sbuf_tensor(name, shape, dt))

        def sem(name):
            sems.append(nc.alloc_semaphore(name))
            return sems[-1]

        w_raw = sb("lstm_w_raw", [P, 2, 2, 1024])
        w_hi = sb("lstm_w_hi", [P, 2, E, 2, 1024], F16)
        w_lo = sb("lstm_w_lo", [P, 2, E, 2, 1024], F16)
        w_peak = sb("lstm_w_peak", [P, 2 * E])
        w_max = sb("lstm_w_max", [P, 1])
        w_allmax = sb("lstm_w_allmax", [P, 1])
        w_scale = sb("lstm_w_scale", [P, 1])
        w_inv = sb("lstm_w_inv", [P, 1])
        xw_sb = sb("lstm_xw", [P, 2, E, S, GC])
        hist = sb("lstm_hist", [P, 2, E * 2, S, B])
        h_parts = sb("lstm_h_parts", [P, 2, E, 2, 2, B], F16)
        part_sum = sb("lstm_part_sum", [P, 2, E * GC])
        z_sb = sb("lstm_z", [P, 2, E, GC])
        gate_sb = sb("lstm_gates", [P, 2, E, GC])
        c_sb = sb("lstm_c", [P, 2, E * 8])
        fc_sb = sb("lstm_fc", [P, 2, E * 8])
        ig_sb = sb("lstm_ig", [P, 2, E * 8])
        tc_sb = sb("lstm_tc", [P, 2, E * 8])
        z_ps = [ctx.enter_context(nc.psum_tensor(f"lstm_z_ps{d}", [P, E, 8, 2, B], F32)) for d in range(2)]

        w_loaded = [sem(f"lstm_w_loaded{k}") for k in range(2)]
        w_read = sem("lstm_w_read")
        peak_done = sem("lstm_peak_done")
        allmax_done = sem("lstm_allmax_done")
        scale_step = sem("lstm_scale_step")
        hi_done = sem("lstm_hi_done")
        split_done = sem("lstm_split_done")
        D = 2
        xw_loaded = [[sem(f"lstm_xw_loaded{d}_{k}") for k in range(len(PIECES))] for d in range(D)]
        hist_stored = [[sem(f"lstm_hist_stored{d}_{k}") for k in range(len(PIECES))] for d in range(D)]
        z_ready = [sem(f"lstm_z_ready{d}") for d in range(D)]
        sum_done = [sem(f"lstm_sum_done{d}") for d in range(D)]
        z_done = [sem(f"lstm_z_done{d}") for d in range(D)]
        sig_done = [sem(f"lstm_sig_done{d}") for d in range(D)]
        tanh_done = [sem(f"lstm_tanh_done{d}") for d in range(D)]
        fc_done = [sem(f"lstm_fc_done{d}") for d in range(D)]
        ig_done = [sem(f"lstm_ig_done{d}") for d in range(D)]
        c_done = [sem(f"lstm_c_done{d}") for d in range(D)]
        tc_done = [sem(f"lstm_tc_done{d}") for d in range(D)]
        h_done = [sem(f"lstm_h_done{d}") for d in range(D)]
        h_hi_done = [sem(f"lstm_h_hi_done{d}") for d in range(D)]
        h_lo_done = [sem(f"lstm_h_lo_done{d}") for d in range(D)]
        zero_done = sem("lstm_zero_done")


        def slot(d, j):
            return j if d == 0 else S - 1 - j

        def slots(d, k):
            a, b = PIECES[k]
            return (a, b) if d == 0 else (S - b, S - a)

        def xw_move(eng, d, k, i):
            a, b = slots(d, k)
            start = i * S + a if d == 0 else i * -S + (T - S + a)
            return eng.dma_start(xw_sb[:, d, :, a:b, :],
                                 xw[d].rearrange("e p t g -> p e t g")[:, :, bass.ds(start, b - a), :])

        def hist_move(eng, d, k, i):
            a, b = slots(d, k)
            start = i * S + a if d == 0 else i * -S + (T - S + a)
            return eng.dma_start(mem[d].rearrange("e c p t b -> p (e c) t b")[:, :, bass.ds(start, b - a), :],
                                 hist[:, d, :, a:b, :])

        start_from_one(nc, (hist_stored,))
        block = ctx.enter_context(nc.Block())

        @block.sync
        def _(sp):
            for n in range(2 * 2 * E):
                d, e = (n // E) % 2, n % E
                if 2 <= n < 2 * E + 2:
                    sp.wait_ge(w_read, n - 1)
                elif n >= 2:
                    sp.wait_ge(split_done, n - 2 * E - 1)
                sp.dma_start(w_raw[:, n % 2], wh[d][e].rearrange("(k p) n -> p k n", p=P)).then_inc(w_loaded[n % 2], 16)
            for d in range(D):
                for k in range(len(PIECES)):
                    xw_move(sp, d, k, 0).then_inc(xw_loaded[d][k], 16)
            with sp.Fori(0, trips - 1) as i:
                for k, (_, last) in enumerate(PIECES):
                    for d in range(D):
                        sp.wait_ge(sum_done[d], i * S + last)
                        xw_move(sp, d, k, i + 1).then_inc(xw_loaded[d][k], 16)
                        sp.wait_ge(h_lo_done[d], i * S + last + 1)
                        hist_move(sp, d, k, i).then_inc(hist_stored[d][k], 16)
            for k, (_, last) in enumerate(PIECES):
                for d in range(D):
                    sp.wait_ge(h_lo_done[d], (trips - 1) * S + last + 1)
                    hist_move(sp, d, k, trips - 1).then_inc(hist_stored[d][k], 16)
            for k in range(len(PIECES)):
                for d in range(D):
                    sp.wait_ge(hist_stored[d][k], 16 * trips + 1)

        @block.gpsimd
        def _(pool):
            pool.wait_ge(peak_done, 1)
            nc.gpsimd.partition_all_reduce(w_allmax[:], w_max[:], P, bass.bass_isa.ReduceOp.max).then_inc(allmax_done, 1)

        @block.tensor
        def _(pe):
            pe.wait_ge(split_done, 2 * E)
            with pe.Fori(0, trips) as i:
                for j in range(S):
                    for d in range(D):
                        pe.wait_ge(h_lo_done[d], i * S + j + 1)
                        for e in range(E):
                            for m in range(8):
                                for n, (k, w) in enumerate(((0, w_hi), (0, w_lo), (1, w_hi), (1, w_lo))):
                                    mm = nc.tensor.matmul(
                                        z_ps[d][:, e, m].rearrange("p q b -> p (q b)"), w[:, d, e, k, COLS[m] * P:(COLS[m] + 1) * P],
                                        h_parts[:, d, e, k].rearrange("p q b -> p (q b)"), start=(n == 0), stop=(n == 3))
                        mm.then_inc(z_ready[d], 1)

        @block.scalar
        def _(act):
            for n in range(2 * E):
                d, e = n // E, n % E
                act.wait_ge(scale_step, 4)
                act.wait_ge(w_loaded[n % 2], 16 * ((2 * E + n) // 2 + 1))
                nc.scalar.activation(w_hi[:, d, e], w_raw[:, n % 2], ACT.Copy, scale=w_inv[:, 0:1]).then_inc(hi_done, 1)
            with act.Fori(0, trips) as i:
                for j in range(S):
                    for d in range(D):
                        step = i * S + j + 1
                        act.wait_ge(z_done[d], step)
                        nc.scalar.activation(gate_sb[:, d, :, 0:24], z_sb[:, d, :, 0:24], ACT.Sigmoid).then_inc(sig_done[d], 1)
                        nc.scalar.activation(gate_sb[:, d, :, 24:32], z_sb[:, d, :, 24:32], ACT.Tanh).then_inc(tanh_done[d], 1)
                        act.wait_ge(c_done[d], step)
                        nc.scalar.activation(tc_sb[:, d], c_sb[:, d], ACT.Tanh).then_inc(tc_done[d], 1)

        @block.vector
        def _(dve):
            for n in range(2 * E):
                dve.wait_ge(w_loaded[n % 2], 16 * (n // 2 + 1))
                nc.vector.tensor_reduce(w_peak[:, n:n + 1], w_raw[:, n % 2].rearrange("p k n -> p (k n)"), AX, ALU.max,
                                        apply_absolute_value=True).then_inc(w_read, 1)
            dve.wait_ge(w_read, 2 * E)
            nc.vector.tensor_reduce(w_max[:], w_peak[:], AX, ALU.max).then_inc(peak_done, 1)
            dve.wait_ge(allmax_done, 1)
            nc.vector.tensor_scalar(w_scale[:], w_allmax[:], 1e-30, None, ALU.max).then_inc(scale_step, 1)
            dve.wait_ge(scale_step, 1)
            nc.vector.tensor_scalar(w_scale[:].bitcast(mybir.dt.uint32), w_scale[:].bitcast(mybir.dt.uint32), 0x7f800000, None, ALU.bitwise_and).then_inc(scale_step, 1)
            dve.wait_ge(scale_step, 2)
            nc.vector.reciprocal(w_inv[:], w_scale[:]).then_inc(scale_step, 1)
            nc.vector.memset(c_sb[:], 0.0).then_inc(scale_step, 1)
            dve.wait_ge(scale_step, 4)
            for n in range(2 * E):
                d, e = n // E, n % E
                dve.wait_ge(hi_done, n + 1)
                nc.vector.scalar_tensor_tensor(w_lo[:, d, e], w_raw[:, n % 2], w_inv[:, 0:1], w_hi[:, d, e], ALU.mult, ALU.subtract).then_inc(split_done, 1)
            for d in range(D):
                nc.vector.memset(h_parts[:, d], 0.0).then_inc(h_lo_done[d], 1)
            with dve.Fori(0, trips) as i:
                for j in range(S):
                    k = 0 if j < PIECES[0][1] else 1
                    for d in range(D):
                        step = i * S + j + 1
                        s = slot(d, j)
                        hi = h_parts[:, d, :, :, 0].rearrange("p e c b -> p (e c) b")
                        lo = h_parts[:, d, :, :, 1].rearrange("p e c b -> p (e c) b")
                        o_gate = gate_sb[:, d, :, 16:24].rearrange("p e (c b) -> p e c b", c=2)
                        if j == PIECES[k][0]:
                            dve.wait_ge(xw_loaded[d][k], i * 16 + 16)
                            dve.wait_ge(hist_stored[d][k], i * 16 + 1)
                        dve.wait_ge(z_ready[d], step)
                        nc.vector.scalar_tensor_tensor(
                            part_sum[:, d].rearrange("p (e g b) -> p e g b", e=E, g=8), z_ps[d][:, :, :, 0], w_scale[:, 0:1],
                            xw_sb[:, d, :, s].rearrange("p e (g b) -> p e g b", g=8), ALU.mult, ALU.add).then_inc(sum_done[d], 1)
                        dve.wait_ge(sum_done[d], step)
                        nc.vector.scalar_tensor_tensor(
                            z_sb[:, d].rearrange("p e (g b) -> p (e g) b", g=8), z_ps[d][:, :, :, 1].rearrange("p e g b -> p (e g) b"),
                            w_scale[:, 0:1], part_sum[:, d].rearrange("p (n b) -> p n b", b=B), ALU.mult, ALU.add).then_inc(z_done[d], 1)
                        dve.wait_ge(sig_done[d], step)
                        nc.vector.tensor_tensor(fc_sb[:, d].rearrange("p (e x) -> p e x", e=E), gate_sb[:, d, :, 8:16],
                                                c_sb[:, d].rearrange("p (e x) -> p e x", e=E), ALU.mult).then_inc(fc_done[d], 1)
                        dve.wait_ge(tanh_done[d], step)
                        nc.vector.tensor_tensor(ig_sb[:, d].rearrange("p (e x) -> p e x", e=E), gate_sb[:, d, :, 0:8],
                                                gate_sb[:, d, :, 24:32], ALU.mult).then_inc(ig_done[d], 1)
                        dve.wait_ge(ig_done[d], step)
                        nc.vector.tensor_tensor(c_sb[:, d], fc_sb[:, d], ig_sb[:, d], ALU.add).then_inc(c_done[d], 1)
                        dve.wait_ge(tc_done[d], step)
                        h_now = hist[:, d, :, s]
                        tc = tc_sb[:, d].rearrange("p (e c b) -> p e c b", e=E, c=2)
                        nc.vector.tensor_tensor(h_parts[:, d, :, :, 0], o_gate, tc, ALU.mult).then_inc(h_hi_done[d], 1)
                        nc.vector.tensor_tensor(h_now.rearrange("p (e c) b -> p e c b", e=E), o_gate, tc, ALU.mult).then_inc(h_done[d], 1)
                        dve.wait_ge(h_done[d], step)
                        nc.vector.tensor_tensor(lo, h_now, hi, ALU.subtract).then_inc(h_lo_done[d], 1)


def audio_tower(nc, a, out):
    def scratch(name, shape, dt=F32):
        return nc.dram_tensor(f"scratch_{name}", list(shape), dt, kind="Internal").ap()

    def attention(name, src, w, cols, v_bias, experts, heads, scale, top_k=False):
        units = experts * B * heads // QUAD
        q = scratch(f"{name}_q", (units, 3, QUAD * HD, T), BF16)
        k = scratch(f"{name}_k", (units, 3, QUAD * HD, T), BF16)
        v = scratch(f"{name}_v", (units, T, P))
        o = scratch(f"{name}_o", (units, QUAD * HD, T))
        stage_qkv(nc, f"{name}p", src, w, cols, v_bias, q, k, v, experts, heads, scale)
        stage_attention(nc, name, q, k, v, o, a["sel_sum"], a["ident"], units, top_k)
        return o

    h0, h1, h2, h3 = (scratch(f"h{n}", (P, B, T)) for n in range(4))
    n0, n1, n2, n3 = (scratch(f"n{n}", (P, B, T)) for n in range(4))
    as_source = lambda n: n.rearrange("(e k p) b t -> e k p b t", e=1, k=1)
    by_batch = lambda o: o.rearrange("(b g) r t -> b (g r) t", b=B)

    stage_tok(nc, a["x"], a["w_tok"], a["b_tok"], h0)
    stage_norm(nc, "norm0", h0, n0)
    o0 = attention("att0", as_source(n0), a["w_qkv0"], a["cols_qkv0"], a["bv0"], 1, 8, 1.0 / 4.0)
    stage_norm(nc, "norm1", h0, n1, by_batch(o0), a["wo0"], a["cols_o0"], h1)

    enc = scratch("enc", (E, 2, P, B, T))
    stage_encode(nc, n1, a["enc_w1"], a["enc_w2"], a["cols_enc"], enc)
    oe = attention("atte", enc, a["attn_in_w"], a["cols_qkve"], a["bve"], E, 16, 1.0 / 4.0)
    xw = scratch("xw", (2, E, P, T, GC))
    mem = scratch("mem", (2, E, 2, P, T, B))
    stage_lstm_inputs(nc, oe.rearrange("(e b g) r t -> e b (g r) t", e=E, b=B), a["attn_out_w"], (a["wi_f"], a["wi_b"]),
                      a["cols_xw"], xw)
    stage_lstm(nc, (a["wh_f"], a["wh_b"]), xw, mem)
    stage_decode(nc, mem, n1, h1, a["sig_w1"], a["sig_w2"], a["tan_w1"], a["tan_w2"], a["dec_w1"], a["dec_w2"],
                 a["router_w"], a["cols_dec"], h2)

    stage_norm(nc, "norm2", h2, n2)
    stage_retention(nc, n2, h2, a["w_q1"], a["w_k1"], a["w_v1"], a["decay"], h3)
    stage_norm(nc, "norm3", h3, n3, cols=a["cols_o1"], conv=True)
    o1 = attention("att1", as_source(n3), a["w_qkv1"], a["cols_qkv1"], a["bv1"], 1, 8, float(P) ** -0.5, top_k=True)
    stage_norm(nc, "norm4", h3, None, by_batch(o1), a["wo1"], a["cols_o1"], out)


def kernel(**inputs):
    import numpy as np
    import concourse.bacc as bacc
    from concourse.bass_utils import run_bass_kernel_spmd as run

    g = {k: np.asarray(v) for k, v in inputs.items()}
    ffn = lambda n: g["L0_ffn_" + n]
    columns = lambda v: v.reshape(-1, P).T
    ecolumns = lambda v: v.reshape(E, -1, P).transpose(0, 2, 1)
    zero = np.zeros((P, 1), np.float32)

    sel_sum = np.zeros((P, P), np.float32)
    for h in range(QUAD):
        sel_sum[32 * h + HD, 32 * h:32 * h + 32] = 1.0
    off = P * (TILES - 1)
    distance = np.abs(np.arange(P)[:, None] - np.arange(off + T)[None] + off)
    decay = (0.96875 ** distance).astype(np.float32)

    taps = ("L0_tok_W_z", "L0_tok_W_f", "L0_tok_W_o")
    arrays = {
        "x": g["x"].transpose(2, 0, 1),
        "w_tok": np.stack([g[n].transpose(1, 2, 0) for n in taps], axis=1),
        "b_tok": np.stack([g["L0_tok_b_z"], g["L0_tok_b_f"], g["L0_tok_b_o"]], axis=1),
        "w_qkv0": np.concatenate([g["L0_attn_Wqk"], g["L0_attn_Wv"]], axis=1)[None],
        "cols_qkv0": columns(g["L0_attn_bqk"])[None],
        "bv0": g["L0_attn_bv"][None],
        "wo0": g["L0_attn_Wo"],
        "cols_o0": np.concatenate([columns(g["L0_attn_bo"])] + [zero] * 4, axis=1),
        "enc_w1": ffn("enc_w1"), "enc_w2": ffn("enc_w2"),
        "cols_enc": np.concatenate([ecolumns(ffn(n)) for n in ("enc_b1", "enc_b2", "enc_g", "enc_beta")], axis=2),
        "attn_in_w": ffn("attn_in_w"),
        "cols_qkve": ecolumns(ffn("attn_in_b")[:, :2 * D_EXPERT]),
        "bve": ffn("attn_in_b")[:, 2 * D_EXPERT:],
        "attn_out_w": ffn("attn_out_w"),
        "wi_f": ffn("lstm_wi_f"), "wi_b": ffn("lstm_wi_b"), "wh_f": ffn("lstm_wh_f"), "wh_b": ffn("lstm_wh_b"),
        "cols_xw": np.concatenate([ecolumns(ffn(n)) for n in ("attn_out_b", "lstm_b_f", "lstm_b_b")], axis=2),
        "sig_w1": ffn("sig_w1"), "sig_w2": ffn("sig_w2"), "tan_w1": ffn("tan_w1"), "tan_w2": ffn("tan_w2"),
        "dec_w1": ffn("dec_w1"), "dec_w2": ffn("dec_w2"),
        "router_w": ffn("router_w"),
        "cols_dec": np.concatenate(
            [ecolumns(ffn(n)) for n in ("sig_b1", "sig_b2", "tan_b1", "tan_b2", "dec_b1", "dec_b2", "dec_g", "dec_beta")]
            + [np.broadcast_to(ffn("router_b")[:, None, None], (E, P, 1))], axis=2),
        "w_q1": g["L1_attn_W_Q"], "w_k1": g["L1_attn_W_K"], "w_v1": g["L1_attn_W_V"],
        "decay": decay,
        "cols_o1": np.concatenate([columns(g["L1_ffn_wo_b"]), columns(g["L1_ffn_pos_b"]), g["L1_ffn_pos_w"][:, 0]], axis=1),
        "w_qkv1": g["L1_ffn_qkv_w"].T[None],
        "cols_qkv1": columns(g["L1_ffn_qkv_b"][:2 * P])[None],
        "bv1": g["L1_ffn_qkv_b"][None, 2 * P:],
        "wo1": g["L1_ffn_wo_w"].T,
        "sel_sum": sel_sum,
        "ident": np.eye(P, dtype=np.float32),
    }
    nc = bacc.Bacc("TRN2", target_bir_lowering=False, num_devices=1)
    feed, a = {}, {}
    for name, array in arrays.items():
        feed[f"in_{name}"] = np.ascontiguousarray(array)
        a[name] = nc.dram_tensor(f"in_{name}", list(array.shape), mybir.dt.from_np(array.dtype), kind="ExternalInput").ap()
    out = nc.dram_tensor("out", [P, B, T], F32, kind="ExternalOutput").ap()
    audio_tower(nc, a, out)
    r = run(nc, [feed], core_ids=[0])
    return r.results[0]["out"].transpose(1, 2, 0)
```

```python
from contextlib import ExitStack

import concourse.bass as bass
from concourse import mybir

ALU = mybir.AluOpType
ACT = mybir.ActivationFunctionType
F32 = mybir.dt.float32
F16 = mybir.dt.float16
BF16 = mybir.dt.bfloat16
AX = mybir.AxisListType.X

P = 128
B, T, E = 4, 749, 4
D_EXPERT = 2 * P
BANK = 512
HD = 16
EPS = 1e-5
COLS_OF = ((0, BANK), (BANK, T))

QUAD = 4
TILES = -(-T // P)
Q_START = [min(P * t, T - P) for t in range(TILES)]
K_SIZE = [min(P, T - P * t) for t in range(TILES)]
HALF = 3 * P
Q_PARTS = (0, 0, 0, 1, 1, 2)
K_PARTS = (0, 1, 2, 0, 1, 0)
STACK = HD * len(Q_PARTS)
HROWS = 2 * HD
TP = TILES * P
MAX_PARTS = 2
AHEAD = 4
TAKEN = -2.0 ** 126

S = 7
GC = 32
COLS = (0, 1, 2, 3, 6, 7, 4, 5)
PIECES = ((0, 4), (4, 7))
CT = 107
CW = CT * B


def start_from_one(nc, sems):
    for s in sems:
        for each in s if isinstance(s, list) else (s,):
            for one in each if isinstance(each, list) else (each,):
                nc.gpsimd.sem_inc(one, 1)
    nc.all_engine_barrier()


def end_stage(nc, sems):
    nc.clear_and_free_semaphores(sems)
    nc.all_engine_barrier()


def stage_tok(nc, x, w_tok, b_tok, h_out):
    with ExitStack() as ctx:
        sems = []
        ctx.callback(end_stage, nc, sems)
        sb = lambda n, shape, dt=F32: ctx.enter_context(nc.sbuf_tensor(f"tok_{n}", shape, dt))

        def sem(n):
            sems.append(nc.alloc_semaphore(f"tok_{n}"))
            return sems[-1]

        x_sb = sb("x", [P, B, T + 1])
        w_sb = sb("w", [P, 3, 2, P])
        b_sb = sb("b", [P, 3])
        gate = sb("gate", [P, 2, 3, T])
        fz = sb("fz", [P, 2, T])
        inp = sb("inp", [P, 2, T])
        cell = sb("cell", [P, 2, T])
        h_sb = sb("h", [P, 2, T])
        g_ps = [ctx.enter_context(nc.psum_tensor(f"tok_g_ps{g}", [P, 2 * BANK], F32)) for g in range(3)]
        w_loaded = sem("w_loaded")
        x_loaded = [sem(f"x_loaded{b}") for b in range(B)]
        gate_mm = sem("gate_mm")
        gate_out = sem("gate_out")
        step = sem("step")
        stored = [sem(f"stored{k}") for k in range(2)]
        block = ctx.enter_context(nc.Block())

        @block.sync
        def _(sp):
            sp.dma_start(w_sb[:], w_tok).then_inc(w_loaded, 16)
            sp.dma_start(b_sb[:], b_tok).then_inc(w_loaded, 16)
            for b in range(B):
                sp.dma_start(x_sb[:, b], x[:, b]).then_inc(x_loaded[b], 16)
            for b in range(B):
                sp.wait_ge(step, 4 * b + 4)
                sp.dma_start(h_out[:, b], h_sb[:, b % 2]).then_inc(stored[b % 2], 16)
            for k in range(2):
                sp.wait_ge(stored[k], 16 * (B // 2))

        @block.tensor
        def _(pe):
            pe.wait_ge(w_loaded, 32)
            for b in range(B):
                pe.wait_ge(x_loaded[b], 16)
                for g in range(3):
                    if b:
                        pe.wait_ge(gate_out, 3 * (b - 1) + g + 1)
                    for lo, hi in COLS_OF:
                        for tap in range(2):
                            mm = nc.tensor.matmul(g_ps[g][:, lo:hi], w_sb[:, g, tap], x_sb[:, b, lo + tap:hi + tap],
                                                  start=(tap == 0), stop=(tap == 1))
                    mm.then_inc(gate_mm, 1)

        @block.scalar
        def _(act):
            for b in range(B):
                for g in range(3):
                    act.wait_ge(gate_mm, 3 * b + g + 1)
                    if b >= 2 and g == 0:
                        act.wait_ge(step, 4 * (b - 2) + 4)
                    nc.scalar.activation(gate[:, b % 2, g], g_ps[g][:, 0:T], ACT.Tanh if g == 0 else ACT.Sigmoid,
                                         bias=b_sb[:, g:g + 1]).then_inc(gate_out, 1)

        @block.vector
        def _(dve):
            for b in range(B):
                k = b % 2
                dve.wait_ge(gate_out, 3 * b + 3)
                nc.vector.tensor_tensor(fz[:, k], gate[:, k, 1], gate[:, k, 0], ALU.mult).then_inc(step, 1)
                dve.wait_ge(step, 4 * b + 1)
                nc.vector.tensor_tensor(inp[:, k], gate[:, k, 0], fz[:, k], ALU.subtract).then_inc(step, 1)
                dve.wait_ge(step, 4 * b + 2)
                nc.vector.tensor_tensor_scan(cell[:, k], gate[:, k, 1], inp[:, k], 0.0, ALU.mult, ALU.add).then_inc(step, 1)
                dve.wait_ge(step, 4 * b + 3)
                if b >= 2:
                    dve.wait_ge(stored[k], 16 * (b // 2))
                nc.vector.tensor_tensor(h_sb[:, k], gate[:, k, 2], cell[:, k], ALU.mult).then_inc(step, 1)


def stage_norm(nc, name, h_in, n_out, o_in=None, sum_in=None, w_o=None, cols=None, h_out=None, conv=False):
    with ExitStack() as ctx:
        sems = []
        ctx.callback(end_stage, nc, sems)
        sb = lambda n, shape, dt=F32: ctx.enter_context(nc.sbuf_tensor(f"{name}_{n}", shape, dt))

        def sem(n):
            sems.append(nc.alloc_semaphore(f"{name}_{n}"))
            return sems[-1]

        norm = n_out is not None
        h_sb = sb("h", [P, B, T])
        col_sb = sb("cols", [P, 5])
        avg = sb("avg", [P, P])
        eps_sb = sb("eps", [P, 1])
        d_sb = sb("d", [P, 2, T])
        sq = sb("sq", [P, 2, T])
        r_sb = sb("r", [P, 2, T])
        n_sb = sb("n", [P, 2, T + 2])
        y_sb = sb("y", [P, 2, T])
        o_sb = sb("o", [P, B, T])
        sum_sb = sb("sum", [P, B, T])
        w_sb = sb("w", [P, P])
        o_ps = [ctx.enter_context(nc.psum_tensor(f"{name}_o_ps{k}", [P, 2 * BANK], F32)) for k in range(2)]
        m_ps = ctx.enter_context(nc.psum_tensor(f"{name}_m_ps", [P, 2 * BANK], F32))
        v_ps = ctx.enter_context(nc.psum_tensor(f"{name}_v_ps", [P, 2 * BANK], F32))
        w_loaded = sem("w_loaded")
        loaded = [sem(f"loaded{b}") for b in range(B)]
        share_step = sem("share_step")
        o_mm = sem("o_mm")
        h_done = sem("h_done")
        mean_mm = sem("mean_mm")
        d_done = sem("d_done")
        sq_done = sem("sq_done")
        var_mm = sem("var_mm")
        root_done = sem("root_done")
        r_done = sem("r_done")
        n_done = sem("n_done")
        conv_step = sem("conv_step")
        ready = sem("ready")
        edge_done = sem("edge_done")
        h_stored = sem("h_stored")
        n_stored = [sem(f"n_stored{k}") for k in range(2)]
        LOADS = 48 if o_in is not None else 16
        W_LOADS = 32 if o_in is not None else 16
        block = ctx.enter_context(nc.Block())

        @block.sync
        def _(sp):
            if cols is not None:
                sp.dma_start(col_sb[:], cols).then_inc(w_loaded, 16)
            if o_in is not None:
                sp.dma_start(w_sb[:], w_o).then_inc(w_loaded, 16)
            for b in range(B):
                sp.dma_start(h_sb[:, b], h_in[:, b]).then_inc(loaded[b], 16)
                if o_in is not None:
                    sp.dma_start(o_sb[:, b], o_in[b]).then_inc(loaded[b], 16)
                    sp.dma_start(sum_sb[:, b], sum_in[b]).then_inc(loaded[b], 16)
            for b in range(B):
                if h_out is not None:
                    sp.wait_ge(h_done, b + 1)
                    sp.dma_start(h_out[:, b], h_sb[:, b]).then_inc(h_stored, 16)
                if norm:
                    sp.wait_ge(ready, b + 1)
                    sp.dma_start(n_out[:, b], (y_sb if conv else n_sb)[:, b % 2, 0:T] if conv else n_sb[:, b % 2, 1:T + 1]
                                 ).then_inc(n_stored[b % 2], 16)
            if h_out is not None:
                sp.wait_ge(h_stored, 16 * B)
            if norm:
                for k in range(2):
                    sp.wait_ge(n_stored[k], 16 * (B // 2))

        @block.tensor
        def _(pe):
            def project(b):
                if b == 0:
                    pe.wait_ge(w_loaded, 32)
                pe.wait_ge(share_step, 2 * b + 2)
                if b >= 2:
                    pe.wait_ge(h_done, b - 1)
                for lo, hi in COLS_OF:
                    mm = nc.tensor.matmul(o_ps[b % 2][:, lo:hi], w_sb[:], o_sb[:, b, lo:hi], start=True, stop=True)
                mm.then_inc(o_mm, 1)
            if o_in is not None:
                project(0)
            if norm:
                pe.wait_ge(edge_done, 1)
            for b in range(B):
                if o_in is not None and b + 1 < B:
                    project(b + 1)
                if not norm:
                    continue
                if o_in is not None:
                    pe.wait_ge(h_done, b + 1)
                else:
                    pe.wait_ge(loaded[b], LOADS)
                if b:
                    pe.wait_ge(d_done, b)
                for lo, hi in COLS_OF:
                    mm = nc.tensor.matmul(m_ps[:, lo:hi], avg[:], h_sb[:, b, lo:hi], start=True, stop=True)
                mm.then_inc(mean_mm, 1)
                pe.wait_ge(sq_done, b + 1)
                if b:
                    pe.wait_ge(root_done, b)
                for lo, hi in COLS_OF:
                    mm = nc.tensor.matmul(v_ps[:, lo:hi], avg[:], sq[:, b % 2, lo:hi], start=True, stop=True)
                mm.then_inc(var_mm, 1)

        @block.scalar
        def _(act):
            if norm:
                act.wait_ge(edge_done, 1)
            for b in range(B if norm else 0):
                act.wait_ge(d_done, b + 1)
                if b >= 2:
                    act.wait_ge(var_mm, b - 1)
                nc.scalar.activation(sq[:, b % 2], d_sb[:, b % 2], ACT.Square).then_inc(sq_done, 1)
                act.wait_ge(var_mm, b + 1)
                if b >= 2:
                    act.wait_ge(ready, b - 1)
                nc.scalar.activation(r_sb[:, b % 2], v_ps[:, 0:T], ACT.Sqrt, bias=eps_sb[:]).then_inc(root_done, 1)

        @block.vector
        def _(dve):
            nc.vector.memset(avg[:], 1.0 / P)
            nc.vector.memset(eps_sb[:], EPS)
            nc.vector.memset(n_sb[:], 0.0).then_inc(edge_done, 1)
            dve.wait_ge(edge_done, 1)
            if cols is not None:
                dve.wait_ge(w_loaded, W_LOADS)

            def share(b):
                dve.wait_ge(loaded[b], LOADS)
                nc.vector.reciprocal(sum_sb[:, b], sum_sb[:, b]).then_inc(share_step, 1)
                dve.wait_ge(share_step, 2 * b + 1)
                nc.vector.tensor_tensor(o_sb[:, b], o_sb[:, b], sum_sb[:, b], ALU.mult).then_inc(share_step, 1)
            if o_in is not None:
                share(0)
            for b in range(B):
                k = b % 2
                if o_in is not None and b + 1 < B:
                    share(b + 1)
                if o_in is not None:
                    dve.wait_ge(o_mm, b + 1)
                    dve.wait_ge(loaded[b], LOADS)
                    nc.vector.scalar_tensor_tensor(h_sb[:, b], o_ps[k][:, 0:T], col_sb[:, 0:1], h_sb[:, b],
                                                   ALU.add, ALU.add).then_inc(h_done, 1)
                if not norm:
                    continue
                dve.wait_ge(mean_mm, b + 1)
                nc.vector.tensor_tensor(d_sb[:, k], h_sb[:, b], m_ps[:, 0:T], ALU.subtract).then_inc(d_done, 1)
                dve.wait_ge(root_done, b + 1)
                nc.vector.reciprocal(r_sb[:, k], r_sb[:, k]).then_inc(r_done, 1)
                dve.wait_ge(r_done, b + 1)
                if b >= 2:
                    dve.wait_ge(n_stored[k], 16 * (b // 2))
                done = n_done if conv else ready
                nc.vector.tensor_tensor(n_sb[:, k, 1:T + 1], d_sb[:, k], r_sb[:, k], ALU.mult).then_inc(done, 1)
                if conv:
                    dve.wait_ge(n_done, b + 1)
                    nc.vector.tensor_scalar(y_sb[:, k], n_sb[:, k, 0:T], col_sb[:, 2:3], col_sb[:, 1:2],
                                            ALU.mult, ALU.add).then_inc(conv_step, 1)
                    for tap in (1, 2):
                        dve.wait_ge(conv_step, 3 * b + tap)
                        nc.vector.scalar_tensor_tensor(y_sb[:, k], n_sb[:, k, tap:T + tap], col_sb[:, 2 + tap:3 + tap],
                                                       y_sb[:, k], ALU.mult, ALU.add).then_inc(conv_step, 1)
                    dve.wait_ge(conv_step, 3 * b + 3)
                    nc.vector.tensor_tensor(y_sb[:, k], n_sb[:, k, 1:T + 1], y_sb[:, k], ALU.add).then_inc(ready, 1)


def stage_qkv(nc, name, src, w_qkv, cols, v_bias, q_parts, k_parts, v_aug, experts, heads, scale):
    KC = src.shape[1]
    F = heads * HD
    MC = F // P
    G = heads // 4
    TT = [(lo, min(lo + P, T)) for lo in range(0, T, P)]
    NT = len(TT)
    U = B * G
    with ExitStack() as ctx:
        sems = []
        ctx.callback(end_stage, nc, sems)
        sb = lambda n, shape, dt=F32: ctx.enter_context(nc.sbuf_tensor(f"{name}_{n}", shape, dt))

        def sem(n):
            sems.append(nc.alloc_semaphore(f"{name}_{n}"))
            return sems[-1]

        w_sb = sb("w", [P, experts, KC, 3 * F])
        col_sb = sb("cols", [P, experts, 2 * MC])
        vb_sb = sb("vb", [P, experts, F])
        s_sb = sb("s", [P, 2, KC, T])
        whole = sb("whole", [P, 2, T])
        rest = sb("rest", [P, 2, T])
        part = sb("part", [P, 2, 3, T], BF16)
        v_sb = sb("v", [P, 2, G, 4, 2 * HD])
        qk_ps = [ctx.enter_context(nc.psum_tensor(f"{name}_qk_ps{k}", [P, 2 * BANK], F32)) for k in range(2)]
        v_ps = [ctx.enter_context(nc.psum_tensor(f"{name}_v_ps{k}", [P, BANK], F32)) for k in range(2)]
        w_loaded = sem("w_loaded")
        s_loaded = [sem(f"s_loaded{k}") for k in range(2)]
        qk_mm = sem("qk_mm")
        whole_done = sem("whole_done")
        part_done = [sem(f"part{p}_done") for p in range(3)]
        rest_done = sem("rest_done")
        part_stored = [sem(f"part_stored{k}") for k in range(2)]
        v_mm = sem("v_mm")
        v_done = sem("v_done")
        v_stored = [sem(f"v_stored{k}") for k in range(2)]
        ones_done = sem("ones_done")
        QK = 2 * MC
        start_from_one(nc, (part_stored, v_done, v_stored, whole_done,))
        block = ctx.enter_context(nc.Block())
        JOBS = 2 * experts
        trips = B // 2

        def put_source(sp, n, i):
            bb, e = divmod(n, experts)
            sp.dma_start(s_sb[:, n % 2], src[e].rearrange("k p b t -> p k b t")[:, :, bass.ds(2 * i + bb, 1), :]
                         .rearrange("p k o t -> p k (o t)")).then_inc(s_loaded[n % 2], 16)

        @block.sync
        def _(sp):
            for e in range(experts):
                sp.dma_start(w_sb[:, e], w_qkv[e].rearrange("(k p) n -> p k n", p=P)).then_inc(w_loaded, 16)
                sp.dma_start(col_sb[:, e], cols[e]).then_inc(w_loaded, 16)
                sp.dma_start(vb_sb[:, e], v_bias[e:e + 1].partition_broadcast(P)).then_inc(w_loaded, 16)
            put_source(sp, 0, 0)
            put_source(sp, 1, 0)

            def trip(i, last):
                for n in range(JOBS):
                    job = i * JOBS + n
                    bb, e = divmod(n, experts)
                    u = (2 * i + bb) * G + e * U
                    u = u if last else sp.snap(u)
                    for m in range(max(QK, NT)):
                        if m < QK:
                            dst = q_parts if m < MC else k_parts
                            g = 2 * (m % MC)
                            sp.wait_ge(part_done[2], QK * job + m + 1)
                            for half in range(2):
                                sp.dma_start(dst[bass.ds(u + g + half, 1)].rearrange("o s r t -> r (o s) t"),
                                               part[half * 64:half * 64 + 64, m % 2]).then_inc(part_stored[m % 2], 16)
                        if m < NT:
                            lo, hi = TT[m]
                            sp.wait_ge(v_done, NT * job + m + 2)
                            sp.dma_start(v_aug[bass.ds(u, G), lo:hi].rearrange("g t n -> t g n"),
                                         v_sb[0:hi - lo, m % 2].rearrange("p g h d -> p g (h d)")).then_inc(v_stored[m % 2], 16)
                    if n + 2 < JOBS:
                        put_source(sp, n + 2, i)
                    elif not last:
                        put_source(sp, n + 2 - JOBS, i + 1)
            if trips > 1:
                with sp.Fori(0, trips - 1) as i:
                    trip(i, False)
            trip(trips - 1, True)
            for k in range(2):
                sp.wait_ge(part_stored[k], 32 * (QK // 2) * JOBS * trips + 1)
                sp.wait_ge(v_stored[k], 16 * (NT // 2) * JOBS * trips + 1)

        @block.tensor
        def _(pe):
            pe.wait_ge(w_loaded, 48 * experts)
            with pe.Fori(0, trips) as i:
                for n in range(JOBS):
                    bb, e = divmod(n, experts)
                    job = i * JOBS + n
                    pe.wait_ge(s_loaded[n % 2], i * (16 * (JOBS // 2)) + 16 * (n // 2 + 1))
                    for m in range(max(QK, NT)):
                        if m < QK:
                            if n or m >= 2:
                                pe.wait_ge(whole_done, QK * job + m)
                            else:
                                pe.wait_ge(whole_done, QK * job + 1)
                            for lo, hi in COLS_OF:
                                for c in range(KC):
                                    mm = nc.tensor.matmul(qk_ps[m % 2][:, lo:hi], w_sb[:, e, c, m * P:(m + 1) * P],
                                                          s_sb[:, n % 2, c, lo:hi], start=(c == 0), stop=(c == KC - 1))
                            mm.then_inc(qk_mm, 1)
                        if m < NT:
                            lo, hi = TT[m]
                            if n or m >= 2:
                                pe.wait_ge(v_done, NT * job + m)
                            else:
                                pe.wait_ge(v_done, NT * job + 1)
                            for c in range(KC):
                                mm = nc.tensor.matmul(v_ps[m % 2][0:hi - lo, 0:F], s_sb[:, n % 2, c, lo:hi],
                                                      w_sb[:, e, c, 2 * F:3 * F], start=(c == 0), stop=(c == KC - 1))
                            mm.then_inc(v_mm, 1)

        @block.scalar
        def _(act):
            with act.Fori(0, trips) as i:
                for n in range(JOBS):
                    job = i * JOBS + n
                    for m in range(QK):
                        count = QK * job + m + 1
                        k = m % 2
                        act.wait_ge(whole_done, count + 1)
                        act.wait_ge(part_stored[k], 32 * ((QK // 2) * job + m // 2) + 1)
                        nc.scalar.activation(part[:, k, 0], whole[:, k], ACT.Copy).then_inc(part_done[0], 1)
                        act.wait_ge(rest_done, count)
                        nc.scalar.activation(part[:, k, 1], rest[:, k], ACT.Copy).then_inc(part_done[1], 1)

        @block.vector
        def _(dve):
            nc.vector.memset(v_sb[:], 1.0).then_inc(ones_done, 1)
            dve.wait_ge(ones_done, 1)
            dve.wait_ge(w_loaded, 48 * experts)
            with dve.Fori(0, trips) as i:
                for n in range(JOBS):
                    bb, e = divmod(n, experts)
                    job = i * JOBS + n

                    def last_part(m):
                        k = m % 2
                        dve.wait_ge(part_done[1], QK * job + m + 1)
                        nc.vector.tensor_tensor(part[:, k, 2], rest[:, k], part[:, k, 1], ALU.subtract
                                                ).then_inc(part_done[2], 1)

                    for m in range(max(QK, NT)):
                        if m < QK:
                            k = m % 2
                            dve.wait_ge(qk_mm, QK * job + m + 1)
                            nc.vector.tensor_scalar(whole[:, k], qk_ps[k][:, 0:T], col_sb[:, e, m:m + 1],
                                                    scale if m < MC else 1.0, ALU.add, ALU.mult).then_inc(whole_done, 1)
                        if m < NT:
                            lo, hi = TT[m]
                            dve.wait_ge(v_mm, NT * job + m + 1)
                            dve.wait_ge(v_stored[m % 2], 16 * ((NT // 2) * job + m // 2) + 1)
                            nc.vector.tensor_tensor(v_sb[0:hi - lo, m % 2, :, :, 0:HD],
                                                    v_ps[m % 2][0:hi - lo, 0:F].rearrange("p (g h d) -> p g h d", g=G, h=4),
                                                    vb_sb[0:hi - lo, e].rearrange("p (g h d) -> p g h d", g=G, h=4), ALU.add
                                                    ).then_inc(v_done, 1)
                        if m < QK:
                            dve.wait_ge(part_done[0], QK * job + m + 1)
                            nc.vector.tensor_tensor(rest[:, k], whole[:, k], part[:, k, 0], ALU.subtract).then_inc(rest_done, 1)
                            last_part(m)


def stage_encode(nc, n_in, w1, w2, cols, e_out):
    D = D_EXPERT
    with ExitStack() as ctx:
        sems = []
        ctx.callback(end_stage, nc, sems)
        sb = lambda n, shape, dt=F32: ctx.enter_context(nc.sbuf_tensor(f"enc_{n}", shape, dt))

        def sem(n):
            sems.append(nc.alloc_semaphore(f"enc_{n}"))
            return sems[-1]

        w1_sb = sb("w1", [P, E, D])
        w2_sb = sb("w2", [P, E, 2, D])
        col_sb = sb("cols", [P, E, 8])
        avg = sb("avg", [P, P])
        eps_sb = sb("eps", [P, 1])
        n_sb = sb("n", [P, 2, T])
        a_sb = sb("a", [P, 2, 2, T])
        x_sb = sb("x", [P, 2, 2, T])
        sq = sb("sq", [P, 2, T])
        r_sb = sb("r", [P, T])
        h_sb = sb("h", [P, 2, 2, T])
        a_ps = [ctx.enter_context(nc.psum_tensor(f"enc_a_ps{k}", [P, 2 * BANK], F32)) for k in range(2)]
        m_ps = ctx.enter_context(nc.psum_tensor("enc_m_ps", [P, 2 * BANK], F32))
        w_loaded = sem("w_loaded")
        n_loaded = [sem(f"n_loaded{k}") for k in range(2)]
        const_done = sem("const_done")
        a_mm, a_out, x_mm, x_out = sem("a_mm"), sem("a_out"), sem("x_mm"), sem("x_out")
        mean_mm, var_mm = sem("mean_mm"), sem("var_mm")
        d_done, sq_done, y_done, h_done = sem("d_done"), sem("sq_done"), sem("y_done"), sem("h_done")
        root_done, r_done = sem("root_done"), sem("r_done")
        stored = [sem(f"stored{k}") for k in range(2)]
        JOBS, trips = 2 * E, B // 2
        start_from_one(nc, (a_mm, root_done, stored, var_mm, x_out, y_done,))
        block = ctx.enter_context(nc.Block())

        @block.sync
        def _(sp):
            for e in range(E):
                sp.dma_start(w1_sb[:, e], w1[e]).then_inc(w_loaded, 16)
                sp.dma_start(w2_sb[:, e], w2[e].rearrange("(k p) n -> p k n", p=P)).then_inc(w_loaded, 16)
                sp.dma_start(col_sb[:, e], cols[e]).then_inc(w_loaded, 16)
            with sp.Fori(0, trips) as i:
                for n in range(JOBS):
                    if n % E == 0:
                        bb = n // E
                        sp.wait_ge(a_mm, i * (2 * JOBS) + 1)
                        sp.dma_start(n_sb[:, bb], n_in[:, bass.ds(2 * i + bb, 1)].rearrange("p o t -> p (o t)")
                                     ).then_inc(n_loaded[bb], 16)
                for n in range(JOBS):
                    sp.wait_ge(h_done, (i * JOBS + n) * 2 + 2)
                    sp.dma_start(e_out[n % E].rearrange("c p b t -> p c b t")[:, :, bass.ds(2 * i + n // E, 1)]
                                 .rearrange("p c o t -> p c (o t)"), h_sb[:, n % 2]).then_inc(stored[n % 2], 16)
            for k in range(2):
                sp.wait_ge(stored[k], 16 * (JOBS // 2) * trips + 1)

        @block.tensor
        def _(pe):
            pe.wait_ge(w_loaded, 48 * E)
            pe.wait_ge(const_done, 1)
            with pe.Fori(0, trips) as i:
                def first(e):
                    if e % E == 0:
                        pe.wait_ge(n_loaded[e // E], i * 16 + 16)
                    for m in range(2):
                        pe.wait_ge(x_out, ((i * JOBS + e - 1) * 2 + m + 1 if e else i * (JOBS * 2)) + 1)
                        for lo, hi in COLS_OF:
                            mm = nc.tensor.matmul(a_ps[m][:, lo:hi], w1_sb[:, e % E, m * P:(m + 1) * P], n_sb[:, e // E, lo:hi],
                                                  start=True, stop=True)
                        mm.then_inc(a_mm, 1)

                def second(e):
                    for m in range(2):
                        pe.wait_ge(a_out, (i * JOBS + e) * 2 + 2)
                        for lo, hi in COLS_OF:
                            for c in range(2):
                                mm = nc.tensor.matmul(a_ps[m][:, lo:hi], w2_sb[:, e % E, c, m * P:(m + 1) * P],
                                                      a_sb[:, e % 2, c, lo:hi], start=(c == 0), stop=(c == 1))
                        mm.then_inc(x_mm, 1)

                def mean(e):
                    pe.wait_ge(x_out, (i * JOBS + e) * 2 + 3)
                    pe.wait_ge(root_done, i * JOBS + e + 1)
                    for lo, hi in COLS_OF:
                        for c in range(2):
                            mm = nc.tensor.matmul(m_ps[:, lo:hi], avg[:], x_sb[:, e % 2, c, lo:hi], start=(c == 0), stop=(c == 1))
                    mm.then_inc(mean_mm, 1)

                def variance(e):
                    pe.wait_ge(sq_done, (i * JOBS + e) * 2 + 2)
                    for lo, hi in COLS_OF:
                        for c in range(2):
                            mm = nc.tensor.matmul(m_ps[:, lo:hi], avg[:], sq[:, c, lo:hi], start=(c == 0), stop=(c == 1))
                    mm.then_inc(var_mm, 1)

                first(0)
                second(0)
                first(1)
                for e in range(JOBS):
                    mean(e)
                    if e + 1 < JOBS:
                        second(e + 1)
                    variance(e)
                    if e + 2 < JOBS:
                        first(e + 2)

        @block.scalar
        def _(act):
            act.wait_ge(const_done, 1)
            act.wait_ge(w_loaded, 48 * E)
            with act.Fori(0, trips) as i:
                def hidden(e):
                    for m in range(2):
                        act.wait_ge(a_mm, (i * JOBS + e) * 2 + m + 2)
                        nc.scalar.activation(a_sb[:, e % 2, m], a_ps[m][:, 0:T], ACT.Relu, bias=col_sb[:, e % E, m:m + 1]
                                             ).then_inc(a_out, 1)

                def scaled(e):
                    for m in range(2):
                        act.wait_ge(y_done, (i * JOBS + e) * 2 + m + 2)
                        act.wait_ge(stored[e % 2], i * (16 * JOBS // 2) + 16 * (e // 2) + 1)
                        nc.scalar.activation(h_sb[:, e % 2, m], x_sb[:, e % 2, m], ACT.Identity, bias=col_sb[:, e % E, 6 + m:7 + m],
                                             scale=col_sb[:, e % E, 4 + m:5 + m]).then_inc(h_done, 1)

                hidden(0)
                for e in range(JOBS):
                    for m in range(2):
                        act.wait_ge(x_mm, (i * JOBS + e) * 2 + m + 1)
                        if e >= 2:
                            act.wait_ge(h_done, (i * JOBS + e - 1) * 2)
                        nc.scalar.activation(x_sb[:, e % 2, m], a_ps[m][:, 0:T], ACT.Identity, bias=col_sb[:, e % E, 2 + m:3 + m]
                                             ).then_inc(x_out, 1)
                    if e + 1 < JOBS:
                        hidden(e + 1)
                    for m in range(2):
                        act.wait_ge(d_done, (i * JOBS + e) * 2 + m + 1)
                        act.wait_ge(var_mm, i * JOBS + e + 1)
                        nc.scalar.activation(sq[:, m], x_sb[:, e % 2, m], ACT.Square).then_inc(sq_done, 1)
                    if e:
                        scaled(e - 1)
                    act.wait_ge(var_mm, i * JOBS + e + 2)
                    act.wait_ge(y_done, (i * JOBS + e) * 2 + 1)
                    nc.scalar.activation(r_sb[:], m_ps[:, 0:T], ACT.Sqrt, bias=eps_sb[:]).then_inc(root_done, 1)
                scaled(JOBS - 1)

        @block.vector
        def _(dve):
            nc.vector.memset(eps_sb[:], EPS)
            nc.vector.memset(avg[:], 1.0 / D).then_inc(const_done, 1)
            with dve.Fori(0, trips) as i:
                for e in range(JOBS):
                    dve.wait_ge(mean_mm, i * JOBS + e + 1)
                    for m in range(2):
                        nc.vector.tensor_tensor(x_sb[:, e % 2, m], x_sb[:, e % 2, m], m_ps[:, 0:T], ALU.subtract
                                                ).then_inc(d_done, 1)
                    dve.wait_ge(root_done, i * JOBS + e + 2)
                    nc.vector.reciprocal(r_sb[:], r_sb[:]).then_inc(r_done, 1)
                    dve.wait_ge(r_done, i * JOBS + e + 1)
                    dve.wait_ge(sq_done, (i * JOBS + e) * 2 + 2)
                    for m in range(2):
                        nc.vector.tensor_tensor(x_sb[:, e % 2, m], x_sb[:, e % 2, m], r_sb[:], ALU.mult).then_inc(y_done, 1)




def stage_lstm_inputs(nc, o_in, sum_in, w_o, w_i, cols, xw):
    D = D_EXPERT
    with ExitStack() as ctx:
        sems = []
        ctx.callback(end_stage, nc, sems)
        sb = lambda n, shape, dt=F32: ctx.enter_context(nc.sbuf_tensor(f"xw_{n}", shape, dt))

        def sem(n):
            sems.append(nc.alloc_semaphore(f"xw_{n}"))
            return sems[-1]

        wo_sb = sb("wo", [P, E, 2, D])
        wi_sb = sb("wi", [P, E, 2, 2, 4 * D])
        col_sb = sb("cols", [P, E, 18])
        o_sb = sb("o", [P, 2, 2, B, CT])
        sum_sb = sb("sum", [P, 2, 2, B, CT])
        a_sb = sb("a", [P, 2, 2, CW])
        x_sb = sb("x", [P, 2, 2, CT, 8, B])
        a_ps = [ctx.enter_context(nc.psum_tensor(f"xw_a_ps{k}", [P, BANK], F32)) for k in range(2)]
        x_ps = [ctx.enter_context(nc.psum_tensor(f"xw_x_ps{k}", [P, BANK], F32)) for k in range(4)]
        w_loaded = sem("w_loaded")
        o_loaded = [sem(f"o_loaded{k}") for k in range(2)]
        share_step = sem("share_step")
        a_mm, a_out = sem("a_mm"), sem("a_out")
        x_mm = sem("x_mm")
        x_out = sem("x_out")
        stored = [sem(f"stored{k}") for k in range(2)]
        start_from_one(nc, (a_out, stored, x_out,))
        block = ctx.enter_context(nc.Block())
        trips = T // CT
        half = E // 2

        def put_o(sp, i, e):
            for c in range(2):
                for dst, src in ((o_sb, o_in), (sum_sb, sum_in)):
                    sp.dma_start(dst[:, e % 2, c], src[e].rearrange("b (c p) t -> c p b t", p=P)[c][:, :, bass.ds(i * CT, CT)]
                                 ).then_inc(o_loaded[e % 2], 16)

        @block.sync
        def _(sp):
            for e in range(E):
                sp.dma_start(wo_sb[:, e], w_o[e].rearrange("(k p) n -> p k n", p=P)).then_inc(w_loaded, 16)
                sp.dma_start(col_sb[:, e], cols[e]).then_inc(w_loaded, 16)
                for d in range(2):
                    sp.dma_start(wi_sb[:, e, d], w_i[d][e].rearrange("(k p) n -> p k n", p=P)).then_inc(w_loaded, 16)
            put_o(sp, 0, 0)
            put_o(sp, 0, 1)

            def trip(i, last):
                for e in range(E):
                    job = i * E + e
                    sp.wait_ge(a_mm, job * 2 + 2)
                    if e + 2 < E:
                        put_o(sp, i, e + 2)
                    elif not last:
                        put_o(sp, i + 1, e + 2 - E)
                    for d in range(2):
                        sp.wait_ge(x_out, job * 16 + 8 * d + 8 + 1)
                        sp.dma_start(xw[d, e][:, bass.ds(i * CT, CT)].rearrange("p t g -> p (t g)"),
                                     x_sb[:, e % 2, d].rearrange("p t m b -> p (t m b)")).then_inc(stored[e % 2], 16)
            with sp.Fori(0, trips - 1) as i:
                trip(i, False)
            trip(trips - 1, True)
            for k in range(2):
                sp.wait_ge(stored[k], 32 * half * trips + 1)

        @block.tensor
        def _(pe):
            pe.wait_ge(w_loaded, 64 * E)
            with pe.Fori(0, trips) as i:
                def attend(e):
                    pe.wait_ge(share_step, (i * E + e) * 2 + 2)
                    for m in range(2):
                        pe.wait_ge(a_out, ((i * E + e - 1) * 2 + m + 1 if e else i * (E * 2)) + 1)
                        for c in range(2):
                            mm = nc.tensor.matmul(a_ps[m][:, 0:CW], wo_sb[:, e, c, m * P:(m + 1) * P],
                                                  o_sb[:, e % 2, c].rearrange("p b t -> p t b"), start=(c == 0), stop=(c == 1))
                        mm.then_inc(a_mm, 1)
                attend(0)
                for e in range(E):
                    job = i * E + e
                    for n in range(16):
                        d, m = divmod(n, 8)
                        if n == 0:
                            pe.wait_ge(a_out, job * 2 + 3)
                        if e or n >= 4:
                            pe.wait_ge(x_out, job * 16 + n - 3 + 1)
                        else:
                            pe.wait_ge(x_out, job * 16 + 1)
                        for c in range(2):
                            mm = nc.tensor.matmul(x_ps[n % 4][:, 0:CW], wi_sb[:, e, d, c, COLS[m] * P:(COLS[m] + 1) * P],
                                                  a_sb[:, e % 2, c], start=(c == 0), stop=(c == 1))
                        mm.then_inc(x_mm, 1)
                        if n == 7 and e + 1 < E:
                            attend(e + 1)

        def put_x(eng, i, e, n):
            d, m = divmod(n, 8)
            job = i * E + e
            eng.wait_ge(x_mm, job * 16 + n + 1)
            if n < 2:
                eng.wait_ge(stored[e % 2], i * (32 * half) + 32 * (e // 2) + 1)
            out = x_sb[:, e % 2, d, :, m]
            src = x_ps[n % 4][:, 0:CW].rearrange("p (t b) -> p t b", b=B)
            return out, src, col_sb[:, e, 2 + 8 * d + COLS[m]:3 + 8 * d + COLS[m]]

        @block.scalar
        def _(act):
            act.wait_ge(w_loaded, 64 * E)
            with act.Fori(0, trips) as i:
                def attended(e):
                    for m in range(2):
                        act.wait_ge(a_mm, (i * E + e) * 2 + m + 1)
                        if e >= 2:
                            act.wait_ge(x_mm, (i * E + e - 1) * 16)
                        nc.scalar.activation(a_sb[:, e % 2, m], a_ps[m][:, 0:CW], ACT.Identity, bias=col_sb[:, e, m:m + 1]
                                             ).then_inc(a_out, 1)
                attended(0)
                for e in range(E):
                    for n in range(16):
                        out, src, bias = put_x(act, i, e, n)
                        nc.scalar.activation(out, src, ACT.Identity, bias=bias).then_inc(x_out, 1)
                        if n == 8 and e + 1 < E:
                            attended(e + 1)

        @block.vector
        def _(dve):
            dve.wait_ge(w_loaded, 64 * E)
            with dve.Fori(0, trips) as i:
                def share(e):
                    dve.wait_ge(o_loaded[e % 2], i * (64 * half) + 64 * (e // 2 + 1))
                    flat = lambda x: x[:, e % 2].rearrange("p c b t -> p (c b t)")
                    nc.vector.reciprocal(flat(sum_sb), flat(sum_sb)).then_inc(share_step, 1)
                    dve.wait_ge(share_step, (i * E + e) * 2 + 1)
                    nc.vector.tensor_tensor(flat(o_sb), flat(o_sb), flat(sum_sb), ALU.mult).then_inc(share_step, 1)
                for e in range(E):
                    share(e)


def stage_decode(nc, mem, n_in, h_in, w_s1, w_s2, w_t1, w_t2, w_d1, w_d2, w_r, cols, h_out):
    D = D_EXPERT
    S1, S2, T1, T2, D1, D2, GG, BETA, RB = 0, 2, 4, 6, 8, 10, 11, 12, 13
    with ExitStack() as ctx:
        sems = []
        ctx.callback(end_stage, nc, sems)
        sb = lambda n, shape, dt=F32: ctx.enter_context(nc.sbuf_tensor(f"dec_{n}", shape, dt))

        def sem(n):
            sems.append(nc.alloc_semaphore(f"dec_{n}"))
            return sems[-1]

        s1, t1 = sb("s1", [P, E, 4, D]), sb("t1", [P, E, 4, D])
        s2, t2, d1 = sb("s2", [P, E, 2, D]), sb("t2", [P, E, 2, D]), sb("d1", [P, E, 2, D])
        d2 = sb("d2", [P, E, 2, P])
        wr_sb = sb("wr", [P, E])
        wr_rep = sb("wr_rep", [P, E, P])
        col_sb = sb("cols", [P, E, 14])
        avg = sb("avg", [P, P])
        eps_sb = sb("eps", [P, 1])
        m_sb = sb("m", [P, 2, 4, CW])
        n_sb = sb("n", [P, B, CT])
        h_sb = sb("h", [P, B, CT])
        log = sb("log", [P, E, CW])
        top = sb("top", [P, 2, CW])
        hid = sb("hid", [P, 4, CW])
        gate = sb("gate", [P, 4, CW])
        g_sb = sb("g", [P, 2, CW])
        dh = sb("dh", [P, 2, CW])
        x_sb = sb("x", [P, 2, CW])
        sq = sb("sq", [P, CW])
        r_sb = sb("r", [P, CW])
        acc = sb("acc", [P, CW])
        u_ps = [ctx.enter_context(nc.psum_tensor(f"dec_u_ps{k}", [P, BANK], F32)) for k in range(4)]
        d_ps = [ctx.enter_context(nc.psum_tensor(f"dec_d_ps{k}", [P, BANK], F32)) for k in range(2)]
        y_ps = ctx.enter_context(nc.psum_tensor("dec_y_ps", [P, BANK], F32))
        m_ps = ctx.enter_context(nc.psum_tensor("dec_m_ps", [P, BANK], F32))
        w_loaded, const_done = sem("w_loaded"), sem("const_done")
        rep_done = sem("rep_done")
        m_loaded = [sem(f"m_loaded{k}") for k in range(2)]
        n_loaded, h_loaded = sem("n_loaded"), sem("h_loaded")
        log_mm, log_out = sem("log_mm"), sem("log_out")
        soft = sem("soft")
        exp_done = sem("exp_done")
        u_mm, hid_out = sem("u_mm"), sem("hid_out")
        v_mm, gate_out = sem("v_mm"), sem("gate_out")
        g_done, d_mm, dh_out = sem("g_done"), sem("d_mm"), sem("dh_out")
        y_mm, x_out, mean_mm, sub_done, sq_done, var_mm, root_done = (
            sem(n) for n in ("y_mm", "x_out", "mean_mm", "sub_done", "sq_done", "var_mm", "root_done"))
        fin = sem("fin")
        ready = sem("ready")
        stored = sem("stored")
        SOFT, FIN = 15, 5
        start_from_one(nc, (d_mm, dh_out, fin, g_done, gate_out, hid_out, log_mm, root_done, stored, v_mm, var_mm, x_out, y_mm,))
        block = ctx.enter_context(nc.Block())
        trips = T // CT
        half = E // 2

        def put_mem(sp, i, e):
            for k in range(4):
                sp.dma_start(m_sb[:, e % 2, k], mem[k // 2, e, k % 2][:, bass.ds(i * CT, CT)].rearrange("p t b -> p (t b)")
                             ).then_inc(m_loaded[e % 2], 16)

        @block.sync
        def _(sp):
            loads = 0
            for e in range(E):
                for dst, src in ((s1, w_s1), (s2, w_s2), (t1, w_t1), (t2, w_t2), (d1, w_d1), (d2, w_d2)):
                    sp.dma_start(dst[:, e], src[e].rearrange("(k p) n -> p k n", p=P)).then_inc(w_loaded, 16)
                sp.dma_start(col_sb[:, e], cols[e]).then_inc(w_loaded, 16)
            sp.dma_start(wr_sb[:], w_r).then_inc(w_loaded, 16)
            put_mem(sp, 0, 0)
            put_mem(sp, 0, 1)

            def trip(i, last):
                sp.wait_ge(log_mm, i * E + 1)
                sp.dma_start(n_sb[:], n_in[:, :, bass.ds(i * CT, CT)]).then_inc(n_loaded, 16)
                sp.wait_ge(stored, i * 16 + 1)
                sp.dma_start(h_sb[:], h_in[:, :, bass.ds(i * CT, CT)]).then_inc(h_loaded, 16)
                for e in range(E):
                    sp.wait_ge(u_mm, (i * E + e) * 4 + 4)
                    if e + 2 < E:
                        put_mem(sp, i, e + 2)
                    elif not last:
                        put_mem(sp, i + 1, e + 2 - E)
                sp.wait_ge(ready, i + 1)
                sp.dma_start(h_out[:, :, bass.ds(i * CT, CT)], h_sb[:]).then_inc(stored, 16)
            with sp.Fori(0, trips - 1) as i:
                trip(i, False)
            trip(trips - 1, True)
            sp.wait_ge(stored, 16 * trips + 1)
        WL = 16 * (7 * E + 1)

        @block.tensor
        def _(pe):
            pe.wait_ge(w_loaded, WL)
            pe.wait_ge(rep_done, E)
            with pe.Fori(0, trips) as i:
                pe.wait_ge(n_loaded, i * 16 + 16)
                pe.wait_ge(hid_out, i * (E * 4) + 1)
                for e in range(E):
                    pe.wait_ge(gate_out, i * (E * 4) + 1)
                    nc.tensor.matmul(u_ps[e][:, 0:CW], wr_rep[:, e], n_sb[:].rearrange("p b t -> p t b"),
                                     start=True, stop=True).then_inc(log_mm, 1)

                def mean(e):
                    pe.wait_ge(x_out, i * E + e + 2)
                    pe.wait_ge(root_done, i * E + e + 1)
                    nc.tensor.matmul(m_ps[:, 0:CW], avg[:], x_sb[:, e % 2], start=True, stop=True).then_inc(mean_mm, 1)

                def variance(e):
                    pe.wait_ge(sq_done, i * E + e + 1)
                    nc.tensor.matmul(m_ps[:, 0:CW], avg[:], sq[:], start=True, stop=True).then_inc(var_mm, 1)

                def first(e, ns):
                    job = i * E + e
                    if 0 in ns:
                        pe.wait_ge(m_loaded[e % 2], i * (64 * half) + 64 * (e // 2 + 1))
                    for n in ns:
                        w, m = (s1, t1)[n // 2], n % 2
                        if e:
                            pe.wait_ge(gate_out, (job - 1) * 4 + n + 2)
                        else:
                            pe.wait_ge(log_out, i * E + n + 1)
                        for c in range(4):
                            mm = nc.tensor.matmul(u_ps[n][:, 0:CW], w[:, e, c, m * P:(m + 1) * P], m_sb[:, e % 2, c],
                                                  start=(c == 0), stop=(c == 3))
                        mm.then_inc(u_mm, 1)

                def second(e):
                    job = i * E + e
                    for n in range(4):
                        w, m = (s2, t2)[n // 2], n % 2
                        pe.wait_ge(hid_out, job * 4 + max(n + 1, 2 * (n // 2) + 2) + 1)
                        for c in range(2):
                            mm = nc.tensor.matmul(u_ps[n][:, 0:CW], w[:, e, c, m * P:(m + 1) * P], hid[:, 2 * (n // 2) + c],
                                                  start=(c == 0), stop=(c == 1))
                        mm.then_inc(v_mm, 1)

                def decode_first(e):
                    job = i * E + e
                    pe.wait_ge(g_done, job * 2 + 3)
                    for m in range(2):
                        pe.wait_ge(dh_out, job * 2 + 1)
                        for c in range(2):
                            mm = nc.tensor.matmul(d_ps[m][:, 0:CW], d1[:, e, c, m * P:(m + 1) * P], g_sb[:, c],
                                                  start=(c == 0), stop=(c == 1))
                        mm.then_inc(d_mm, 1)

                def decode_second(e):
                    job = i * E + e
                    pe.wait_ge(dh_out, job * 2 + 3)
                    pe.wait_ge(x_out, job + 1)
                    for c in range(2):
                        mm = nc.tensor.matmul(y_ps[:, 0:CW], d2[:, e, c], dh[:, c], start=(c == 0), stop=(c == 1))
                    mm.then_inc(y_mm, 1)

                first(0, (0, 1, 2, 3))
                for e in range(E):
                    second(e)
                    if e:
                        mean(e - 1)
                    if e + 1 < E:
                        first(e + 1, (0, 1))
                    decode_first(e)
                    if e:
                        variance(e - 1)
                    if e + 1 < E:
                        first(e + 1, (2, 3))
                    decode_second(e)
                mean(E - 1)
                variance(E - 1)

        @block.scalar
        def _(act):
            act.wait_ge(w_loaded, WL)
            act.wait_ge(const_done, 1)
            with act.Fori(0, trips) as i:
                act.wait_ge(soft, i * SOFT + 7)
                nc.scalar.activation(log[:].rearrange("p e n -> p (e n)"), log[:].rearrange("p e n -> p (e n)"), ACT.Exp
                                     ).then_inc(exp_done, 1)

                def square(e):
                    act.wait_ge(sub_done, i * E + e + 1)
                    act.wait_ge(var_mm, i * E + e + 1)
                    nc.scalar.activation(sq[:], x_sb[:, e % 2], ACT.Square).then_inc(sq_done, 1)

                def root(e):
                    act.wait_ge(var_mm, i * E + e + 2)
                    act.wait_ge(fin, (i * E + e) * FIN + 1)
                    nc.scalar.activation(r_sb[:], m_ps[:, 0:CW], ACT.Sqrt, bias=eps_sb[:]).then_inc(root_done, 1)

                def hidden(e, ns):
                    job = i * E + e
                    for n in ns:
                        act.wait_ge(u_mm, job * 4 + n + 1)
                        act.wait_ge(v_mm, job * 4 + 1)
                        at = (S1, T1)[n // 2] + n % 2
                        nc.scalar.activation(hid[:, n], u_ps[n][:, 0:CW], ACT.Relu, bias=col_sb[:, e, at:at + 1]
                                             ).then_inc(hid_out, 1)

                hidden(0, (0, 1, 2, 3))
                for e in range(E):
                    job = i * E + e
                    for n in range(4):
                        act.wait_ge(v_mm, job * 4 + n + 2)
                        act.wait_ge(g_done, job * 2 + 1)
                        at = (S2, T2)[n // 2] + n % 2
                        nc.scalar.activation(gate[:, n], u_ps[n][:, 0:CW], ACT.Sigmoid if n < 2 else ACT.Tanh,
                                             bias=col_sb[:, e, at:at + 1]).then_inc(gate_out, 1)
                    if e:
                        square(e - 1)
                    if e + 1 < E:
                        hidden(e + 1, (0, 1))
                    if e:
                        root(e - 1)
                    if e + 1 < E:
                        hidden(e + 1, (2, 3))
                square(E - 1)
                root(E - 1)

        @block.vector
        def _(dve):
            nc.vector.memset(eps_sb[:], EPS)
            nc.vector.memset(avg[:], 1.0 / P).then_inc(const_done, 1)
            dve.wait_ge(w_loaded, WL)
            for e in range(E):
                nc.vector.tensor_copy(wr_rep[:, e], wr_sb[:, e:e + 1].to_broadcast([P, P])).then_inc(rep_done, 1)
            with dve.Fori(0, trips) as i:
                at = i * SOFT
                dve.wait_ge(fin, i * (FIN * E) + 1)
                for e in range(E):
                    dve.wait_ge(log_mm, i * E + e + 2)
                    nc.vector.tensor_scalar(log[:, e], u_ps[e][:, 0:CW], col_sb[:, e, RB:RB + 1], None, ALU.add
                                            ).then_inc(log_out, 1)
                dve.wait_ge(log_out, i * E + E)
                for k in range(2):
                    nc.vector.tensor_tensor(top[:, k], log[:, 2 * k], log[:, 2 * k + 1], ALU.max).then_inc(soft, 1)
                dve.wait_ge(soft, at + 2)
                nc.vector.tensor_tensor(top[:, 0], top[:, 0], top[:, 1], ALU.max).then_inc(soft, 1)
                dve.wait_ge(soft, at + 3)
                for e in range(E):
                    nc.vector.tensor_tensor(log[:, e], log[:, e], top[:, 0], ALU.subtract).then_inc(soft, 1)
                dve.wait_ge(exp_done, i + 1)
                for k in range(2):
                    nc.vector.tensor_tensor(top[:, k], log[:, 2 * k], log[:, 2 * k + 1], ALU.add).then_inc(soft, 1)
                dve.wait_ge(soft, at + 9)
                nc.vector.tensor_tensor(top[:, 0], top[:, 0], top[:, 1], ALU.add).then_inc(soft, 1)
                dve.wait_ge(soft, at + 10)
                nc.vector.reciprocal(top[:, 1], top[:, 0]).then_inc(soft, 1)
                dve.wait_ge(soft, at + 11)
                for e in range(E):
                    nc.vector.tensor_tensor(log[:, e], log[:, e], top[:, 1], ALU.mult).then_inc(soft, 1)

                def sub(e):
                    dve.wait_ge(mean_mm, i * E + e + 1)
                    nc.vector.tensor_tensor(x_sb[:, e % 2], x_sb[:, e % 2], m_ps[:, 0:CW], ALU.subtract).then_inc(sub_done, 1)

                def tail(e):
                    f = (i * E + e) * FIN
                    dve.wait_ge(root_done, i * E + e + 2)
                    nc.vector.reciprocal(r_sb[:], r_sb[:]).then_inc(fin, 1)
                    dve.wait_ge(fin, f + 2)
                    dve.wait_ge(sq_done, i * E + e + 1)
                    x = x_sb[:, e % 2]
                    nc.vector.tensor_tensor(x, x, r_sb[:], ALU.mult).then_inc(fin, 1)
                    dve.wait_ge(fin, f + 3)
                    nc.vector.tensor_scalar(x, x, col_sb[:, e, GG:GG + 1], col_sb[:, e, BETA:BETA + 1], ALU.mult, ALU.add
                                            ).then_inc(fin, 1)
                    dve.wait_ge(fin, f + 3 + 1)
                    dve.wait_ge(soft, at + SOFT)
                    dst = x if e else acc[:]
                    nc.vector.tensor_tensor(dst, x, log[:, e], ALU.mult).then_inc(fin, 1)
                    dve.wait_ge(fin, f + 4 + 1)
                    if e:
                        nc.vector.tensor_tensor(acc[:], acc[:], x, ALU.add).then_inc(fin, 1)
                    else:
                        nc.vector.memset(top[:, 0, 0:1], 0.0).then_inc(fin, 1)

                for e in range(E):
                    job = i * E + e
                    for m in range(2):
                        dve.wait_ge(gate_out, job * 4 + 3 + m + 1)
                        dve.wait_ge(d_mm, job * 2 + 1)
                        nc.vector.tensor_tensor(g_sb[:, m], gate[:, m], gate[:, 2 + m], ALU.mult).then_inc(g_done, 1)
                    if e:
                        sub(e - 1)
                    for m in range(2):
                        dve.wait_ge(d_mm, job * 2 + m + 2)
                        dve.wait_ge(y_mm, job + 1)
                        nc.vector.tensor_scalar(dh[:, m], d_ps[m][:, 0:CW], col_sb[:, e, D1 + m:D1 + m + 1], 0.0, ALU.add, ALU.max
                                                ).then_inc(dh_out, 1)
                    if e:
                        tail(e - 1)
                    dve.wait_ge(y_mm, job + 2)
                    nc.vector.tensor_scalar(x_sb[:, e % 2], y_ps[:, 0:CW], col_sb[:, e, D2:D2 + 1], None, ALU.add
                                            ).then_inc(x_out, 1)
                sub(E - 1)
                tail(E - 1)
                dve.wait_ge(fin, (i * E + E) * FIN + 1)
                dve.wait_ge(h_loaded, i * 16 + 16)
                nc.vector.tensor_tensor(h_sb[:], h_sb[:], acc[:].rearrange("p (t b) -> p b t", b=B), ALU.add).then_inc(ready, 1)


def stage_retention(nc, n_in, h_in, w_q, w_k, w_v, decay, h_out):
    TT = [(lo, min(lo + P, T)) for lo in range(0, T, P)]
    NT = len(TT)
    OFF = P * (NT - 1)
    with ExitStack() as ctx:
        sems = []
        ctx.callback(end_stage, nc, sems)
        sb = lambda n, shape, dt=F32: ctx.enter_context(nc.sbuf_tensor(f"ret_{n}", shape, dt))

        def sem(n):
            sems.append(nc.alloc_semaphore(f"ret_{n}"))
            return sems[-1]

        w_sb = sb("w", [P, 3, P])
        dec_sb = sb("dec", [P, OFF + T])
        n_sb = sb("n", [P, B, T])
        h_sb = sb("h", [P, B, T])
        qk = sb("qk", [P, 2, T])
        v_sb = sb("v", [P, NT, P])
        sd = sb("sd", [P, 2, T])
        sg = sb("sg", [P, 2, T])
        a_sb = sb("a", [P, 2, T])
        s_ps = [ctx.enter_context(nc.psum_tensor(f"ret_s_ps{k}", [P, 2 * BANK], F32)) for k in range(2)]
        o_ps = ctx.enter_context(nc.psum_tensor("ret_o_ps", [P, 2 * BANK], F32))
        v_ps = [ctx.enter_context(nc.psum_tensor(f"ret_v_ps{k}", [P, BANK], F32)) for k in range(2)]
        w_loaded = sem("w_loaded")
        loaded = [sem(f"loaded{b}") for b in range(B)]
        qk_mm, qk_out, v_mm, v_out = sem("qk_mm"), sem("qk_out"), sem("v_mm"), sem("v_out")
        s_mm, sd_done, sg_done, a_done, o_mm = sem("s_mm"), sem("sd_done"), sem("sg_done"), sem("a_done"), sem("o_mm")
        ready, stored = sem("ready"), sem("stored")
        block = ctx.enter_context(nc.Block())

        @block.sync
        def _(sp):
            for n, w in enumerate((w_q, w_k, w_v)):
                sp.dma_start(w_sb[:, n], w).then_inc(w_loaded, 16)
            sp.dma_start(dec_sb[:], decay).then_inc(w_loaded, 16)
            for b in range(B):
                sp.dma_start(n_sb[:, b], n_in[:, b]).then_inc(loaded[b], 16)
                sp.dma_start(h_sb[:, b], h_in[:, b]).then_inc(loaded[b], 16)
            for b in range(B):
                sp.wait_ge(ready, b + 1)
                sp.dma_start(h_out[:, b], h_sb[:, b]).then_inc(stored, 16)
            sp.wait_ge(stored, 16 * B)

        @block.tensor
        def _(pe):
            pe.wait_ge(w_loaded, 64)
            for b in range(B):
                pe.wait_ge(loaded[b], 32)
                for n in range(2):
                    if b:
                        pe.wait_ge(sd_done, NT * b)
                    for lo, hi in COLS_OF:
                        mm = nc.tensor.matmul(s_ps[n][:, lo:hi], w_sb[:, n], n_sb[:, b, lo:hi], start=True, stop=True)
                    mm.then_inc(qk_mm, 1)
                for c, (lo, hi) in enumerate(TT):
                    if NT * b + c >= 2:
                        pe.wait_ge(v_out, NT * b + c - 1)
                    nc.tensor.matmul(v_ps[c % 2][0:hi - lo, 0:P], n_sb[:, b, lo:hi], w_sb[:, 2], start=True, stop=True
                                     ).then_inc(v_mm, 1)
                pe.wait_ge(qk_out, 2 * b + 2)

                def scores(c):
                    if c >= 2:
                        pe.wait_ge(sd_done, NT * b + c - 1)
                    k0, k1 = TT[c]
                    for lo, hi in COLS_OF:
                        mm = nc.tensor.matmul(s_ps[c % 2][0:k1 - k0, lo:hi], qk[:, 1, k0:k1], qk[:, 0, lo:hi], start=True, stop=True)
                    mm.then_inc(s_mm, 1)
                scores(0)
                scores(1)
                pe.wait_ge(v_out, NT * b + NT)
                if b:
                    pe.wait_ge(ready, b)
                for c in range(NT):
                    if c + 2 < NT:
                        scores(c + 2)
                    pe.wait_ge(a_done, NT * b + c + 1)
                    k0, k1 = TT[c]
                    for lo, hi in COLS_OF:
                        mm = nc.tensor.matmul(o_ps[:, lo:hi], v_sb[0:k1 - k0, c], a_sb[0:k1 - k0, c % 2, lo:hi],
                                              start=(c == 0), stop=(c == NT - 1))
                    mm.then_inc(o_mm, 1)

        @block.scalar
        def _(act):
            for b in range(B):
                for n in range(2):
                    act.wait_ge(qk_mm, 2 * b + n + 1)
                    nc.scalar.copy(qk[:, n], s_ps[n][:, 0:T]).then_inc(qk_out, 1)
                for c, (k0, k1) in enumerate(TT):
                    act.wait_ge(sd_done, NT * b + c + 1)
                    if NT * b + c >= 2:
                        act.wait_ge(a_done, NT * b + c - 1)
                    nc.scalar.activation(sg[0:k1 - k0, c % 2], sd[0:k1 - k0, c % 2], ACT.Sigmoid).then_inc(sg_done, 1)

        @block.vector
        def _(dve):
            for b in range(B):
                for c, (lo, hi) in enumerate(TT):
                    dve.wait_ge(v_mm, NT * b + c + 1)
                    if b and c == 0:
                        dve.wait_ge(o_mm, NT * b)
                    nc.vector.tensor_copy(v_sb[0:hi - lo, c], v_ps[c % 2][0:hi - lo, 0:P]).then_inc(v_out, 1)

                def weighted(c):
                    k0, k1 = TT[c]
                    dve.wait_ge(s_mm, NT * b + c + 1)
                    if NT * b + c >= 2:
                        dve.wait_ge(a_done, NT * b + c - 1)
                    at = OFF - P * c
                    nc.vector.tensor_tensor(sd[0:k1 - k0, c % 2], s_ps[c % 2][0:k1 - k0, 0:T], dec_sb[0:k1 - k0, at:at + T], ALU.mult
                                            ).then_inc(sd_done, 1)
                weighted(0)
                for c in range(NT):
                    if c + 1 < NT:
                        weighted(c + 1)
                    k0, k1 = TT[c]
                    dve.wait_ge(sg_done, NT * b + c + 1)
                    if NT * b + c >= 2:
                        dve.wait_ge(o_mm, NT * b + c - 1)
                    nc.vector.tensor_tensor(a_sb[0:k1 - k0, c % 2], sd[0:k1 - k0, c % 2], sg[0:k1 - k0, c % 2], ALU.mult
                                            ).then_inc(a_done, 1)
                dve.wait_ge(o_mm, NT * b + NT)
                nc.vector.tensor_tensor(h_sb[:, b], h_sb[:, b], o_ps[:, 0:T], ALU.add).then_inc(ready, 1)


def stage_softmax_attention(nc, name, q_parts, k_parts, v_aug, o_out, sum_out, units):
    with ExitStack() as ctx:
        sems = []
        ctx.callback(end_stage, nc, sems)
        sb = lambda n, shape, dt=F32: ctx.enter_context(nc.sbuf_tensor(f"{name}_{n}", shape, dt))

        def sem(n):
            sems.append(nc.alloc_semaphore(f"{name}_{n}"))
            return sems[-1]

        ROWS = STACK + MAX_PARTS
        q_sb = sb("q", [ROWS, AHEAD, QUAD, TP], BF16)
        k_sb = sb("k", [ROWS, AHEAD, QUAD, T], BF16)
        v_sb = sb("v", [P, AHEAD, TILES, P])
        probT = sb("probT", [P, 3, QUAD, T])
        negmax = sb("negmax", [P, QUAD * TILES])
        max_parts = sb("max_parts", [P, MAX_PARTS, 32], BF16)
        max_rows = sb("max_rows", [P, MAX_PARTS, 32], BF16)
        u_sb = sb("u", [P, 2, T])
        ring = [ctx.enter_context(nc.psum_tensor(f"{name}_ring{k}", [P, 2 * BANK], F32)) for k in range(3)]
        u_ps = ctx.enter_context(nc.psum_tensor(f"{name}_u_ps", [P, 2 * BANK], F32))

        N = QUAD * TILES
        LEAD = N + 6
        HALVES = ((0, 375), (375, T))
        loaded = [sem(f"loaded{k}") for k in range(AHEAD)]
        init_done = sem("init_done")
        logit_ready = sem("logit_ready")
        max_ready = sem("max_ready")
        part_done = sem("part_done")
        turned = sem("turned")
        rows_loaded = sem("rows_loaded")
        key_ready = sem("key_ready")
        exp_done = sem("exp_done")
        summed = sem("summed")
        u_copied = sem("u_copied")
        stored = [sem(f"stored{k}") for k in range(2)]

        def put_unit(sp, k, u):
            for parts, src, dst in ((Q_PARTS, q_parts, q_sb), (K_PARTS, k_parts, k_sb)):
                for slot, part in enumerate(parts):
                    sp.dma_start(dst[slot * HD:(slot + 1) * HD, k, :, 0:T],
                                 src[bass.ds(u, 1), part].rearrange("o (h r) t -> r (o h) t", r=HD)
                                 ).then_inc(loaded[k], 16)
            sp.dma_start(v_sb[:, k, 0:TILES - 1], v_aug[bass.ds(u, 1), 0:(TILES - 1) * P].rearrange("o (c p) n -> p (o c) n", p=P)
                         ).then_inc(loaded[k], 16)
            sp.dma_start(v_sb[0:K_SIZE[-1], k, TILES - 1], v_aug[bass.ds(u, 1), (TILES - 1) * P:T].rearrange("o p n -> (o p) n")
                         ).then_inc(loaded[k], 16)
        LOADS = 16 * (2 * len(Q_PARTS) + 2)

        def put_sums(sp, k, u):
            for h in range(QUAD):
                for row, out in ((HROWS * h, o_out), (HROWS * h + HD, sum_out)):
                    sp.dma_start(out[bass.ds(u, 1), h * HD:(h + 1) * HD].rearrange("o r t -> (o r) t"),
                                 u_sb[row:row + HD, k]).then_inc(stored[k], 16)
        STORES = 16 * 2 * QUAD

        def put_rows(sp, k):
            for block32 in range(4):
                for part in range(MAX_PARTS):
                    sp.dma_start(q_sb[STACK + part:STACK + part + 1, k].rearrange("p h (t x) -> p (h t) x", t=TILES)
                                 [:, :, 32 * block32:32 * block32 + 32],
                                 max_rows[32 * block32:32 * block32 + N, part]).then_inc(rows_loaded, 16)
        ROW_LOADS = 16 * 4 * MAX_PARTS

        block = ctx.enter_context(nc.Block())
        trips = units // AHEAD

        def trip_kinds(eng, unit):
            for k in range(AHEAD):
                unit(0, k, True, trips == 1)
            if trips > 2:
                with eng.Fori(1, trips - 1) as i:
                    for k in range(AHEAD):
                        unit(i, k, False, False)
            if trips > 1:
                for k in range(AHEAD):
                    unit(trips - 1, k, False, True)

        @block.sync
        def _(sp):
            sp.wait_ge(init_done, 1)
            for k in range(AHEAD - 1):
                put_unit(sp, k, k)
            sp.wait_ge(turned, 1)
            put_rows(sp, 0)

            def unit(i, k, first, last):
                u = AHEAD * i + k
                before = not (first and k == 0)
                if before:
                    sp.wait_ge(summed, 2 * TILES * u)
                if not last or k == 0:
                    put_unit(sp, (k + AHEAD - 1) % AHEAD, u + AHEAD - 1)
                if before:
                    sp.wait_ge(u_copied, u)
                    put_sums(sp, (k + 1) % 2, u - 1)
                if not (last and k == AHEAD - 1):
                    sp.wait_ge(turned, u + 2)
                    put_rows(sp, (k + 1) % AHEAD)
            trip_kinds(sp, unit)
            sp.wait_ge(u_copied, units)
            put_sums(sp, (units - 1) % 2, units - 1)
            for k in range(2):
                sp.wait_ge(stored[k], STORES * (units // 2))

        def max_job(k, n, last):
            ahead_units, tile = divmod(n + LEAD, N)
            if last and k + ahead_units >= AHEAD:
                return None
            return k + ahead_units, tile

        def logits(pe, k, n, where):
            h, t = divmod(n, TILES)
            for lo, hi in COLS_OF:
                mm = nc.tensor.matmul(where[0:K_SIZE[t], lo:hi], q_sb[0:STACK, k, h, P * t:P * t + K_SIZE[t]],
                                      k_sb[0:STACK, k, h, lo:hi], start=True, stop=True)
            mm.then_inc(logit_ready, 1)

        @block.tensor
        def _(pe):
            for a in range(LEAD):
                if a % N == 0:
                    pe.wait_ge(loaded[a // N], LOADS)
                if a >= 3:
                    pe.wait_ge(max_ready, a - 2)
                logits(pe, a // N, a % N, ring[a % 3])
            pe.wait_ge(max_ready, LEAD)

            def weigh(u, k, c, half):
                lo, hi = HALVES[half]
                for h in range(QUAD):
                    mm = nc.tensor.matmul(u_ps[HROWS * h:HROWS * (h + 1), BANK * half:BANK * half + hi - lo],
                                          v_sb[0:K_SIZE[c], k, c, HROWS * h:HROWS * (h + 1)],
                                          probT[0:K_SIZE[c], c % 3, h, lo:hi], start=(c == 0), stop=(c == TILES - 1))
                mm.then_inc(summed, 1)

            def unit(i, k, first, last):
                u = AHEAD * i + k
                g0 = N * u
                for n in range(N):
                    c, h = divmod(n, QUAD)
                    very_first = first and k == 0
                    job, before = max_job(k, n, last), max_job(k, n - 1, last)
                    if job:
                        if not (very_first and n < 2):
                            pe.wait_ge(exp_done, g0 + n - 1)
                        ahead, tile = job
                        if tile == 0:
                            pe.wait_ge(loaded[ahead % AHEAD], LOADS * (i + ahead // AHEAD + 1))
                        logits(pe, ahead % AHEAD, tile, ring[2 * n % 3])
                    if n == 0:
                        pe.wait_ge(rows_loaded, ROW_LOADS * (u + 1))
                    if before and not (very_first and n == 0):
                        pe.wait_ge(max_ready, g0 + n + LEAD)
                    elif not before:
                        pe.wait_ge(exp_done, g0 + n - 2)
                    for lo, hi in COLS_OF:
                        mm = nc.tensor.matmul(ring[(2 * n + 1) % 3][0:K_SIZE[c], lo:hi], k_sb[:, k, h, P * c:P * c + K_SIZE[c]],
                                              q_sb[:, k, h, lo:hi], start=True, stop=True)
                    mm.then_inc(key_ready, 1)
                    if n % 2 == 1 and not (very_first and c == 0):
                        if n % QUAD == 1:
                            pe.wait_ge(exp_done, g0 + QUAD * c)
                        if c == 1 and n % QUAD == 1 and not very_first:
                            pe.wait_ge(u_copied, u)
                        weigh(u, k if c else (k - 1) % AHEAD, (c - 1) % TILES, n % QUAD // 2)
            trip_kinds(pe, unit)
            pe.wait_ge(exp_done, N * units)
            for half in range(2):
                weigh(units - 1, AHEAD - 1, TILES - 1, half)

        @block.scalar
        def _(act):
            def unit(i, k, first, last):
                u = AHEAD * i + k
                for n in range(N):
                    c, h = divmod(n, QUAD)
                    act.wait_ge(key_ready, N * u + n + 1)
                    if h == 0 and not (first and k == 0 and c < 3):
                        act.wait_ge(summed, 2 * (TILES * u + c - 2))
                    nc.scalar.activation(probT[0:K_SIZE[c], c % 3, h], ring[(2 * n + 1) % 3][0:K_SIZE[c], 0:T], ACT.Exp
                                         ).then_inc(exp_done, 1)
            trip_kinds(act, unit)

        @block.vector
        def _(dve):
            nc.vector.memset(negmax[:], 0.0)
            nc.vector.memset(max_parts[:], 0.0)
            nc.vector.memset(k_sb[STACK:ROWS], 1.0).then_inc(init_done, 1)
            dve.wait_ge(init_done, 1)

            def maximum(u, n, where):
                t = n % TILES
                dve.wait_ge(logit_ready, N * u + n + 1)
                if n == 0:
                    dve.wait_ge(part_done, 2 * u)
                nc.vector.tensor_reduce(negmax[0:K_SIZE[t], n:n + 1], where[0:K_SIZE[t], 0:T], AX, ALU.max, negate=True
                                        ).then_inc(max_ready, 1)

            def turn_maxima(u):
                dve.wait_ge(max_ready, N * (u + 1))
                nc.vector.tensor_copy(max_parts[:, 0, 0:N], negmax[:]).then_inc(part_done, 1)
                dve.wait_ge(part_done, 2 * u + 1)
                nc.vector.tensor_tensor(max_parts[:, 1, 0:N], negmax[:], max_parts[:, 0, 0:N], ALU.subtract
                                        ).then_inc(part_done, 1)
                dve.wait_ge(part_done, 2 * u + 2)
                dve.wait_ge(rows_loaded, ROW_LOADS * u)
                nc.vector.transpose(max_rows[:].rearrange("p a b -> p (a b)"), max_parts[:].rearrange("p a b -> p (a b)")
                                    ).then_inc(turned, 1)

            def copy_sums(i, k, first):
                u = AHEAD * i + k
                dve.wait_ge(summed, 2 * TILES * (u + 1))
                if not (first and k < 2):
                    dve.wait_ge(stored[k % 2], STORES * ((AHEAD // 2) * i + k // 2))
                nc.vector.tensor_copy(u_sb[:, k % 2, 0:HALVES[0][1]], u_ps[:, 0:HALVES[0][1]])
                nc.vector.tensor_copy(u_sb[:, k % 2, HALVES[1][0]:T], u_ps[:, BANK:BANK + T - HALVES[1][0]]
                                      ).then_inc(u_copied, 1)

            for a in range(LEAD):
                maximum(a // N, a % N, ring[a % 3])
                if a == N - 1:
                    turn_maxima(0)

            def unit(i, k, first, last):
                u = AHEAD * i + k
                for n in range(N):
                    job = max_job(k, n, last)
                    if job:
                        ahead, tile = job
                        maximum(AHEAD * i + ahead, tile, ring[2 * n % 3])
                        if tile == N - 1:
                            turn_maxima(AHEAD * i + ahead)
                    if n == 4 and not (first and k == 0):
                        if k:
                            copy_sums(i, k - 1, first)
                        else:
                            copy_sums(i - 1, AHEAD - 1, False)
            trip_kinds(dve, unit)
            copy_sums(trips - 1, AHEAD - 1, False)


def stage_topk_attention(nc, name, q_parts, k_parts, v_aug, o_out, sum_out, ident, units):
    with ExitStack() as ctx:
        sems = []
        ctx.callback(end_stage, nc, sems)
        sb = lambda n, shape, dt=F32: ctx.enter_context(nc.sbuf_tensor(f"{name}_{n}", shape, dt))

        def sem(n):
            sems.append(nc.alloc_semaphore(f"{name}_{n}"))
            return sems[-1]

        q_sb = sb("q", [STACK, 2, QUAD, T], BF16)
        k_sb = sb("k", [STACK, 2, QUAD, T], BF16)
        v_sb = sb("v", [P, 2, TILES, P])
        prob = sb("prob", [P, 2, T])
        probT = sb("probT", [P, 2, QUAD, TILES, P])
        negmax = sb("negmax", [P, 2])
        u_sb = sb("u", [P, 2, T])
        id_sb = sb("id", [P, P])
        best = sb("best", [P, 2, 2, 8])
        left = sb("left", [P, 2, T])
        expo = sb("expo", [P, 2, T])
        expo_left = sb("expo_left", [P, 2, T])
        pause = sb("pause", [P, 2, 3])
        s_ps = [ctx.enter_context(nc.psum_tensor(f"{name}_s_ps{k}", [P, 2 * BANK], F32)) for k in range(2)]
        t_ps = [ctx.enter_context(nc.psum_tensor(f"{name}_t_ps{k}", [P, BANK], F32)) for k in range(2)]
        u_ps = ctx.enter_context(nc.psum_tensor(f"{name}_u_ps", [P, BANK], F32))

        const_loaded = sem("const_loaded")
        qkv_loaded = [sem(f"qkv_loaded{k}") for k in range(2)]
        s_ready = sem("s_ready")
        max_ready = sem("max_ready")
        exp_done = sem("exp_done")
        t_ready = [sem(f"t_ready{k}") for k in range(2)]
        t_copied = [sem(f"t_copied{k}") for k in range(2)]
        u_ready = sem("u_ready")
        u_copied = sem("u_copied")
        o_stored = [sem(f"o_stored{k}") for k in range(2)]
        top_step = sem("top_step")
        left_done = sem("left_done")
        exp_left_done = sem("exp_left_done")
        sel_done = sem("sel_done")

        TPU = QUAD * TILES

        def put_stack(sp, k, u):
            for parts, src, dst in ((Q_PARTS, q_parts, q_sb), (K_PARTS, k_parts, k_sb)):
                for slot, part in enumerate(parts):
                    sp.dma_start(dst[slot * HD:(slot + 1) * HD, k],
                                 src[bass.ds(u, 1), part].rearrange("o (h r) t -> r (o h) t", r=HD)
                                 ).then_inc(qkv_loaded[k], 16)
            sp.dma_start(v_sb[:, k, 0:TILES - 1], v_aug[bass.ds(u, 1), 0:(TILES - 1) * P].rearrange("o (c p) n -> p (o c) n", p=P)
                         ).then_inc(qkv_loaded[k], 16)
            sp.dma_start(v_sb[0:K_SIZE[-1], k, TILES - 1], v_aug[bass.ds(u, 1), (TILES - 1) * P:T].rearrange("o p n -> (o p) n")
                         ).then_inc(qkv_loaded[k], 16)
        LOADS = 16 * (2 * len(Q_PARTS) + 2)

        def put_out(sp, k, u):
            for h in range(QUAD):
                for row, out in ((2 * HD * h, o_out), (2 * HD * h + HD, sum_out)):
                    sp.dma_start(out[bass.ds(u, 1), h * HD:(h + 1) * HD].rearrange("o r t -> (o r) t"),
                                 u_sb[row:row + HD, k]).then_inc(o_stored[k], 16)
        STORES = 16 * 2 * QUAD

        start_from_one(nc, (o_stored,))
        block = ctx.enter_context(nc.Block())
        pairs = units // 2

        @block.sync
        def _(sp):
            sp.dma_start(id_sb[:], ident).then_inc(const_loaded, 16)
            for k in range(2):
                put_stack(sp, k, k)
            with sp.Fori(0, pairs - 1) as i:
                for k in range(2):
                    sp.wait_ge(u_ready, TILES * (2 * i + k + 1))
                    put_stack(sp, k, 2 * i + 2 + k)
                    sp.wait_ge(u_copied, TILES * (2 * i + k + 1))
                    put_out(sp, k, 2 * i + k)
            for k in range(2):
                sp.wait_ge(u_copied, TILES * (units - 2 + k + 1))
                put_out(sp, k, units - 2 + k)
            for k in range(2):
                sp.wait_ge(o_stored[k], STORES * pairs + 1)

        @block.tensor
        def _(pe):
            pe.wait_ge(const_loaded, 16)
            with pe.Fori(0, pairs) as i:
                N = 2 * TPU
                base, ubase = i * N, i * (2 * TILES)

                def logits(n):
                    k, (t, h) = n // TPU, divmod(n % TPU, QUAD)
                    if n % TPU == 0:
                        pe.wait_ge(qkv_loaded[k], LOADS * i + LOADS)
                    if n >= 2:
                        pe.wait_ge(exp_done, base + n - 1)
                    for a, b in ((0, BANK), (BANK, T)):
                        mm = nc.tensor.matmul(s_ps[n % 2][:, a:b], q_sb[:, k, h, Q_START[t]:Q_START[t] + P],
                                              k_sb[:, k, h, a:b], start=True, stop=True)
                    mm.then_inc(s_ready, 1)

                def turn(n):
                    pe.wait_ge(sel_done, base + n + 1)
                    for half in range(2):
                        if n >= 1:
                            pe.wait_ge(t_copied[half], base + n)
                        for c in range(3 * half, 3 * half + 3):
                            mm = nc.tensor.transpose(t_ps[half][0:K_SIZE[c], (c - 3 * half) * P:(c - 3 * half + 1) * P],
                                                     prob[:, n % 2, c * P:c * P + K_SIZE[c]], id_sb[:])
                        mm.then_inc(t_ready[half], 1)

                def weigh(m):
                    k, t = divmod(m, TILES)
                    for half in range(2):
                        pe.wait_ge(t_copied[half], base + QUAD * (m + 1))
                    if m >= 4:
                        pe.wait_ge(u_copied, ubase + m - 3)
                    for c in range(TILES):
                        for h in range(QUAD):
                            mm = nc.tensor.matmul(u_ps[32 * h:32 * h + 32, (m % 4) * P:(m % 4 + 1) * P],
                                                  v_sb[0:K_SIZE[c], k, c, 32 * h:32 * h + 32],
                                                  probT[0:K_SIZE[c], m % 2, h, c], start=(c == 0), stop=(c == TILES - 1))
                    mm.then_inc(u_ready, 1)

                logits(0)
                logits(1)
                for n in range(N):
                    if n + 2 < N:
                        logits(n + 2)
                    turn(n)
                    if n % QUAD == 1 and n > QUAD:
                        weigh(n // QUAD - 1)
                weigh(2 * TILES - 1)
                pe.wait_ge(exp_done, base + N)
                for half in range(2):
                    pe.wait_ge(t_copied[half], base + N)
                pe.wait_ge(u_copied, ubase + 2 * TILES)

        @block.gpsimd
        def _(pool):
            with pool.Fori(0, pairs) as i:
                N = 2 * TPU
                base = i * N
                for n in range(N):
                    pool.wait_ge(exp_left_done, base + n + 1)
                    pool.wait_ge(exp_done, base + n + 1)
                    if n >= 2:
                        for half in range(2):
                            pool.wait_ge(t_ready[half], base + n - 1)
                    nc.gpsimd.tensor_tensor(prob[:, n % 2], expo[:, n % 2], expo_left[:, n % 2], ALU.subtract).then_inc(sel_done, 1)

        @block.scalar
        def _(act):
            with act.Fori(0, pairs) as i:
                N = 2 * TPU
                base, ubase = i * N, i * (2 * TILES)

                def copy_halves(n):
                    t, h = divmod(n, QUAD)
                    act.wait_ge(t_ready[0], base + n + 1)
                    if t >= 2:
                        act.wait_ge(u_ready, ubase + t - 1)
                    nc.scalar.activation(probT[:, t % 2, h, 0:3].rearrange("p c q -> p (c q)"), t_ps[0][:, 0:HALF],
                                         ACT.Copy).then_inc(t_copied[0], 1)
                    act.wait_ge(t_ready[1], base + n + 1)
                    nc.scalar.activation(probT[:, t % 2, h, 3:5].rearrange("p c q -> p (c q)"), t_ps[1][:, 0:2 * P], ACT.Copy)
                    nc.scalar.activation(probT[0:K_SIZE[5], t % 2, h, 5], t_ps[1][0:K_SIZE[5], 2 * P:3 * P], ACT.Copy
                                         ).then_inc(t_copied[1], 1)

                def exp_left(n):
                    act.wait_ge(left_done, base + n + 1)
                    if n >= 2:
                        act.wait_ge(sel_done, base + n - 1)
                    nc.scalar.activation(expo_left[:, n % 2, :], left[:, n % 2, :], ACT.Exp, bias=negmax[:, n % 2:n % 2 + 1]
                                         ).then_inc(exp_left_done, 1)

                for n in range(N):
                    act.wait_ge(s_ready, base + n + 1)
                    act.wait_ge(max_ready, base + n + 1)
                    if n >= 2:
                        act.wait_ge(sel_done, base + n - 1)
                    nc.scalar.activation(expo[:, n % 2, :], s_ps[n % 2][:, 0:T], ACT.Exp, bias=negmax[:, n % 2:n % 2 + 1]
                                         ).then_inc(exp_done, 1)
                    exp_left(n)
                    if n >= 1:
                        copy_halves(n - 1)
                copy_halves(N - 1)

        @block.vector
        def _(dve):
            with dve.Fori(0, pairs) as i:
                N = 2 * TPU
                base, ubase = i * N, i * (2 * TILES)

                def copy_sums(m):
                    k, t = divmod(m, TILES)
                    dve.wait_ge(u_ready, ubase + m + 1)
                    if t == 0:
                        dve.wait_ge(o_stored[k], STORES * i + 1)
                    nc.vector.tensor_copy(u_sb[:, k, Q_START[t]:Q_START[t] + P], u_ps[:, (m % 4) * P:(m % 4 + 1) * P]
                                          ).then_inc(u_copied, 1)

                for n in range(N):
                    dve.wait_ge(s_ready, base + n + 1)
                    top = i * (3 * N) + 3 * n
                    if n >= 2:
                        dve.wait_ge(exp_left_done, base + n - 1)
                    nc.vector.memset(pause[:, n % 2, 0:1], 0.0)
                    nc.vector.max(best[:, n % 2, 0], s_ps[n % 2][:, 0:T]).then_inc(top_step, 1)
                    dve.wait_ge(top_step, top + 1)
                    nc.vector.tensor_scalar(negmax[:, n % 2:n % 2 + 1], best[:, n % 2, 0, 0:1], -1.0, None, ALU.mult
                                            ).then_inc(top_step, 1)
                    nc.vector.match_replace(left[:, n % 2], best[:, n % 2, 0], s_ps[n % 2][:, 0:T], TAKEN
                                            ).then_inc(max_ready, 1)
                    if n % QUAD == 3 and n > QUAD:
                        copy_sums(n // QUAD - 1)
                    dve.wait_ge(max_ready, base + n + 1)
                    nc.vector.memset(pause[:, n % 2, 1:2], 0.0)
                    nc.vector.max(best[:, n % 2, 1], left[:, n % 2]).then_inc(top_step, 1)
                    dve.wait_ge(top_step, top + 3)
                    nc.vector.memset(pause[:, n % 2, 2:3], 0.0)
                    nc.vector.match_replace(left[:, n % 2], best[:, n % 2, 1], left[:, n % 2], TAKEN
                                            ).then_inc(left_done, 1)
                copy_sums(2 * TILES - 1)


def stage_lstm(nc, wh, xw, mem, trips=T // S):
    with ExitStack() as ctx:
        sems = []
        ctx.callback(end_stage, nc, sems)
        sb = lambda name, shape, dt=F32: ctx.enter_context(nc.sbuf_tensor(name, shape, dt))

        def sem(name):
            sems.append(nc.alloc_semaphore(name))
            return sems[-1]

        w_raw = sb("lstm_w_raw", [P, 2, 2, 1024])
        w_hi = sb("lstm_w_hi", [P, 2, E, 2, 1024], F16)
        w_lo = sb("lstm_w_lo", [P, 2, E, 2, 1024], F16)
        w_peak = sb("lstm_w_peak", [P, 2 * E])
        w_max = sb("lstm_w_max", [P, 1])
        w_allmax = sb("lstm_w_allmax", [P, 1])
        w_scale = sb("lstm_w_scale", [P, 1])
        w_inv = sb("lstm_w_inv", [P, 1])
        xw_sb = sb("lstm_xw", [P, 2, E, S, GC])
        hist = sb("lstm_hist", [P, 2, E * 2, S, B])
        h_parts = sb("lstm_h_parts", [P, 2, E, 2, 2, B], F16)
        part_sum = sb("lstm_part_sum", [P, 2, E * GC])
        z_sb = sb("lstm_z", [P, 2, E, GC])
        gate_sb = sb("lstm_gates", [P, 2, E, GC])
        c_sb = sb("lstm_c", [P, 2, E * 8])
        fc_sb = sb("lstm_fc", [P, 2, E * 8])
        ig_sb = sb("lstm_ig", [P, 2, E * 8])
        tc_sb = sb("lstm_tc", [P, 2, E * 8])
        z_ps = [ctx.enter_context(nc.psum_tensor(f"lstm_z_ps{d}", [P, E, 8, 2, B], F32)) for d in range(2)]

        w_loaded = [sem(f"lstm_w_loaded{k}") for k in range(2)]
        w_read = sem("lstm_w_read")
        peak_done = sem("lstm_peak_done")
        allmax_done = sem("lstm_allmax_done")
        scale_step = sem("lstm_scale_step")
        hi_done = sem("lstm_hi_done")
        split_done = sem("lstm_split_done")
        D = 2
        xw_loaded = [[sem(f"lstm_xw_loaded{d}_{k}") for k in range(len(PIECES))] for d in range(D)]
        hist_stored = [[sem(f"lstm_hist_stored{d}_{k}") for k in range(len(PIECES))] for d in range(D)]
        z_ready = [sem(f"lstm_z_ready{d}") for d in range(D)]
        sum_done = [sem(f"lstm_sum_done{d}") for d in range(D)]
        z_done = [sem(f"lstm_z_done{d}") for d in range(D)]
        sig_done = [sem(f"lstm_sig_done{d}") for d in range(D)]
        tanh_done = [sem(f"lstm_tanh_done{d}") for d in range(D)]
        fc_done = [sem(f"lstm_fc_done{d}") for d in range(D)]
        ig_done = [sem(f"lstm_ig_done{d}") for d in range(D)]
        c_done = [sem(f"lstm_c_done{d}") for d in range(D)]
        tc_done = [sem(f"lstm_tc_done{d}") for d in range(D)]
        h_done = [sem(f"lstm_h_done{d}") for d in range(D)]
        h_hi_done = [sem(f"lstm_h_hi_done{d}") for d in range(D)]
        h_lo_done = [sem(f"lstm_h_lo_done{d}") for d in range(D)]
        zero_done = sem("lstm_zero_done")


        def slot(d, j):
            return j if d == 0 else S - 1 - j

        def slots(d, k):
            a, b = PIECES[k]
            return (a, b) if d == 0 else (S - b, S - a)

        def xw_move(eng, d, k, i):
            a, b = slots(d, k)
            start = i * S + a if d == 0 else i * -S + (T - S + a)
            return eng.dma_start(xw_sb[:, d, :, a:b, :],
                                 xw[d].rearrange("e p t g -> p e t g")[:, :, bass.ds(start, b - a), :])

        def hist_move(eng, d, k, i):
            a, b = slots(d, k)
            start = i * S + a if d == 0 else i * -S + (T - S + a)
            return eng.dma_start(mem[d].rearrange("e c p t b -> p (e c) t b")[:, :, bass.ds(start, b - a), :],
                                 hist[:, d, :, a:b, :])

        start_from_one(nc, (hist_stored,))
        block = ctx.enter_context(nc.Block())

        @block.sync
        def _(sp):
            for n in range(2 * 2 * E):
                d, e = (n // E) % 2, n % E
                if 2 <= n < 2 * E + 2:
                    sp.wait_ge(w_read, n - 1)
                elif n >= 2:
                    sp.wait_ge(split_done, n - 2 * E - 1)
                sp.dma_start(w_raw[:, n % 2], wh[d][e].rearrange("(k p) n -> p k n", p=P)).then_inc(w_loaded[n % 2], 16)
            for d in range(D):
                for k in range(len(PIECES)):
                    xw_move(sp, d, k, 0).then_inc(xw_loaded[d][k], 16)
            with sp.Fori(0, trips - 1) as i:
                for k, (_, last) in enumerate(PIECES):
                    for d in range(D):
                        sp.wait_ge(sum_done[d], i * S + last)
                        xw_move(sp, d, k, i + 1).then_inc(xw_loaded[d][k], 16)
                        sp.wait_ge(h_lo_done[d], i * S + last + 1)
                        hist_move(sp, d, k, i).then_inc(hist_stored[d][k], 16)
            for k, (_, last) in enumerate(PIECES):
                for d in range(D):
                    sp.wait_ge(h_lo_done[d], (trips - 1) * S + last + 1)
                    hist_move(sp, d, k, trips - 1).then_inc(hist_stored[d][k], 16)
            for k in range(len(PIECES)):
                for d in range(D):
                    sp.wait_ge(hist_stored[d][k], 16 * trips + 1)

        @block.gpsimd
        def _(pool):
            pool.wait_ge(peak_done, 1)
            nc.gpsimd.partition_all_reduce(w_allmax[:], w_max[:], P, bass.bass_isa.ReduceOp.max).then_inc(allmax_done, 1)

        @block.tensor
        def _(pe):
            pe.wait_ge(split_done, 2 * E)
            with pe.Fori(0, trips) as i:
                for j in range(S):
                    for d in range(D):
                        pe.wait_ge(h_lo_done[d], i * S + j + 1)
                        for e in range(E):
                            for m in range(8):
                                for n, (k, w) in enumerate(((0, w_hi), (0, w_lo), (1, w_hi), (1, w_lo))):
                                    mm = nc.tensor.matmul(
                                        z_ps[d][:, e, m].rearrange("p q b -> p (q b)"), w[:, d, e, k, COLS[m] * P:(COLS[m] + 1) * P],
                                        h_parts[:, d, e, k].rearrange("p q b -> p (q b)"), start=(n == 0), stop=(n == 3))
                        mm.then_inc(z_ready[d], 1)

        @block.scalar
        def _(act):
            for n in range(2 * E):
                d, e = n // E, n % E
                act.wait_ge(scale_step, 4)
                act.wait_ge(w_loaded[n % 2], 16 * ((2 * E + n) // 2 + 1))
                nc.scalar.activation(w_hi[:, d, e], w_raw[:, n % 2], ACT.Copy, scale=w_inv[:, 0:1]).then_inc(hi_done, 1)
            with act.Fori(0, trips) as i:
                for j in range(S):
                    for d in range(D):
                        step = i * S + j + 1
                        act.wait_ge(z_done[d], step)
                        nc.scalar.activation(gate_sb[:, d, :, 0:24], z_sb[:, d, :, 0:24], ACT.Sigmoid).then_inc(sig_done[d], 1)
                        nc.scalar.activation(gate_sb[:, d, :, 24:32], z_sb[:, d, :, 24:32], ACT.Tanh).then_inc(tanh_done[d], 1)
                        act.wait_ge(c_done[d], step)
                        nc.scalar.activation(tc_sb[:, d], c_sb[:, d], ACT.Tanh).then_inc(tc_done[d], 1)

        @block.vector
        def _(dve):
            for n in range(2 * E):
                dve.wait_ge(w_loaded[n % 2], 16 * (n // 2 + 1))
                nc.vector.tensor_reduce(w_peak[:, n:n + 1], w_raw[:, n % 2].rearrange("p k n -> p (k n)"), AX, ALU.max,
                                        apply_absolute_value=True).then_inc(w_read, 1)
            dve.wait_ge(w_read, 2 * E)
            nc.vector.tensor_reduce(w_max[:], w_peak[:], AX, ALU.max).then_inc(peak_done, 1)
            dve.wait_ge(allmax_done, 1)
            nc.vector.tensor_scalar(w_scale[:], w_allmax[:], 1e-30, None, ALU.max).then_inc(scale_step, 1)
            dve.wait_ge(scale_step, 1)
            nc.vector.tensor_scalar(w_scale[:].bitcast(mybir.dt.uint32), w_scale[:].bitcast(mybir.dt.uint32), 0x7f800000, None, ALU.bitwise_and).then_inc(scale_step, 1)
            dve.wait_ge(scale_step, 2)
            nc.vector.reciprocal(w_inv[:], w_scale[:]).then_inc(scale_step, 1)
            nc.vector.memset(c_sb[:], 0.0).then_inc(scale_step, 1)
            dve.wait_ge(scale_step, 4)
            for n in range(2 * E):
                d, e = n // E, n % E
                dve.wait_ge(hi_done, n + 1)
                nc.vector.scalar_tensor_tensor(w_lo[:, d, e], w_raw[:, n % 2], w_inv[:, 0:1], w_hi[:, d, e], ALU.mult, ALU.subtract).then_inc(split_done, 1)
            for d in range(D):
                nc.vector.memset(h_parts[:, d], 0.0).then_inc(h_lo_done[d], 1)
            with dve.Fori(0, trips) as i:
                for j in range(S):
                    k = 0 if j < PIECES[0][1] else 1
                    for d in range(D):
                        step = i * S + j + 1
                        s = slot(d, j)
                        hi = h_parts[:, d, :, :, 0].rearrange("p e c b -> p (e c) b")
                        lo = h_parts[:, d, :, :, 1].rearrange("p e c b -> p (e c) b")
                        o_gate = gate_sb[:, d, :, 16:24].rearrange("p e (c b) -> p e c b", c=2)
                        if j == PIECES[k][0]:
                            dve.wait_ge(xw_loaded[d][k], i * 16 + 16)
                            dve.wait_ge(hist_stored[d][k], i * 16 + 1)
                        dve.wait_ge(z_ready[d], step)
                        nc.vector.scalar_tensor_tensor(
                            part_sum[:, d].rearrange("p (e g b) -> p e g b", e=E, g=8), z_ps[d][:, :, :, 0], w_scale[:, 0:1],
                            xw_sb[:, d, :, s].rearrange("p e (g b) -> p e g b", g=8), ALU.mult, ALU.add).then_inc(sum_done[d], 1)
                        dve.wait_ge(sum_done[d], step)
                        nc.vector.scalar_tensor_tensor(
                            z_sb[:, d].rearrange("p e (g b) -> p (e g) b", g=8), z_ps[d][:, :, :, 1].rearrange("p e g b -> p (e g) b"),
                            w_scale[:, 0:1], part_sum[:, d].rearrange("p (n b) -> p n b", b=B), ALU.mult, ALU.add).then_inc(z_done[d], 1)
                        dve.wait_ge(sig_done[d], step)
                        nc.vector.tensor_tensor(fc_sb[:, d].rearrange("p (e x) -> p e x", e=E), gate_sb[:, d, :, 8:16],
                                                c_sb[:, d].rearrange("p (e x) -> p e x", e=E), ALU.mult).then_inc(fc_done[d], 1)
                        dve.wait_ge(tanh_done[d], step)
                        nc.vector.tensor_tensor(ig_sb[:, d].rearrange("p (e x) -> p e x", e=E), gate_sb[:, d, :, 0:8],
                                                gate_sb[:, d, :, 24:32], ALU.mult).then_inc(ig_done[d], 1)
                        dve.wait_ge(ig_done[d], step)
                        nc.vector.tensor_tensor(c_sb[:, d], fc_sb[:, d], ig_sb[:, d], ALU.add).then_inc(c_done[d], 1)
                        dve.wait_ge(tc_done[d], step)
                        h_now = hist[:, d, :, s]
                        tc = tc_sb[:, d].rearrange("p (e c b) -> p e c b", e=E, c=2)
                        nc.vector.tensor_tensor(h_parts[:, d, :, :, 0], o_gate, tc, ALU.mult).then_inc(h_hi_done[d], 1)
                        nc.vector.tensor_tensor(h_now.rearrange("p (e c) b -> p e c b", e=E), o_gate, tc, ALU.mult).then_inc(h_done[d], 1)
                        dve.wait_ge(h_done[d], step)
                        nc.vector.tensor_tensor(lo, h_now, hi, ALU.subtract).then_inc(h_lo_done[d], 1)


def audio_tower(nc, a, out):
    def scratch(name, shape, dt=F32):
        return nc.dram_tensor(f"scratch_{name}", list(shape), dt, kind="Internal").ap()

    def attention(name, src, w, cols, v_bias, experts, heads, scale, top_k=False):
        units = experts * B * heads // QUAD
        q = scratch(f"{name}_q", (units, 3, QUAD * HD, T), BF16)
        k = scratch(f"{name}_k", (units, 3, QUAD * HD, T), BF16)
        v = scratch(f"{name}_v", (units, T, P))
        o = scratch(f"{name}_o", (units, QUAD * HD, T))
        sums = scratch(f"{name}_sums", (units, QUAD * HD, T))
        stage_qkv(nc, f"{name}p", src, w, cols, v_bias, q, k, v, experts, heads, scale)
        if top_k:
            stage_topk_attention(nc, name, q, k, v, o, sums, a["ident"], units)
        else:
            stage_softmax_attention(nc, name, q, k, v, o, sums, units)
        return o, sums

    h0, h1, h2, h3 = (scratch(f"h{n}", (P, B, T)) for n in range(4))
    n0, n1, n2, n3 = (scratch(f"n{n}", (P, B, T)) for n in range(4))
    as_source = lambda n: n.rearrange("(e k p) b t -> e k p b t", e=1, k=1)
    by_batch = lambda pair: [o.rearrange("(b g) r t -> b (g r) t", b=B) for o in pair]
    by_expert = lambda pair: [o.rearrange("(e b g) r t -> e b (g r) t", e=E, b=B) for o in pair]

    stage_tok(nc, a["x"], a["w_tok"], a["b_tok"], h0)
    stage_norm(nc, "norm0", h0, n0)
    o0 = attention("att0", as_source(n0), a["w_qkv0"], a["cols_qkv0"], a["bv0"], 1, 8, 1.0 / 4.0)
    stage_norm(nc, "norm1", h0, n1, *by_batch(o0), a["wo0"], a["cols_o0"], h1)

    enc = scratch("enc", (E, 2, P, B, T))
    stage_encode(nc, n1, a["enc_w1"], a["enc_w2"], a["cols_enc"], enc)
    oe = attention("atte", enc, a["attn_in_w"], a["cols_qkve"], a["bve"], E, 16, 1.0 / 4.0)
    xw = scratch("xw", (2, E, P, T, GC))
    mem = scratch("mem", (2, E, 2, P, T, B))
    stage_lstm_inputs(nc, *by_expert(oe), a["attn_out_w"], (a["wi_f"], a["wi_b"]),
                      a["cols_xw"], xw)
    stage_lstm(nc, (a["wh_f"], a["wh_b"]), xw, mem)
    stage_decode(nc, mem, n1, h1, a["sig_w1"], a["sig_w2"], a["tan_w1"], a["tan_w2"], a["dec_w1"], a["dec_w2"],
                 a["router_w"], a["cols_dec"], h2)

    stage_norm(nc, "norm2", h2, n2)
    stage_retention(nc, n2, h2, a["w_q1"], a["w_k1"], a["w_v1"], a["decay"], h3)
    stage_norm(nc, "norm3", h3, n3, cols=a["cols_o1"], conv=True)
    o1 = attention("att1", as_source(n3), a["w_qkv1"], a["cols_qkv1"], a["bv1"], 1, 8, float(P) ** -0.5, top_k=True)
    stage_norm(nc, "norm4", h3, None, *by_batch(o1), a["wo1"], a["cols_o1"], out)


def kernel(**inputs):
    import numpy as np
    import concourse.bacc as bacc
    from concourse.bass_utils import run_bass_kernel_spmd as run

    g = {k: np.asarray(v) for k, v in inputs.items()}
    ffn = lambda n: g["L0_ffn_" + n]
    columns = lambda v: v.reshape(-1, P).T
    ecolumns = lambda v: v.reshape(E, -1, P).transpose(0, 2, 1)
    zero = np.zeros((P, 1), np.float32)

    off = P * (TILES - 1)
    distance = np.abs(np.arange(P)[:, None] - np.arange(off + T)[None] + off)
    decay = (0.96875 ** distance).astype(np.float32)

    taps = ("L0_tok_W_z", "L0_tok_W_f", "L0_tok_W_o")
    arrays = {
        "x": g["x"].transpose(2, 0, 1),
        "w_tok": np.stack([g[n].transpose(1, 2, 0) for n in taps], axis=1),
        "b_tok": np.stack([g["L0_tok_b_z"], g["L0_tok_b_f"], g["L0_tok_b_o"]], axis=1),
        "w_qkv0": np.concatenate([g["L0_attn_Wqk"], g["L0_attn_Wv"]], axis=1)[None],
        "cols_qkv0": columns(g["L0_attn_bqk"])[None],
        "bv0": g["L0_attn_bv"][None],
        "wo0": g["L0_attn_Wo"],
        "cols_o0": np.concatenate([columns(g["L0_attn_bo"])] + [zero] * 4, axis=1),
        "enc_w1": ffn("enc_w1"), "enc_w2": ffn("enc_w2"),
        "cols_enc": np.concatenate([ecolumns(ffn(n)) for n in ("enc_b1", "enc_b2", "enc_g", "enc_beta")], axis=2),
        "attn_in_w": ffn("attn_in_w"),
        "cols_qkve": ecolumns(ffn("attn_in_b")[:, :2 * D_EXPERT]),
        "bve": ffn("attn_in_b")[:, 2 * D_EXPERT:],
        "attn_out_w": ffn("attn_out_w"),
        "wi_f": ffn("lstm_wi_f"), "wi_b": ffn("lstm_wi_b"), "wh_f": ffn("lstm_wh_f"), "wh_b": ffn("lstm_wh_b"),
        "cols_xw": np.concatenate([ecolumns(ffn(n)) for n in ("attn_out_b", "lstm_b_f", "lstm_b_b")], axis=2),
        "sig_w1": ffn("sig_w1"), "sig_w2": ffn("sig_w2"), "tan_w1": ffn("tan_w1"), "tan_w2": ffn("tan_w2"),
        "dec_w1": ffn("dec_w1"), "dec_w2": ffn("dec_w2"),
        "router_w": ffn("router_w"),
        "cols_dec": np.concatenate(
            [ecolumns(ffn(n)) for n in ("sig_b1", "sig_b2", "tan_b1", "tan_b2", "dec_b1", "dec_b2", "dec_g", "dec_beta")]
            + [np.broadcast_to(ffn("router_b")[:, None, None], (E, P, 1))], axis=2),
        "w_q1": g["L1_attn_W_Q"], "w_k1": g["L1_attn_W_K"], "w_v1": g["L1_attn_W_V"],
        "decay": decay,
        "cols_o1": np.concatenate([columns(g["L1_ffn_wo_b"]), columns(g["L1_ffn_pos_b"]), g["L1_ffn_pos_w"][:, 0]], axis=1),
        "w_qkv1": g["L1_ffn_qkv_w"].T[None],
        "cols_qkv1": columns(g["L1_ffn_qkv_b"][:2 * P])[None],
        "bv1": g["L1_ffn_qkv_b"][None, 2 * P:],
        "wo1": g["L1_ffn_wo_w"].T,
        "ident": np.eye(P, dtype=np.float32),
    }
    nc = bacc.Bacc("TRN2", target_bir_lowering=False, num_devices=1)
    feed, a = {}, {}
    for name, array in arrays.items():
        feed[f"in_{name}"] = np.ascontiguousarray(array)
        a[name] = nc.dram_tensor(f"in_{name}", list(array.shape), mybir.dt.from_np(array.dtype), kind="ExternalInput").ap()
    out = nc.dram_tensor("out", [P, B, T], F32, kind="ExternalOutput").ap()
    audio_tower(nc, a, out)
    r = run(nc, [feed], core_ids=[0])
    return r.results[0]["out"].transpose(1, 2, 0)
```

```python
from contextlib import ExitStack

import concourse.bass as bass
from concourse import mybir

ALU = mybir.AluOpType
ACT = mybir.ActivationFunctionType
F32 = mybir.dt.float32
F16 = mybir.dt.float16
BF16 = mybir.dt.bfloat16
AX = mybir.AxisListType.X

P = 128
B, T, E = 4, 749, 4
D_EXPERT = 2 * P
BANK = 512
HD = 16
EPS = 1e-5
COLS_OF = ((0, BANK), (BANK, T))

QUAD = 4
TILES = -(-T // P)
Q_START = [min(P * t, T - P) for t in range(TILES)]
K_SIZE = [min(P, T - P * t) for t in range(TILES)]
HALF = 3 * P
Q_PARTS = (0, 0, 0, 1, 1, 2)
K_PARTS = (0, 1, 2, 0, 1, 0)
STACK = HD * len(Q_PARTS)
HROWS = 2 * HD
TP = TILES * P
MAX_PARTS = 2
AHEAD = 4
TAKEN = -2.0 ** 126

S = 7
GC = 32
COLS = (0, 1, 2, 3, 6, 7, 4, 5)
PIECES = ((0, 4), (4, 7))
CT = 107
CW = CT * B


def start_from_one(nc, sems):
    for s in sems:
        for each in s if isinstance(s, list) else (s,):
            for one in each if isinstance(each, list) else (each,):
                nc.gpsimd.sem_inc(one, 1)
    nc.all_engine_barrier()


def end_stage(nc, sems):
    nc.clear_and_free_semaphores(sems)
    nc.all_engine_barrier()


def stage_tok(nc, x, w_tok, b_tok, h_out):
    with ExitStack() as ctx:
        sems = []
        ctx.callback(end_stage, nc, sems)
        sb = lambda n, shape, dt=F32: ctx.enter_context(nc.sbuf_tensor(f"tok_{n}", shape, dt))

        def sem(n):
            sems.append(nc.alloc_semaphore(f"tok_{n}"))
            return sems[-1]

        x_sb = sb("x", [P, B, T + 1])
        w_sb = sb("w", [P, 3, 2, P])
        b_sb = sb("b", [P, 3])
        gate = sb("gate", [P, 2, 3, T])
        fz = sb("fz", [P, 2, T])
        inp = sb("inp", [P, 2, T])
        cell = sb("cell", [P, 2, T])
        h_sb = sb("h", [P, 2, T])
        g_ps = [ctx.enter_context(nc.psum_tensor(f"tok_g_ps{g}", [P, 2 * BANK], F32)) for g in range(3)]
        w_loaded = sem("w_loaded")
        x_loaded = [sem(f"x_loaded{b}") for b in range(B)]
        gate_mm = sem("gate_mm")
        gate_out = sem("gate_out")
        step = sem("step")
        stored = [sem(f"stored{k}") for k in range(2)]
        block = ctx.enter_context(nc.Block())

        @block.sync
        def _(sp):
            sp.dma_start(w_sb[:], w_tok).then_inc(w_loaded, 16)
            sp.dma_start(b_sb[:], b_tok).then_inc(w_loaded, 16)
            for b in range(B):
                sp.dma_start(x_sb[:, b], x[:, b]).then_inc(x_loaded[b], 16)
            for b in range(B):
                sp.wait_ge(step, 4 * b + 4)
                sp.dma_start(h_out[:, b], h_sb[:, b % 2]).then_inc(stored[b % 2], 16)
            for k in range(2):
                sp.wait_ge(stored[k], 16 * (B // 2))

        @block.tensor
        def _(pe):
            pe.wait_ge(w_loaded, 32)
            for b in range(B):
                pe.wait_ge(x_loaded[b], 16)
                for g in range(3):
                    if b:
                        pe.wait_ge(gate_out, 3 * (b - 1) + g + 1)
                    for lo, hi in COLS_OF:
                        for tap in range(2):
                            mm = nc.tensor.matmul(g_ps[g][:, lo:hi], w_sb[:, g, tap], x_sb[:, b, lo + tap:hi + tap],
                                                  start=(tap == 0), stop=(tap == 1))
                    mm.then_inc(gate_mm, 1)

        @block.scalar
        def _(act):
            for b in range(B):
                for g in range(3):
                    act.wait_ge(gate_mm, 3 * b + g + 1)
                    if b >= 2 and g == 0:
                        act.wait_ge(step, 4 * (b - 2) + 4)
                    nc.scalar.activation(gate[:, b % 2, g], g_ps[g][:, 0:T], ACT.Tanh if g == 0 else ACT.Sigmoid,
                                         bias=b_sb[:, g:g + 1]).then_inc(gate_out, 1)

        @block.vector
        def _(dve):
            for b in range(B):
                k = b % 2
                dve.wait_ge(gate_out, 3 * b + 3)
                nc.vector.tensor_tensor(fz[:, k], gate[:, k, 1], gate[:, k, 0], ALU.mult).then_inc(step, 1)
                dve.wait_ge(step, 4 * b + 1)
                nc.vector.tensor_tensor(inp[:, k], gate[:, k, 0], fz[:, k], ALU.subtract).then_inc(step, 1)
                dve.wait_ge(step, 4 * b + 2)
                nc.vector.tensor_tensor_scan(cell[:, k], gate[:, k, 1], inp[:, k], 0.0, ALU.mult, ALU.add).then_inc(step, 1)
                dve.wait_ge(step, 4 * b + 3)
                if b >= 2:
                    dve.wait_ge(stored[k], 16 * (b // 2))
                nc.vector.tensor_tensor(h_sb[:, k], gate[:, k, 2], cell[:, k], ALU.mult).then_inc(step, 1)


def stage_norm(nc, name, h_in, n_out, o_in=None, sum_in=None, w_o=None, cols=None, h_out=None, conv=False):
    with ExitStack() as ctx:
        sems = []
        ctx.callback(end_stage, nc, sems)
        sb = lambda n, shape, dt=F32: ctx.enter_context(nc.sbuf_tensor(f"{name}_{n}", shape, dt))

        def sem(n):
            sems.append(nc.alloc_semaphore(f"{name}_{n}"))
            return sems[-1]

        norm = n_out is not None
        h_sb = sb("h", [P, B, T])
        col_sb = sb("cols", [P, 5])
        avg = sb("avg", [P, P])
        eps_sb = sb("eps", [P, 1])
        d_sb = sb("d", [P, 2, T])
        sq = sb("sq", [P, 2, T])
        r_sb = sb("r", [P, 2, T])
        n_sb = sb("n", [P, 2, T + 2])
        y_sb = sb("y", [P, 2, T])
        o_sb = sb("o", [P, B, T])
        sum_sb = sb("sum", [P, B, T])
        w_sb = sb("w", [P, P])
        o_ps = [ctx.enter_context(nc.psum_tensor(f"{name}_o_ps{k}", [P, 2 * BANK], F32)) for k in range(2)]
        m_ps = ctx.enter_context(nc.psum_tensor(f"{name}_m_ps", [P, 2 * BANK], F32))
        v_ps = ctx.enter_context(nc.psum_tensor(f"{name}_v_ps", [P, 2 * BANK], F32))
        w_loaded = sem("w_loaded")
        loaded = [sem(f"loaded{b}") for b in range(B)]
        share_step = sem("share_step")
        o_mm = sem("o_mm")
        h_done = sem("h_done")
        mean_mm = sem("mean_mm")
        d_done = sem("d_done")
        sq_done = sem("sq_done")
        var_mm = sem("var_mm")
        root_done = sem("root_done")
        r_done = sem("r_done")
        n_done = sem("n_done")
        conv_step = sem("conv_step")
        ready = sem("ready")
        edge_done = sem("edge_done")
        h_stored = sem("h_stored")
        n_stored = [sem(f"n_stored{k}") for k in range(2)]
        LOADS = 48 if o_in is not None else 16
        W_LOADS = 32 if o_in is not None else 16
        block = ctx.enter_context(nc.Block())

        @block.sync
        def _(sp):
            if cols is not None:
                sp.dma_start(col_sb[:], cols).then_inc(w_loaded, 16)
            if o_in is not None:
                sp.dma_start(w_sb[:], w_o).then_inc(w_loaded, 16)
            for b in range(B):
                sp.dma_start(h_sb[:, b], h_in[:, b]).then_inc(loaded[b], 16)
                if o_in is not None:
                    sp.dma_start(o_sb[:, b], o_in[b]).then_inc(loaded[b], 16)
                    sp.dma_start(sum_sb[:, b], sum_in[b]).then_inc(loaded[b], 16)
            for b in range(B):
                if h_out is not None:
                    sp.wait_ge(h_done, b + 1)
                    sp.dma_start(h_out[:, b], h_sb[:, b]).then_inc(h_stored, 16)
                if norm:
                    sp.wait_ge(ready, b + 1)
                    sp.dma_start(n_out[:, b], (y_sb if conv else n_sb)[:, b % 2, 0:T] if conv else n_sb[:, b % 2, 1:T + 1]
                                 ).then_inc(n_stored[b % 2], 16)
            if h_out is not None:
                sp.wait_ge(h_stored, 16 * B)
            if norm:
                for k in range(2):
                    sp.wait_ge(n_stored[k], 16 * (B // 2))

        @block.tensor
        def _(pe):
            def project(b):
                if b == 0:
                    pe.wait_ge(w_loaded, 32)
                pe.wait_ge(share_step, 2 * b + 2)
                if b >= 2:
                    pe.wait_ge(h_done, b - 1)
                for lo, hi in COLS_OF:
                    mm = nc.tensor.matmul(o_ps[b % 2][:, lo:hi], w_sb[:], o_sb[:, b, lo:hi], start=True, stop=True)
                mm.then_inc(o_mm, 1)
            def mean(b):
                if o_in is not None:
                    project(b)
                if not norm:
                    return
                if o_in is not None:
                    pe.wait_ge(h_done, b + 1)
                else:
                    pe.wait_ge(loaded[b], LOADS)
                if b:
                    pe.wait_ge(d_done, b)
                for lo, hi in COLS_OF:
                    mm = nc.tensor.matmul(m_ps[:, lo:hi], avg[:], h_sb[:, b, lo:hi], start=True, stop=True)
                mm.then_inc(mean_mm, 1)

            def variance(b):
                pe.wait_ge(sq_done, b + 1)
                if b:
                    pe.wait_ge(root_done, b)
                for lo, hi in COLS_OF:
                    mm = nc.tensor.matmul(v_ps[:, lo:hi], avg[:], sq[:, b % 2, lo:hi], start=True, stop=True)
                mm.then_inc(var_mm, 1)

            if norm:
                pe.wait_ge(edge_done, 1)
            mean(0)
            for b in range(B):
                if b + 1 < B:
                    mean(b + 1)
                if norm:
                    variance(b)

        @block.scalar
        def _(act):
            if norm:
                act.wait_ge(edge_done, 1)

            def square(b):
                act.wait_ge(d_done, b + 1)
                if b >= 2:
                    act.wait_ge(var_mm, b - 1)
                nc.scalar.activation(sq[:, b % 2], d_sb[:, b % 2], ACT.Square).then_inc(sq_done, 1)

            if norm:
                square(0)
            for b in range(B if norm else 0):
                if b + 1 < B:
                    square(b + 1)
                act.wait_ge(var_mm, b + 1)
                if b >= 2:
                    act.wait_ge(ready, b - 1)
                nc.scalar.activation(r_sb[:, b % 2], v_ps[:, 0:T], ACT.Sqrt, bias=eps_sb[:]).then_inc(root_done, 1)

        @block.vector
        def _(dve):
            nc.vector.memset(avg[:], 1.0 / P)
            nc.vector.memset(eps_sb[:], EPS)
            nc.vector.memset(n_sb[:], 0.0).then_inc(edge_done, 1)
            dve.wait_ge(edge_done, 1)
            if cols is not None:
                dve.wait_ge(w_loaded, W_LOADS)

            def share(b):
                dve.wait_ge(loaded[b], LOADS)
                nc.vector.reciprocal(sum_sb[:, b], sum_sb[:, b]).then_inc(share_step, 1)
                dve.wait_ge(share_step, 2 * b + 1)
                nc.vector.tensor_tensor(o_sb[:, b], o_sb[:, b], sum_sb[:, b], ALU.mult).then_inc(share_step, 1)

            def differ(b):
                k = b % 2
                if o_in is not None:
                    dve.wait_ge(o_mm, b + 1)
                    dve.wait_ge(loaded[b], LOADS)
                    nc.vector.scalar_tensor_tensor(h_sb[:, b], o_ps[k][:, 0:T], col_sb[:, 0:1], h_sb[:, b],
                                                   ALU.add, ALU.add).then_inc(h_done, 1)
                if norm:
                    dve.wait_ge(mean_mm, b + 1)
                    if b >= 2:
                        dve.wait_ge(ready, b - 1)
                    nc.vector.tensor_tensor(d_sb[:, k], h_sb[:, b], m_ps[:, 0:T], ALU.subtract).then_inc(d_done, 1)

            if o_in is not None:
                share(0)
                share(1)
            differ(0)
            for b in range(B):
                k = b % 2
                if o_in is not None and b + 2 < B:
                    share(b + 2)
                if b + 1 < B:
                    differ(b + 1)
                if not norm:
                    continue
                dve.wait_ge(root_done, b + 1)
                nc.vector.reciprocal(r_sb[:, k], r_sb[:, k]).then_inc(r_done, 1)
                dve.wait_ge(r_done, b + 1)
                if b >= 2:
                    dve.wait_ge(n_stored[k], 16 * (b // 2))
                done = n_done if conv else ready
                nc.vector.tensor_tensor(n_sb[:, k, 1:T + 1], d_sb[:, k], r_sb[:, k], ALU.mult).then_inc(done, 1)
                if conv:
                    dve.wait_ge(n_done, b + 1)
                    nc.vector.tensor_scalar(y_sb[:, k], n_sb[:, k, 0:T], col_sb[:, 2:3], col_sb[:, 1:2],
                                            ALU.mult, ALU.add).then_inc(conv_step, 1)
                    for tap in (1, 2):
                        dve.wait_ge(conv_step, 3 * b + tap)
                        nc.vector.scalar_tensor_tensor(y_sb[:, k], n_sb[:, k, tap:T + tap], col_sb[:, 2 + tap:3 + tap],
                                                       y_sb[:, k], ALU.mult, ALU.add).then_inc(conv_step, 1)
                    dve.wait_ge(conv_step, 3 * b + 3)
                    nc.vector.tensor_tensor(y_sb[:, k], n_sb[:, k, 1:T + 1], y_sb[:, k], ALU.add).then_inc(ready, 1)


def stage_qkv(nc, name, src, w_qkv, cols, v_bias, q_parts, k_parts, v_aug, experts, heads, scale):
    KC = src.shape[1]
    F = heads * HD
    MC = F // P
    G = heads // 4
    TT = [(lo, min(lo + P, T)) for lo in range(0, T, P)]
    NT = len(TT)
    U = B * G
    QK = 2 * MC
    with ExitStack() as ctx:
        sems = []
        ctx.callback(end_stage, nc, sems)
        sb = lambda n, shape, dt=F32: ctx.enter_context(nc.sbuf_tensor(f"{name}_{n}", shape, dt))

        def sem(n):
            sems.append(nc.alloc_semaphore(f"{name}_{n}"))
            return sems[-1]

        w_sb = sb("w", [P, experts, KC, 3 * F])
        col_sb = sb("cols", [P, experts, 2 * MC])
        vb_sb = sb("vb", [P, experts, F])
        s_sb = sb("s", [P, 2, KC, T])
        whole = sb("whole", [P, 2, T])
        rest = sb("rest", [P, 2, T])
        part = sb("part", [P, QK, 3, T], BF16)
        v_sb = sb("v", [P, NT, G, 4, 2 * HD])
        qk_ps = [ctx.enter_context(nc.psum_tensor(f"{name}_qk_ps{k}", [P, 2 * BANK], F32)) for k in range(2)]
        v_ps = [ctx.enter_context(nc.psum_tensor(f"{name}_v_ps{k}", [P, BANK], F32)) for k in range(2)]
        w_loaded = [sem(f"w_loaded{e}") for e in range(experts)]
        s_loaded = [sem(f"s_loaded{k}") for k in range(2)]
        qk_mm = sem("qk_mm")
        whole_done = sem("whole_done")
        part_done = [sem(f"part{p}_done") for p in range(3)]
        rest_done = sem("rest_done")
        part_stored = [sem(f"part_stored{m}") for m in range(QK)]
        v_mm = sem("v_mm")
        v_done = sem("v_done")
        v_stored = [sem(f"v_stored{m}") for m in range(NT)]
        ones_done = sem("ones_done")
        start_from_one(nc, (part_stored, v_done, v_stored, whole_done,))
        block = ctx.enter_context(nc.Block())
        JOBS = 2 * experts
        trips = B // 2

        def put_source(sp, n, i):
            bb, e = divmod(n, experts)
            sp.dma_start(s_sb[:, n % 2], src[e].rearrange("k p b t -> p k b t")[:, :, bass.ds(2 * i + bb, 1), :]
                         .rearrange("p k o t -> p k (o t)")).then_inc(s_loaded[n % 2], 16)

        @block.sync
        def _(sp):
            put_source(sp, 0, 0)
            for e in range(experts):
                sp.dma_start(w_sb[:, e], w_qkv[e].rearrange("(k p) n -> p k n", p=P)).then_inc(w_loaded[e], 16)
                sp.dma_start(col_sb[:, e], cols[e]).then_inc(w_loaded[e], 16)
                sp.dma_start(vb_sb[:, e], v_bias[e:e + 1].partition_broadcast(P)).then_inc(w_loaded[e], 16)
                if e == 0:
                    put_source(sp, 1, 0)

            def trip(i, last):
                for n in range(JOBS):
                    job = i * JOBS + n
                    bb, e = divmod(n, experts)
                    u = (2 * i + bb) * G + e * U
                    u = u if last else sp.snap(u)
                    for m in range(max(QK + 1, NT)):
                        if m < NT:
                            lo, hi = TT[m]
                            sp.wait_ge(v_done, NT * job + m + 2)
                            sp.dma_start(v_aug[bass.ds(u, G), lo:hi].rearrange("g t n -> t g n"),
                                         v_sb[0:hi - lo, m].rearrange("p g h d -> p g (h d)")).then_inc(v_stored[m], 16)
                        if 1 <= m <= QK:
                            qk = m - 1
                            dst = q_parts if qk < MC else k_parts
                            g = 2 * (qk % MC)
                            sp.wait_ge(part_done[2], QK * job + qk + 1)
                            for half in range(2):
                                sp.dma_start(dst[bass.ds(u + g + half, 1)].rearrange("o s r t -> r (o s) t"),
                                               part[half * 64:half * 64 + 64, qk]).then_inc(part_stored[qk], 16)
                    if n + 2 < JOBS:
                        put_source(sp, n + 2, i)
                    elif not last:
                        put_source(sp, n + 2 - JOBS, i + 1)
            if trips > 1:
                with sp.Fori(0, trips - 1) as i:
                    trip(i, False)
            trip(trips - 1, True)
            for m in range(QK):
                sp.wait_ge(part_stored[m], 32 * JOBS * trips + 1)
            for m in range(NT):
                sp.wait_ge(v_stored[m], 16 * JOBS * trips + 1)

        @block.tensor
        def _(pe):
            with pe.Fori(0, trips) as i:
                for n in range(JOBS):
                    bb, e = divmod(n, experts)
                    job = i * JOBS + n
                    if n < experts:
                        pe.wait_ge(w_loaded[e], 48)
                    pe.wait_ge(s_loaded[n % 2], i * (16 * (JOBS // 2)) + 16 * (n // 2 + 1))
                    for m in range(max(QK, NT)):
                        if m < QK:
                            if n or m >= 2:
                                pe.wait_ge(whole_done, QK * job + m)
                            else:
                                pe.wait_ge(whole_done, QK * job + 1)
                            for lo, hi in COLS_OF:
                                for c in range(KC):
                                    mm = nc.tensor.matmul(qk_ps[m % 2][:, lo:hi], w_sb[:, e, c, m * P:(m + 1) * P],
                                                          s_sb[:, n % 2, c, lo:hi], start=(c == 0), stop=(c == KC - 1))
                            mm.then_inc(qk_mm, 1)
                        if m < NT:
                            lo, hi = TT[m]
                            if n or m >= 2:
                                pe.wait_ge(v_done, NT * job + m)
                            else:
                                pe.wait_ge(v_done, NT * job + 1)
                            for c in range(KC):
                                mm = nc.tensor.matmul(v_ps[m % 2][0:hi - lo, 0:F], s_sb[:, n % 2, c, lo:hi],
                                                      w_sb[:, e, c, 2 * F:3 * F], start=(c == 0), stop=(c == KC - 1))
                            mm.then_inc(v_mm, 1)

        @block.scalar
        def _(act):
            with act.Fori(0, trips) as i:
                for n in range(JOBS):
                    job = i * JOBS + n
                    for m in range(QK):
                        count = QK * job + m + 1
                        k = m % 2
                        act.wait_ge(whole_done, count + 1)
                        act.wait_ge(part_stored[m], job * 32 + 1)
                        nc.scalar.activation(part[:, m, 0], whole[:, k], ACT.Copy).then_inc(part_done[0], 1)
                        act.wait_ge(rest_done, count)
                        nc.scalar.activation(part[:, m, 1], rest[:, k], ACT.Copy).then_inc(part_done[1], 1)

        @block.vector
        def _(dve):
            nc.vector.memset(v_sb[:], 1.0).then_inc(ones_done, 1)
            dve.wait_ge(ones_done, 1)
            with dve.Fori(0, trips) as i:
                for n in range(JOBS):
                    bb, e = divmod(n, experts)
                    job = i * JOBS + n
                    if n < experts:
                        dve.wait_ge(w_loaded[e], 48)

                    def last_part(m):
                        k = m % 2
                        dve.wait_ge(part_done[1], QK * job + m + 1)
                        nc.vector.tensor_tensor(part[:, m, 2], rest[:, k], part[:, m, 1], ALU.subtract
                                                ).then_inc(part_done[2], 1)

                    for m in range(max(QK, NT)):
                        if m < QK:
                            k = m % 2
                            dve.wait_ge(qk_mm, QK * job + m + 1)
                            nc.vector.tensor_scalar(whole[:, k], qk_ps[k][:, 0:T], col_sb[:, e, m:m + 1],
                                                    scale if m < MC else 1.0, ALU.add, ALU.mult).then_inc(whole_done, 1)
                        if m < NT:
                            lo, hi = TT[m]
                            dve.wait_ge(v_mm, NT * job + m + 1)
                            dve.wait_ge(v_stored[m], job * 16 + 1)
                            nc.vector.tensor_tensor(v_sb[0:hi - lo, m, :, :, 0:HD],
                                                    v_ps[m % 2][0:hi - lo, 0:F].rearrange("p (g h d) -> p g h d", g=G, h=4),
                                                    vb_sb[0:hi - lo, e].rearrange("p (g h d) -> p g h d", g=G, h=4), ALU.add
                                                    ).then_inc(v_done, 1)
                        if 1 <= m <= QK:
                            last_part(m - 1)
                        if m < QK:
                            dve.wait_ge(part_done[0], QK * job + m + 1)
                            nc.vector.tensor_tensor(rest[:, k], whole[:, k], part[:, m, 0], ALU.subtract).then_inc(rest_done, 1)


def stage_encode(nc, n_in, w1, w2, cols, e_out):
    D = D_EXPERT
    with ExitStack() as ctx:
        sems = []
        ctx.callback(end_stage, nc, sems)
        sb = lambda n, shape, dt=F32: ctx.enter_context(nc.sbuf_tensor(f"enc_{n}", shape, dt))

        def sem(n):
            sems.append(nc.alloc_semaphore(f"enc_{n}"))
            return sems[-1]

        w1_sb = sb("w1", [P, E, D])
        w2_sb = sb("w2", [P, E, 2, D])
        col_sb = sb("cols", [P, E, 8])
        avg = sb("avg", [P, P])
        eps_sb = sb("eps", [P, 1])
        n_sb = sb("n", [P, B, T])
        a_sb = sb("a", [P, 2, 2, T])
        x_sb = sb("x", [P, 2, 2, T])
        sq = sb("sq", [P, 2, T])
        r_sb = sb("r", [P, T])
        h_sb = sb("h", [P, 2, 2, T])
        a_ps = [ctx.enter_context(nc.psum_tensor(f"enc_a_ps{k}", [P, 2 * BANK], F32)) for k in range(2)]
        m_ps = ctx.enter_context(nc.psum_tensor("enc_m_ps", [P, 2 * BANK], F32))
        w_loaded = [sem(f"w_loaded{e}") for e in range(E)]
        n_loaded = [sem(f"n_loaded{b}") for b in range(B)]
        const_done = sem("const_done")
        a_mm, a_out, x_mm, x_out = sem("a_mm"), sem("a_out"), sem("x_mm"), sem("x_out")
        mean_mm, var_mm = sem("mean_mm"), sem("var_mm")
        d_done, sq_done, y_done, h_done = sem("d_done"), sem("sq_done"), sem("y_done"), sem("h_done")
        root_done, r_done = sem("root_done"), sem("r_done")
        stored = [sem(f"stored{k}") for k in range(2)]
        JOBS = B * E
        block = ctx.enter_context(nc.Block())

        @block.sync
        def _(sp):
            sp.dma_start(n_sb[:, 0], n_in[:, 0]).then_inc(n_loaded[0], 16)
            for e in range(E):
                sp.dma_start(w1_sb[:, e], w1[e]).then_inc(w_loaded[e], 16)
                sp.dma_start(w2_sb[:, e], w2[e].rearrange("(k p) n -> p k n", p=P)).then_inc(w_loaded[e], 16)
                sp.dma_start(col_sb[:, e], cols[e]).then_inc(w_loaded[e], 16)
            for b in range(1, B):
                sp.dma_start(n_sb[:, b], n_in[:, b]).then_inc(n_loaded[b], 16)
            for n in range(JOBS):
                sp.wait_ge(h_done, n * 2 + 2)
                sp.dma_start(e_out[n % E].rearrange("c p b t -> p c b t")[:, :, n // E:n // E + 1]
                             .rearrange("p c o t -> p c (o t)"), h_sb[:, n % 2]).then_inc(stored[n % 2], 16)
            for k in range(2):
                sp.wait_ge(stored[k], 16 * (JOBS // 2))

        @block.tensor
        def _(pe):
            pe.wait_ge(const_done, 1)
            def first(e):
                if e < E:
                    pe.wait_ge(w_loaded[e], 48)
                if e % E == 0:
                    pe.wait_ge(n_loaded[e // E], 16)
                for m in range(2):
                    if e:
                        pe.wait_ge(x_out, (e - 1) * 2 + m + 1)
                    for lo, hi in COLS_OF:
                        mm = nc.tensor.matmul(a_ps[m][:, lo:hi], w1_sb[:, e % E, m * P:(m + 1) * P], n_sb[:, e // E, lo:hi],
                                              start=True, stop=True)
                    mm.then_inc(a_mm, 1)

            def second(e):
                for m in range(2):
                    pe.wait_ge(a_out, e * 2 + 2)
                    for lo, hi in COLS_OF:
                        for c in range(2):
                            mm = nc.tensor.matmul(a_ps[m][:, lo:hi], w2_sb[:, e % E, c, m * P:(m + 1) * P],
                                                  a_sb[:, e % 2, c, lo:hi], start=(c == 0), stop=(c == 1))
                    mm.then_inc(x_mm, 1)

            def mean(e):
                pe.wait_ge(x_out, e * 2 + 2)
                pe.wait_ge(root_done, e)
                for lo, hi in COLS_OF:
                    for c in range(2):
                        mm = nc.tensor.matmul(m_ps[:, lo:hi], avg[:], x_sb[:, e % 2, c, lo:hi], start=(c == 0), stop=(c == 1))
                mm.then_inc(mean_mm, 1)

            def variance(e):
                pe.wait_ge(sq_done, e * 2 + 2)
                for lo, hi in COLS_OF:
                    for c in range(2):
                        mm = nc.tensor.matmul(m_ps[:, lo:hi], avg[:], sq[:, c, lo:hi], start=(c == 0), stop=(c == 1))
                mm.then_inc(var_mm, 1)

            first(0)
            second(0)
            first(1)
            for e in range(JOBS):
                mean(e)
                if e + 1 < JOBS:
                    second(e + 1)
                variance(e)
                if e + 2 < JOBS:
                    first(e + 2)

        @block.scalar
        def _(act):
            act.wait_ge(const_done, 1)
            def hidden(e):
                for m in range(2):
                    act.wait_ge(a_mm, e * 2 + m + 1)
                    nc.scalar.activation(a_sb[:, e % 2, m], a_ps[m][:, 0:T], ACT.Relu, bias=col_sb[:, e % E, m:m + 1]
                                         ).then_inc(a_out, 1)

            def scaled(e):
                for m in range(2):
                    act.wait_ge(y_done, e * 2 + m + 1)
                    act.wait_ge(stored[e % 2], 16 * (e // 2))
                    nc.scalar.activation(h_sb[:, e % 2, m], x_sb[:, e % 2, m], ACT.Identity, bias=col_sb[:, e % E, 6 + m:7 + m],
                                         scale=col_sb[:, e % E, 4 + m:5 + m]).then_inc(h_done, 1)

            def evacuate(e):
                for m in range(2):
                    act.wait_ge(x_mm, e * 2 + m + 1)
                    if e >= 2:
                        act.wait_ge(h_done, (e - 1) * 2)
                    nc.scalar.activation(x_sb[:, e % 2, m], a_ps[m][:, 0:T], ACT.Identity, bias=col_sb[:, e % E, 2 + m:3 + m]
                                         ).then_inc(x_out, 1)

            hidden(0)
            evacuate(0)
            hidden(1)
            for e in range(JOBS):
                for m in range(2):
                    act.wait_ge(d_done, e * 2 + m + 1)
                    act.wait_ge(var_mm, e)
                    nc.scalar.activation(sq[:, m], x_sb[:, e % 2, m], ACT.Square).then_inc(sq_done, 1)
                if e:
                    scaled(e - 1)
                if e + 1 < JOBS:
                    evacuate(e + 1)
                act.wait_ge(var_mm, e + 1)
                act.wait_ge(y_done, e * 2)
                nc.scalar.activation(r_sb[:], m_ps[:, 0:T], ACT.Sqrt, bias=eps_sb[:]).then_inc(root_done, 1)
                if e + 2 < JOBS:
                    hidden(e + 2)
            scaled(JOBS - 1)

        @block.vector
        def _(dve):
            nc.vector.memset(eps_sb[:], EPS)
            nc.vector.memset(avg[:], 1.0 / D).then_inc(const_done, 1)
            for e in range(JOBS):
                dve.wait_ge(mean_mm, e + 1)
                for m in range(2):
                    nc.vector.tensor_tensor(x_sb[:, e % 2, m], x_sb[:, e % 2, m], m_ps[:, 0:T], ALU.subtract
                                            ).then_inc(d_done, 1)
                dve.wait_ge(root_done, e + 1)
                nc.vector.reciprocal(r_sb[:], r_sb[:]).then_inc(r_done, 1)
                dve.wait_ge(r_done, e + 1)
                dve.wait_ge(sq_done, e * 2 + 2)
                for m in range(2):
                    nc.vector.tensor_tensor(x_sb[:, e % 2, m], x_sb[:, e % 2, m], r_sb[:], ALU.mult).then_inc(y_done, 1)




def stage_lstm_inputs(nc, o_in, sum_in, w_o, w_i, cols, xw):
    D = D_EXPERT
    with ExitStack() as ctx:
        sems = []
        ctx.callback(end_stage, nc, sems)
        sb = lambda n, shape, dt=F32: ctx.enter_context(nc.sbuf_tensor(f"xw_{n}", shape, dt))

        def sem(n):
            sems.append(nc.alloc_semaphore(f"xw_{n}"))
            return sems[-1]

        wo_sb = sb("wo", [P, E, 2, D])
        wi_sb = sb("wi", [P, E, 2, 2, 4 * D])
        col_sb = sb("cols", [P, E, 18])
        o_sb = sb("o", [P, 2, 2, B, CT])
        sum_sb = sb("sum", [P, 2, 2, B, CT])
        a_sb = sb("a", [P, 2, 2, CW])
        x_sb = sb("x", [P, 2, 2, CT, 8, B])
        a_ps = [ctx.enter_context(nc.psum_tensor(f"xw_a_ps{k}", [P, BANK], F32)) for k in range(2)]
        x_ps = [ctx.enter_context(nc.psum_tensor(f"xw_x_ps{k}", [P, BANK], F32)) for k in range(4)]
        w_loaded = [sem(f"w_loaded{e}") for e in range(E)]
        cols_loaded = sem("cols_loaded")
        o_loaded = [sem(f"o_loaded{k}") for k in range(2)]
        share_step = sem("share_step")
        a_mm, a_out = sem("a_mm"), sem("a_out")
        x_mm = sem("x_mm")
        x_out = sem("x_out")
        stored = [sem(f"stored{k}") for k in range(2)]
        start_from_one(nc, (a_out, stored, x_out,))
        block = ctx.enter_context(nc.Block())
        trips = T // CT
        half = E // 2

        def put_o(sp, i, e):
            for c in range(2):
                for dst, src in ((o_sb, o_in), (sum_sb, sum_in)):
                    sp.dma_start(dst[:, e % 2, c], src[e].rearrange("b (c p) t -> c p b t", p=P)[c][:, :, bass.ds(i * CT, CT)]
                                 ).then_inc(o_loaded[e % 2], 16)

        @block.sync
        def _(sp):
            for e in range(E):
                sp.dma_start(col_sb[:, e], cols[e]).then_inc(cols_loaded, 16)
            put_o(sp, 0, 0)
            for e in range(E):
                sp.dma_start(wo_sb[:, e], w_o[e].rearrange("(k p) n -> p k n", p=P)).then_inc(w_loaded[e], 16)
                for d in range(2):
                    sp.dma_start(wi_sb[:, e, d], w_i[d][e].rearrange("(k p) n -> p k n", p=P)).then_inc(w_loaded[e], 16)
                if e == 0:
                    put_o(sp, 0, 1)

            def trip(i, last):
                for e in range(E):
                    job = i * E + e
                    sp.wait_ge(a_mm, job * 2 + 2)
                    if e + 2 < E:
                        put_o(sp, i, e + 2)
                    elif not last:
                        put_o(sp, i + 1, e + 2 - E)
                    for d in range(2):
                        sp.wait_ge(x_out, job * 16 + 8 * d + 8 + 1)
                        sp.dma_start(xw[d, e][:, bass.ds(i * CT, CT)].rearrange("p t g -> p (t g)"),
                                     x_sb[:, e % 2, d].rearrange("p t m b -> p (t m b)")).then_inc(stored[e % 2], 16)
            with sp.Fori(0, trips - 1) as i:
                trip(i, False)
            trip(trips - 1, True)
            for k in range(2):
                sp.wait_ge(stored[k], 32 * half * trips + 1)

        @block.tensor
        def _(pe):
            with pe.Fori(0, trips) as i:
                def attend(e):
                    pe.wait_ge(w_loaded[e], 48)
                    pe.wait_ge(share_step, (i * E + e) * 2 + 2)
                    for m in range(2):
                        pe.wait_ge(a_out, ((i * E + e - 1) * 2 + m + 1 if e else i * (E * 2)) + 1)
                        for c in range(2):
                            mm = nc.tensor.matmul(a_ps[m][:, 0:CW], wo_sb[:, e, c, m * P:(m + 1) * P],
                                                  o_sb[:, e % 2, c].rearrange("p b t -> p t b"), start=(c == 0), stop=(c == 1))
                        mm.then_inc(a_mm, 1)
                attend(0)
                for e in range(E):
                    job = i * E + e
                    for n in range(16):
                        d, m = divmod(n, 8)
                        if n == 0:
                            pe.wait_ge(a_out, job * 2 + 3)
                        if e or n >= 4:
                            pe.wait_ge(x_out, job * 16 + n - 3 + 1)
                        else:
                            pe.wait_ge(x_out, job * 16 + 1)
                        for c in range(2):
                            mm = nc.tensor.matmul(x_ps[n % 4][:, 0:CW], wi_sb[:, e, d, c, COLS[m] * P:(COLS[m] + 1) * P],
                                                  a_sb[:, e % 2, c], start=(c == 0), stop=(c == 1))
                        mm.then_inc(x_mm, 1)
                        if n == 7 and e + 1 < E:
                            attend(e + 1)

        def put_x(eng, i, e, n):
            d, m = divmod(n, 8)
            job = i * E + e
            eng.wait_ge(x_mm, job * 16 + n + 1)
            if n < 2:
                eng.wait_ge(stored[e % 2], i * (32 * half) + 32 * (e // 2) + 1)
            out = x_sb[:, e % 2, d, :, m]
            src = x_ps[n % 4][:, 0:CW].rearrange("p (t b) -> p t b", b=B)
            return out, src, col_sb[:, e, 2 + 8 * d + COLS[m]:3 + 8 * d + COLS[m]]

        @block.scalar
        def _(act):
            act.wait_ge(cols_loaded, 16 * E)
            with act.Fori(0, trips) as i:
                def attended(e):
                    for m in range(2):
                        act.wait_ge(a_mm, (i * E + e) * 2 + m + 1)
                        if e >= 2:
                            act.wait_ge(x_mm, (i * E + e - 1) * 16)
                        nc.scalar.activation(a_sb[:, e % 2, m], a_ps[m][:, 0:CW], ACT.Identity, bias=col_sb[:, e, m:m + 1]
                                             ).then_inc(a_out, 1)
                attended(0)
                for e in range(E):
                    for n in range(16):
                        out, src, bias = put_x(act, i, e, n)
                        nc.scalar.activation(out, src, ACT.Identity, bias=bias).then_inc(x_out, 1)
                        if n == 8 and e + 1 < E:
                            attended(e + 1)

        @block.vector
        def _(dve):
            with dve.Fori(0, trips) as i:
                def share(e):
                    dve.wait_ge(o_loaded[e % 2], i * (64 * half) + 64 * (e // 2 + 1))
                    flat = lambda x: x[:, e % 2].rearrange("p c b t -> p (c b t)")
                    nc.vector.reciprocal(flat(sum_sb), flat(sum_sb)).then_inc(share_step, 1)
                    dve.wait_ge(share_step, (i * E + e) * 2 + 1)
                    nc.vector.tensor_tensor(flat(o_sb), flat(o_sb), flat(sum_sb), ALU.mult).then_inc(share_step, 1)
                for e in range(E):
                    share(e)


def stage_decode(nc, mem, n_in, h_in, w_s1, w_s2, w_t1, w_t2, w_d1, w_d2, w_r, cols, h_out):
    D = D_EXPERT
    S1, S2, T1, T2, D1, D2, GG, BETA, RB = 0, 2, 4, 6, 8, 10, 11, 12, 13
    with ExitStack() as ctx:
        sems = []
        ctx.callback(end_stage, nc, sems)
        sb = lambda n, shape, dt=F32: ctx.enter_context(nc.sbuf_tensor(f"dec_{n}", shape, dt))

        def sem(n):
            sems.append(nc.alloc_semaphore(f"dec_{n}"))
            return sems[-1]

        s1, t1 = sb("s1", [P, E, 4, D]), sb("t1", [P, E, 4, D])
        s2, t2, d1 = sb("s2", [P, E, 2, D]), sb("t2", [P, E, 2, D]), sb("d1", [P, E, 2, D])
        d2 = sb("d2", [P, E, 2, P])
        wr_sb = sb("wr", [P, E])
        wr_rep = sb("wr_rep", [P, E, P])
        col_sb = sb("cols", [P, E, 14])
        avg = sb("avg", [P, P])
        eps_sb = sb("eps", [P, 1])
        m_sb = sb("m", [P, 2, 4, CW])
        n_sb = sb("n", [P, B, CT])
        h_sb = sb("h", [P, B, CT])
        log = sb("log", [P, E, CW])
        top = sb("top", [P, 2, CW])
        hid = sb("hid", [P, 4, CW])
        gate = sb("gate", [P, 4, CW])
        g_sb = sb("g", [P, 2, CW])
        dh = sb("dh", [P, 2, CW])
        x_sb = sb("x", [P, 2, CW])
        sq = sb("sq", [P, CW])
        r_sb = sb("r", [P, CW])
        acc = sb("acc", [P, CW])
        share = sb("share", [P, CW])
        u_ps = [ctx.enter_context(nc.psum_tensor(f"dec_u_ps{k}", [P, BANK], F32)) for k in range(4)]
        d_ps = [ctx.enter_context(nc.psum_tensor(f"dec_d_ps{k}", [P, BANK], F32)) for k in range(2)]
        y_ps = ctx.enter_context(nc.psum_tensor("dec_y_ps", [P, BANK], F32))
        m_ps = ctx.enter_context(nc.psum_tensor("dec_m_ps", [P, BANK], F32))
        w_loaded = [sem(f"w_loaded{e}") for e in range(E)]
        cols_loaded, const_done = sem("cols_loaded"), sem("const_done")
        rep_done = sem("rep_done")
        m_loaded = [sem(f"m_loaded{k}") for k in range(2)]
        n_loaded, h_loaded = sem("n_loaded"), sem("h_loaded")
        log_mm, log_out = sem("log_mm"), sem("log_out")
        soft = sem("soft")
        exp_done = sem("exp_done")
        u_mm, hid_out = sem("u_mm"), sem("hid_out")
        v_mm, gate_out = sem("v_mm"), sem("gate_out")
        g_done, d_mm, dh_out = sem("g_done"), sem("d_mm"), sem("dh_out")
        y_mm, x_out, mean_mm, sub_done, sq_done, var_mm, root_done = (
            sem(n) for n in ("y_mm", "x_out", "mean_mm", "sub_done", "sq_done", "var_mm", "root_done"))
        fin = sem("fin")
        ready = sem("ready")
        stored = sem("stored")
        SOFT, FIN = 15, 5
        start_from_one(nc, (d_mm, dh_out, fin, g_done, gate_out, hid_out, log_mm, root_done, stored, v_mm, var_mm, x_out, y_mm,))
        block = ctx.enter_context(nc.Block())
        trips = T // CT
        half = E // 2

        def put_mem(sp, i, e):
            for k in range(4):
                sp.dma_start(m_sb[:, e % 2, k], mem[k // 2, e, k % 2][:, bass.ds(i * CT, CT)].rearrange("p t b -> p (t b)")
                             ).then_inc(m_loaded[e % 2], 16)

        @block.sync
        def _(sp):
            for e in range(E):
                sp.dma_start(col_sb[:, e], cols[e]).then_inc(cols_loaded, 16)
            sp.dma_start(wr_sb[:], w_r).then_inc(cols_loaded, 16)
            sp.dma_start(n_sb[:], n_in[:, :, 0:CT]).then_inc(n_loaded, 16)
            for e in range(E):
                for dst, src in ((s1, w_s1), (s2, w_s2), (t1, w_t1), (t2, w_t2), (d1, w_d1), (d2, w_d2)):
                    sp.dma_start(dst[:, e], src[e].rearrange("(k p) n -> p k n", p=P)).then_inc(w_loaded[e], 16)
                if e < 2:
                    put_mem(sp, 0, e)

            def put_h(i):
                sp.wait_ge(ready, i)
                sp.dma_start(h_out[:, :, bass.ds(i * CT - CT, CT)], h_sb[:]).then_inc(stored, 16)

            def trip(i, first, last):
                if not first:
                    sp.wait_ge(log_mm, i * E + 1)
                    sp.dma_start(n_sb[:], n_in[:, :, bass.ds(i * CT, CT)]).then_inc(n_loaded, 16)
                for e in range(E):
                    sp.wait_ge(u_mm, (i * E + e) * 4 + 4)
                    if e + 2 < E:
                        put_mem(sp, i, e + 2)
                    elif not last:
                        put_mem(sp, i + 1, e + 2 - E)
                    if e == 1:
                        if not first:
                            put_h(i)
                            sp.wait_ge(stored, i * 16 + 1)
                        sp.dma_start(h_sb[:], h_in[:, :, bass.ds(i * CT, CT)]).then_inc(h_loaded, 16)
            trip(0, True, False)
            with sp.Fori(1, trips - 1) as i:
                trip(i, False, False)
            trip(trips - 1, False, True)
            put_h(trips)
            sp.wait_ge(stored, 16 * trips + 1)
        COL_LOADS = 16 * (E + 1)

        @block.tensor
        def _(pe):
            pe.wait_ge(rep_done, E)

            def mean(i, e):
                pe.wait_ge(x_out, i * E + e + 2)
                pe.wait_ge(root_done, i * E + e + 1)
                nc.tensor.matmul(m_ps[:, 0:CW], avg[:], x_sb[:, e % 2], start=True, stop=True).then_inc(mean_mm, 1)

            def variance(i, e):
                pe.wait_ge(sq_done, i * E + e + 1)
                nc.tensor.matmul(m_ps[:, 0:CW], avg[:], sq[:], start=True, stop=True).then_inc(var_mm, 1)

            def trip(i, first_trip):
                pe.wait_ge(n_loaded, i * 16 + 16)
                pe.wait_ge(hid_out, i * (E * 4) + 1)
                for e in range(E):
                    pe.wait_ge(gate_out, i * (E * 4) + 1)
                    nc.tensor.matmul(u_ps[e][:, 0:CW], wr_rep[:, e], n_sb[:].rearrange("p b t -> p t b"),
                                     start=True, stop=True).then_inc(log_mm, 1)

                def first(e, ns):
                    job = i * E + e
                    if 0 in ns and first_trip:
                        pe.wait_ge(w_loaded[e], 16 * 6)
                    if 0 in ns:
                        pe.wait_ge(m_loaded[e % 2], i * (64 * half) + 64 * (e // 2 + 1))
                    for n in ns:
                        w, m = (s1, t1)[n // 2], n % 2
                        if e:
                            pe.wait_ge(gate_out, (job - 1) * 4 + n + 2)
                        else:
                            pe.wait_ge(log_out, i * E + n + 1)
                        for c in range(4):
                            mm = nc.tensor.matmul(u_ps[n][:, 0:CW], w[:, e, c, m * P:(m + 1) * P], m_sb[:, e % 2, c],
                                                  start=(c == 0), stop=(c == 3))
                        mm.then_inc(u_mm, 1)

                def second(e):
                    job = i * E + e
                    for n in range(4):
                        w, m = (s2, t2)[n // 2], n % 2
                        pe.wait_ge(hid_out, job * 4 + max(n + 1, 2 * (n // 2) + 2) + 1)
                        for c in range(2):
                            mm = nc.tensor.matmul(u_ps[n][:, 0:CW], w[:, e, c, m * P:(m + 1) * P], hid[:, 2 * (n // 2) + c],
                                                  start=(c == 0), stop=(c == 1))
                        mm.then_inc(v_mm, 1)

                def decode_first(e):
                    job = i * E + e
                    pe.wait_ge(g_done, job * 2 + 3)
                    for m in range(2):
                        pe.wait_ge(dh_out, job * 2 + 1)
                        for c in range(2):
                            mm = nc.tensor.matmul(d_ps[m][:, 0:CW], d1[:, e, c, m * P:(m + 1) * P], g_sb[:, c],
                                                  start=(c == 0), stop=(c == 1))
                        mm.then_inc(d_mm, 1)

                def decode_second(e):
                    job = i * E + e
                    pe.wait_ge(dh_out, job * 2 + 3)
                    pe.wait_ge(x_out, job + 1)
                    for c in range(2):
                        mm = nc.tensor.matmul(y_ps[:, 0:CW], d2[:, e, c], dh[:, c], start=(c == 0), stop=(c == 1))
                    mm.then_inc(y_mm, 1)

                if not first_trip:
                    mean(i, -1)
                first(0, (0, 1))
                if not first_trip:
                    variance(i, -1)
                first(0, (2, 3))
                for e in range(E):
                    second(e)
                    if e:
                        mean(i, e - 1)
                    if e + 1 < E:
                        first(e + 1, (0, 1))
                    decode_first(e)
                    if e:
                        variance(i, e - 1)
                    if e + 1 < E:
                        first(e + 1, (2, 3))
                    decode_second(e)
            trip(0, True)
            with pe.Fori(1, trips) as i:
                trip(i, False)
            mean(trips, -1)
            variance(trips, -1)

        @block.scalar
        def _(act):
            act.wait_ge(cols_loaded, COL_LOADS)
            act.wait_ge(const_done, 1)

            def square(i, e):
                act.wait_ge(sub_done, i * E + e + 1)
                act.wait_ge(var_mm, i * E + e + 1)
                nc.scalar.activation(sq[:], x_sb[:, e % 2], ACT.Square).then_inc(sq_done, 1)

            def root(i, e):
                act.wait_ge(var_mm, i * E + e + 2)
                act.wait_ge(fin, (i * E + e) * FIN + 1)
                nc.scalar.activation(r_sb[:], m_ps[:, 0:CW], ACT.Sqrt, bias=eps_sb[:]).then_inc(root_done, 1)

            def trip(i, first_trip):
                if not first_trip:
                    square(i, -1)
                act.wait_ge(soft, i * SOFT + 7)
                nc.scalar.activation(log[:].rearrange("p e n -> p (e n)"), log[:].rearrange("p e n -> p (e n)"), ACT.Exp
                                     ).then_inc(exp_done, 1)

                def hidden(e, ns):
                    job = i * E + e
                    for n in ns:
                        act.wait_ge(u_mm, job * 4 + n + 1)
                        act.wait_ge(v_mm, job * 4 + 1)
                        at = (S1, T1)[n // 2] + n % 2
                        nc.scalar.activation(hid[:, n], u_ps[n][:, 0:CW], ACT.Relu, bias=col_sb[:, e, at:at + 1]
                                             ).then_inc(hid_out, 1)

                hidden(0, (0, 1))
                if not first_trip:
                    root(i, -1)
                hidden(0, (2, 3))
                for e in range(E):
                    job = i * E + e
                    for n in range(4):
                        act.wait_ge(v_mm, job * 4 + n + 2)
                        act.wait_ge(g_done, job * 2 + 1)
                        at = (S2, T2)[n // 2] + n % 2
                        nc.scalar.activation(gate[:, n], u_ps[n][:, 0:CW], ACT.Sigmoid if n < 2 else ACT.Tanh,
                                             bias=col_sb[:, e, at:at + 1]).then_inc(gate_out, 1)
                    if e:
                        square(i, e - 1)
                    if e + 1 < E:
                        hidden(e + 1, (0, 1))
                    if e:
                        root(i, e - 1)
                    if e + 1 < E:
                        hidden(e + 1, (2, 3))
            trip(0, True)
            with act.Fori(1, trips) as i:
                trip(i, False)
            square(trips, -1)
            root(trips, -1)

        @block.vector
        def _(dve):
            nc.vector.memset(eps_sb[:], EPS)
            nc.vector.memset(avg[:], 1.0 / P).then_inc(const_done, 1)
            dve.wait_ge(cols_loaded, COL_LOADS)
            for e in range(E):
                nc.vector.tensor_copy(wr_rep[:, e], wr_sb[:, e:e + 1].to_broadcast([P, P])).then_inc(rep_done, 1)

            def sub(i, e):
                dve.wait_ge(mean_mm, i * E + e + 1)
                nc.vector.tensor_tensor(x_sb[:, e % 2], x_sb[:, e % 2], m_ps[:, 0:CW], ALU.subtract).then_inc(sub_done, 1)

            def tail(i, e):
                f = (i * E + e) * FIN
                dve.wait_ge(root_done, i * E + e + 2)
                nc.vector.reciprocal(r_sb[:], r_sb[:]).then_inc(fin, 1)
                dve.wait_ge(fin, f + 2)
                dve.wait_ge(sq_done, i * E + e + 1)
                x = x_sb[:, e % 2]
                nc.vector.tensor_tensor(x, x, r_sb[:], ALU.mult).then_inc(fin, 1)
                dve.wait_ge(fin, f + 3)
                nc.vector.tensor_scalar(x, x, col_sb[:, e % E, GG:GG + 1], col_sb[:, e % E, BETA:BETA + 1], ALU.mult, ALU.add
                                        ).then_inc(fin, 1)
                dve.wait_ge(fin, f + 3 + 1)
                dve.wait_ge(soft, (i + e // E) * SOFT + SOFT)
                dst = x if e else acc[:]
                nc.vector.tensor_tensor(dst, x, share[:] if e % E == E - 1 else log[:, e], ALU.mult).then_inc(fin, 1)
                dve.wait_ge(fin, f + 4 + 1)
                if e:
                    nc.vector.tensor_tensor(acc[:], acc[:], x, ALU.add).then_inc(fin, 1)
                else:
                    nc.vector.memset(top[:, 0, 0:1], 0.0).then_inc(fin, 1)

            def finish(i):
                dve.wait_ge(fin, i * (E * FIN) + 1)
                dve.wait_ge(h_loaded, i * 16)
                nc.vector.tensor_tensor(h_sb[:], h_sb[:], acc[:].rearrange("p (t b) -> p b t", b=B), ALU.add).then_inc(ready, 1)

            def trip(i, first_trip):
                at = i * SOFT
                if not first_trip:
                    dve.wait_ge(fin, i * (FIN * E) - FIN + 1)
                for e in range(E):
                    dve.wait_ge(log_mm, i * E + e + 2)
                    nc.vector.tensor_scalar(log[:, e], u_ps[e][:, 0:CW], col_sb[:, e, RB:RB + 1], None, ALU.add
                                            ).then_inc(log_out, 1)
                if not first_trip:
                    sub(i, -1)
                dve.wait_ge(log_out, i * E + E)
                for k in range(2):
                    nc.vector.tensor_tensor(top[:, k], log[:, 2 * k], log[:, 2 * k + 1], ALU.max).then_inc(soft, 1)
                dve.wait_ge(soft, at + 2)
                nc.vector.tensor_tensor(top[:, 0], top[:, 0], top[:, 1], ALU.max).then_inc(soft, 1)
                dve.wait_ge(soft, at + 3)
                for e in range(E):
                    nc.vector.tensor_tensor(log[:, e], log[:, e], top[:, 0], ALU.subtract).then_inc(soft, 1)
                if not first_trip:
                    tail(i, -1)
                    finish(i)
                dve.wait_ge(exp_done, i + 1)
                for k in range(2):
                    nc.vector.tensor_tensor(top[:, k], log[:, 2 * k], log[:, 2 * k + 1], ALU.add).then_inc(soft, 1)
                dve.wait_ge(soft, at + 9)
                nc.vector.tensor_tensor(top[:, 0], top[:, 0], top[:, 1], ALU.add).then_inc(soft, 1)
                dve.wait_ge(soft, at + 10)
                nc.vector.reciprocal(top[:, 1], top[:, 0]).then_inc(soft, 1)
                dve.wait_ge(soft, at + 11)
                for e in range(E):
                    nc.vector.tensor_tensor(log[:, e] if e < E - 1 else share[:], log[:, e], top[:, 1], ALU.mult).then_inc(soft, 1)

                for e in range(E):
                    job = i * E + e
                    for m in range(2):
                        dve.wait_ge(gate_out, job * 4 + 3 + m + 1)
                        dve.wait_ge(d_mm, job * 2 + 1)
                        nc.vector.tensor_tensor(g_sb[:, m], gate[:, m], gate[:, 2 + m], ALU.mult).then_inc(g_done, 1)
                    if e:
                        sub(i, e - 1)
                    for m in range(2):
                        dve.wait_ge(d_mm, job * 2 + m + 2)
                        dve.wait_ge(y_mm, job + 1)
                        nc.vector.tensor_scalar(dh[:, m], d_ps[m][:, 0:CW], col_sb[:, e, D1 + m:D1 + m + 1], 0.0, ALU.add, ALU.max
                                                ).then_inc(dh_out, 1)
                    if e:
                        tail(i, e - 1)
                    dve.wait_ge(y_mm, job + 2)
                    nc.vector.tensor_scalar(x_sb[:, e % 2], y_ps[:, 0:CW], col_sb[:, e, D2:D2 + 1], None, ALU.add
                                            ).then_inc(x_out, 1)
            trip(0, True)
            with dve.Fori(1, trips) as i:
                trip(i, False)
            sub(trips, -1)
            tail(trips, -1)
            finish(trips)


def stage_retention(nc, n_in, h_in, w_q, w_k, w_v, decay, h_out):
    TT = [(lo, min(lo + P, T)) for lo in range(0, T, P)]
    NT = len(TT)
    OFF = P * (NT - 1)
    with ExitStack() as ctx:
        sems = []
        ctx.callback(end_stage, nc, sems)
        sb = lambda n, shape, dt=F32: ctx.enter_context(nc.sbuf_tensor(f"ret_{n}", shape, dt))

        def sem(n):
            sems.append(nc.alloc_semaphore(f"ret_{n}"))
            return sems[-1]

        w_sb = sb("w", [P, 3, P])
        dec_sb = sb("dec", [P, OFF + T])
        n_sb = sb("n", [P, B, T])
        h_sb = sb("h", [P, B, T])
        qk = sb("qk", [P, 2, T])
        v_sb = sb("v", [P, NT, P])
        sd = sb("sd", [P, 2, T])
        sg = sb("sg", [P, 2, T])
        a_sb = sb("a", [P, 2, T])
        s_ps = [ctx.enter_context(nc.psum_tensor(f"ret_s_ps{k}", [P, 2 * BANK], F32)) for k in range(2)]
        o_ps = ctx.enter_context(nc.psum_tensor("ret_o_ps", [P, 2 * BANK], F32))
        v_ps = [ctx.enter_context(nc.psum_tensor(f"ret_v_ps{k}", [P, BANK], F32)) for k in range(2)]
        w_loaded = sem("w_loaded")
        loaded = [sem(f"loaded{b}") for b in range(B)]
        qk_mm, qk_out, v_mm, v_out = sem("qk_mm"), sem("qk_out"), sem("v_mm"), sem("v_out")
        s_mm, sd_done, sg_done, a_done, o_mm = sem("s_mm"), sem("sd_done"), sem("sg_done"), sem("a_done"), sem("o_mm")
        ready, stored = sem("ready"), sem("stored")
        block = ctx.enter_context(nc.Block())

        @block.sync
        def _(sp):
            for n, w in enumerate((w_q, w_k, w_v)):
                sp.dma_start(w_sb[:, n], w).then_inc(w_loaded, 16)
            sp.dma_start(dec_sb[:], decay).then_inc(w_loaded, 16)
            for b in range(B):
                sp.dma_start(n_sb[:, b], n_in[:, b]).then_inc(loaded[b], 16)
                sp.dma_start(h_sb[:, b], h_in[:, b]).then_inc(loaded[b], 16)
            for b in range(B):
                sp.wait_ge(ready, b + 1)
                sp.dma_start(h_out[:, b], h_sb[:, b]).then_inc(stored, 16)
            sp.wait_ge(stored, 16 * B)

        @block.tensor
        def _(pe):
            pe.wait_ge(w_loaded, 64)
            for b in range(B):
                pe.wait_ge(loaded[b], 32)
                for n in range(2):
                    if b:
                        pe.wait_ge(sd_done, NT * b)
                    for lo, hi in COLS_OF:
                        mm = nc.tensor.matmul(s_ps[n][:, lo:hi], w_sb[:, n], n_sb[:, b, lo:hi], start=True, stop=True)
                    mm.then_inc(qk_mm, 1)
                for c, (lo, hi) in enumerate(TT):
                    if NT * b + c >= 2:
                        pe.wait_ge(v_out, NT * b + c - 1)
                    nc.tensor.matmul(v_ps[c % 2][0:hi - lo, 0:P], n_sb[:, b, lo:hi], w_sb[:, 2], start=True, stop=True
                                     ).then_inc(v_mm, 1)
                pe.wait_ge(qk_out, 2 * b + 2)

                def scores(c):
                    if c >= 2:
                        pe.wait_ge(sd_done, NT * b + c - 1)
                    k0, k1 = TT[c]
                    for lo, hi in COLS_OF:
                        mm = nc.tensor.matmul(s_ps[c % 2][0:k1 - k0, lo:hi], qk[:, 1, k0:k1], qk[:, 0, lo:hi], start=True, stop=True)
                    mm.then_inc(s_mm, 1)
                scores(0)
                scores(1)
                pe.wait_ge(v_out, NT * b + NT)
                if b:
                    pe.wait_ge(ready, b)
                for c in range(NT):
                    if c + 2 < NT:
                        scores(c + 2)
                    pe.wait_ge(a_done, NT * b + c + 1)
                    k0, k1 = TT[c]
                    for lo, hi in COLS_OF:
                        mm = nc.tensor.matmul(o_ps[:, lo:hi], v_sb[0:k1 - k0, c], a_sb[0:k1 - k0, c % 2, lo:hi],
                                              start=(c == 0), stop=(c == NT - 1))
                    mm.then_inc(o_mm, 1)

        @block.scalar
        def _(act):
            for b in range(B):
                for n in range(2):
                    act.wait_ge(qk_mm, 2 * b + n + 1)
                    nc.scalar.copy(qk[:, n], s_ps[n][:, 0:T]).then_inc(qk_out, 1)
                for c, (k0, k1) in enumerate(TT):
                    act.wait_ge(sd_done, NT * b + c + 1)
                    if NT * b + c >= 2:
                        act.wait_ge(a_done, NT * b + c - 1)
                    nc.scalar.activation(sg[0:k1 - k0, c % 2], sd[0:k1 - k0, c % 2], ACT.Sigmoid).then_inc(sg_done, 1)

        @block.vector
        def _(dve):
            for b in range(B):
                for c, (lo, hi) in enumerate(TT):
                    dve.wait_ge(v_mm, NT * b + c + 1)
                    if b and c == 0:
                        dve.wait_ge(o_mm, NT * b)
                    nc.vector.tensor_copy(v_sb[0:hi - lo, c], v_ps[c % 2][0:hi - lo, 0:P]).then_inc(v_out, 1)

                def weighted(c):
                    k0, k1 = TT[c]
                    dve.wait_ge(s_mm, NT * b + c + 1)
                    if NT * b + c >= 2:
                        dve.wait_ge(a_done, NT * b + c - 1)
                    at = OFF - P * c
                    nc.vector.tensor_tensor(sd[0:k1 - k0, c % 2], s_ps[c % 2][0:k1 - k0, 0:T], dec_sb[0:k1 - k0, at:at + T], ALU.mult
                                            ).then_inc(sd_done, 1)
                weighted(0)
                for c in range(NT):
                    if c + 1 < NT:
                        weighted(c + 1)
                    k0, k1 = TT[c]
                    dve.wait_ge(sg_done, NT * b + c + 1)
                    if NT * b + c >= 2:
                        dve.wait_ge(o_mm, NT * b + c - 1)
                    nc.vector.tensor_tensor(a_sb[0:k1 - k0, c % 2], sd[0:k1 - k0, c % 2], sg[0:k1 - k0, c % 2], ALU.mult
                                            ).then_inc(a_done, 1)
                dve.wait_ge(o_mm, NT * b + NT)
                nc.vector.tensor_tensor(h_sb[:, b], h_sb[:, b], o_ps[:, 0:T], ALU.add).then_inc(ready, 1)


def stage_softmax_attention(nc, name, q_parts, k_parts, v_aug, o_out, sum_out, units):
    with ExitStack() as ctx:
        sems = []
        ctx.callback(end_stage, nc, sems)
        sb = lambda n, shape, dt=F32: ctx.enter_context(nc.sbuf_tensor(f"{name}_{n}", shape, dt))

        def sem(n):
            sems.append(nc.alloc_semaphore(f"{name}_{n}"))
            return sems[-1]

        ROWS = STACK + MAX_PARTS
        q_sb = sb("q", [ROWS, AHEAD, QUAD, TP], BF16)
        k_sb = sb("k", [ROWS, AHEAD, QUAD, T], BF16)
        v_sb = sb("v", [P, AHEAD, TILES, P])
        probT = sb("probT", [P, 3, QUAD, T])
        negmax = sb("negmax", [P, QUAD * TILES])
        max_parts = sb("max_parts", [P, MAX_PARTS, 32], BF16)
        max_rows = sb("max_rows", [P, MAX_PARTS, 32], BF16)
        u_sb = sb("u", [P, 2, T])
        ring = [ctx.enter_context(nc.psum_tensor(f"{name}_ring{k}", [P, 2 * BANK], F32)) for k in range(3)]
        u_ps = ctx.enter_context(nc.psum_tensor(f"{name}_u_ps", [P, 2 * BANK], F32))

        N = QUAD * TILES
        LEAD = N + 6
        PARTS = ((0, 188), (188, 375), (375, 562), (562, T))
        HALVES = ((0, 375), (375, T))
        loaded = [sem(f"loaded{k}") for k in range(AHEAD)]
        init_done = sem("init_done")
        ones_done = sem("ones_done")
        logit_ready = sem("logit_ready")
        max_ready = sem("max_ready")
        part_done = sem("part_done")
        turned = sem("turned")
        rows_loaded = sem("rows_loaded")
        key_ready = sem("key_ready")
        exp_done = sem("exp_done")
        summed = sem("summed")
        u_copied = sem("u_copied")
        stored = [sem(f"stored{k}") for k in range(2)]

        def put_unit(sp, k, u):
            for parts, src, dst in ((Q_PARTS, q_parts, q_sb), (K_PARTS, k_parts, k_sb)):
                for slot, part in enumerate(parts):
                    sp.dma_start(dst[slot * HD:(slot + 1) * HD, k, :, 0:T],
                                 src[bass.ds(u, 1), part].rearrange("o (h r) t -> r (o h) t", r=HD)
                                 ).then_inc(loaded[k], 16)
            sp.dma_start(v_sb[:, k, 0:TILES - 1], v_aug[bass.ds(u, 1), 0:(TILES - 1) * P].rearrange("o (c p) n -> p (o c) n", p=P)
                         ).then_inc(loaded[k], 16)
            sp.dma_start(v_sb[0:K_SIZE[-1], k, TILES - 1], v_aug[bass.ds(u, 1), (TILES - 1) * P:T].rearrange("o p n -> (o p) n")
                         ).then_inc(loaded[k], 16)
        LOADS = 16 * (2 * len(Q_PARTS) + 2)

        def put_sums(sp, k, u):
            for h in range(QUAD):
                for row, out in ((HROWS * h, o_out), (HROWS * h + HD, sum_out)):
                    sp.dma_start(out[bass.ds(u, 1), h * HD:(h + 1) * HD].rearrange("o r t -> (o r) t"),
                                 u_sb[row:row + HD, k]).then_inc(stored[k], 16)
        STORES = 16 * 2 * QUAD

        def put_rows(sp, k):
            for block32 in range(4):
                for part in range(MAX_PARTS):
                    sp.dma_start(q_sb[STACK + part:STACK + part + 1, k].rearrange("p h (t x) -> p (h t) x", t=TILES)
                                 [:, :, 32 * block32:32 * block32 + 32],
                                 max_rows[32 * block32:32 * block32 + N, part]).then_inc(rows_loaded, 16)
        ROW_LOADS = 16 * 4 * MAX_PARTS

        block = ctx.enter_context(nc.Block())
        trips = units // AHEAD

        def trip_kinds(eng, unit):
            for k in range(AHEAD):
                unit(0, k, True, trips == 1)
            if trips > 2:
                with eng.Fori(1, trips - 1) as i:
                    for k in range(AHEAD):
                        unit(i, k, False, False)
            if trips > 1:
                for k in range(AHEAD):
                    unit(trips - 1, k, False, True)

        @block.sync
        def _(sp):
            for k in range(AHEAD - 1):
                put_unit(sp, k, k)
            sp.wait_ge(turned, 1)
            put_rows(sp, 0)

            def unit(i, k, first, last):
                u = AHEAD * i + k
                before = not (first and k == 0)
                if before:
                    sp.wait_ge(summed, len(PARTS) * TILES * u)
                if not last or k == 0:
                    put_unit(sp, (k + AHEAD - 1) % AHEAD, u + AHEAD - 1)
                if before:
                    sp.wait_ge(u_copied, 2 * u)
                    put_sums(sp, (k + 1) % 2, u - 1)
                if not (last and k == AHEAD - 1):
                    sp.wait_ge(turned, u + 2)
                    put_rows(sp, (k + 1) % AHEAD)
            trip_kinds(sp, unit)
            sp.wait_ge(u_copied, 2 * units)
            put_sums(sp, (units - 1) % 2, units - 1)
            for k in range(2):
                sp.wait_ge(stored[k], STORES * (units // 2))

        def max_job(k, n, last):
            ahead_units, tile = divmod(n + LEAD, N)
            if last and k + ahead_units >= AHEAD:
                return None
            return k + ahead_units, tile

        def logits(pe, k, n, where):
            h, t = divmod(n, TILES)
            for lo, hi in COLS_OF:
                mm = nc.tensor.matmul(where[0:K_SIZE[t], lo:hi], q_sb[0:STACK, k, h, P * t:P * t + K_SIZE[t]],
                                      k_sb[0:STACK, k, h, lo:hi], start=True, stop=True)
            mm.then_inc(logit_ready, 1)

        @block.tensor
        def _(pe):
            for a in range(LEAD):
                if a % N == 0:
                    pe.wait_ge(loaded[a // N], LOADS)
                if a >= 3:
                    pe.wait_ge(max_ready, a - 2)
                logits(pe, a // N, a % N, ring[a % 3])
            pe.wait_ge(max_ready, LEAD)
            pe.wait_ge(ones_done, 1)

            def weigh(k, c, part):
                lo, hi = PARTS[part]
                at = lo + (BANK - HALVES[1][0]) * (part // 2)
                for h in range(QUAD):
                    mm = nc.tensor.matmul(u_ps[HROWS * h:HROWS * (h + 1), at:at + hi - lo],
                                          v_sb[0:K_SIZE[c], k, c, HROWS * h:HROWS * (h + 1)],
                                          probT[0:K_SIZE[c], c % 3, h, lo:hi], start=(c == 0 and part % 2 == 0),
                                          stop=(c == TILES - 1 and part % 2 == 1))
                mm.then_inc(summed, 1)

            def unit(i, k, first, last):
                u = AHEAD * i + k
                g0 = N * u
                for n in range(N):
                    c, h = divmod(n, QUAD)
                    very_first = first and k == 0
                    job, before = max_job(k, n, last), max_job(k, n - 1, last)
                    if job:
                        if not (very_first and n < 2):
                            pe.wait_ge(exp_done, g0 + n - 1)
                        ahead, tile = job
                        if tile == 0:
                            pe.wait_ge(loaded[ahead % AHEAD], LOADS * (i + ahead // AHEAD + 1))
                        logits(pe, ahead % AHEAD, tile, ring[2 * n % 3])
                    key_tile, part = (n - 1) // QUAD - 1, (n - 1) % QUAD
                    if not (very_first and key_tile < 0):
                        if part == 0:
                            pe.wait_ge(exp_done, g0 + QUAD * c)
                        if key_tile == 0 and part % 2 == 0 and not very_first:
                            pe.wait_ge(u_copied, 2 * u - 1 + part // 2)
                        weigh(k if key_tile >= 0 else (k - 1) % AHEAD, key_tile % TILES, part)
                    if n == 0:
                        pe.wait_ge(rows_loaded, ROW_LOADS * (u + 1))
                    if before and not (very_first and n == 0):
                        pe.wait_ge(max_ready, g0 + n + LEAD)
                    elif not before:
                        pe.wait_ge(exp_done, g0 + n - 2)
                    for lo, hi in COLS_OF:
                        mm = nc.tensor.matmul(ring[(2 * n + 1) % 3][0:K_SIZE[c], lo:hi], k_sb[:, k, h, P * c:P * c + K_SIZE[c]],
                                              q_sb[:, k, h, lo:hi], start=True, stop=True)
                    mm.then_inc(key_ready, 1)
            trip_kinds(pe, unit)
            weigh(AHEAD - 1, TILES - 2, len(PARTS) - 1)
            pe.wait_ge(exp_done, N * units)
            for part in range(len(PARTS)):
                weigh(AHEAD - 1, TILES - 1, part)

        @block.gpsimd
        def _(pool):
            nc.gpsimd.memset(k_sb[STACK:ROWS], 1.0).then_inc(ones_done, 1)

        @block.scalar
        def _(act):
            def unit(i, k, first, last):
                u = AHEAD * i + k
                for n in range(N):
                    c, h = divmod(n, QUAD)
                    act.wait_ge(key_ready, N * u + n + 1)
                    if h == 0 and not (first and k == 0 and c < 3):
                        act.wait_ge(summed, len(PARTS) * (TILES * u + c - 2))
                    nc.scalar.activation(probT[0:K_SIZE[c], c % 3, h], ring[(2 * n + 1) % 3][0:K_SIZE[c], 0:T], ACT.Exp
                                         ).then_inc(exp_done, 1)
            trip_kinds(act, unit)

        @block.vector
        def _(dve):
            nc.vector.memset(negmax[:], 0.0)
            nc.vector.memset(max_parts[:], 0.0).then_inc(init_done, 1)
            dve.wait_ge(init_done, 1)

            def maximum(u, n, where):
                t = n % TILES
                dve.wait_ge(logit_ready, N * u + n + 1)
                if n == 0:
                    dve.wait_ge(part_done, 2 * u)
                nc.vector.tensor_reduce(negmax[0:K_SIZE[t], n:n + 1], where[0:K_SIZE[t], 0:T], AX, ALU.max, negate=True
                                        ).then_inc(max_ready, 1)

            def turn_maxima(u):
                dve.wait_ge(max_ready, N * (u + 1))
                nc.vector.tensor_copy(max_parts[:, 0, 0:N], negmax[:]).then_inc(part_done, 1)
                dve.wait_ge(part_done, 2 * u + 1)
                nc.vector.tensor_tensor(max_parts[:, 1, 0:N], negmax[:], max_parts[:, 0, 0:N], ALU.subtract
                                        ).then_inc(part_done, 1)
                dve.wait_ge(part_done, 2 * u + 2)
                dve.wait_ge(rows_loaded, ROW_LOADS * u)
                nc.vector.transpose(max_rows[:].rearrange("p a b -> p (a b)"), max_parts[:].rearrange("p a b -> p (a b)")
                                    ).then_inc(turned, 1)

            def copy_sums(i, k, first, half):
                u = AHEAD * i + k
                lo, hi = HALVES[half]
                dve.wait_ge(summed, len(PARTS) * TILES * (u + 1) - 2 + 2 * half)
                if half == 0 and not (first and k < 2):
                    dve.wait_ge(stored[k % 2], STORES * ((AHEAD // 2) * i + k // 2))
                nc.vector.tensor_copy(u_sb[:, k % 2, lo:hi], u_ps[:, BANK * half:BANK * half + hi - lo]).then_inc(u_copied, 1)

            for a in range(LEAD):
                maximum(a // N, a % N, ring[a % 3])
                if a == N - 1:
                    turn_maxima(0)

            def unit(i, k, first, last):
                u = AHEAD * i + k
                for n in range(N):
                    job = max_job(k, n, last)
                    if job:
                        ahead, tile = job
                        maximum(AHEAD * i + ahead, tile, ring[2 * n % 3])
                        if tile == N - 1:
                            turn_maxima(AHEAD * i + ahead)
                    if n in (3, 5) and not (first and k == 0):
                        if k:
                            copy_sums(i, k - 1, first, n // 4)
                        else:
                            copy_sums(i - 1, AHEAD - 1, False, n // 4)
            trip_kinds(dve, unit)
            for half in range(2):
                copy_sums(trips - 1, AHEAD - 1, False, half)


def stage_topk_attention(nc, name, q_parts, k_parts, v_aug, o_out, sum_out, ident, units):
    with ExitStack() as ctx:
        sems = []
        ctx.callback(end_stage, nc, sems)
        sb = lambda n, shape, dt=F32: ctx.enter_context(nc.sbuf_tensor(f"{name}_{n}", shape, dt))

        def sem(n):
            sems.append(nc.alloc_semaphore(f"{name}_{n}"))
            return sems[-1]

        q_sb = sb("q", [STACK, 2, QUAD, T], BF16)
        k_sb = sb("k", [STACK, 2, QUAD, T], BF16)
        v_sb = sb("v", [P, 2, TILES, P])
        prob = sb("prob", [P, 2, T])
        probT = sb("probT", [P, 2, QUAD, TILES, P])
        negmax = sb("negmax", [P, 2])
        u_sb = sb("u", [P, 2, T])
        id_sb = sb("id", [P, P])
        best = sb("best", [P, 2, 2, 8])
        left = sb("left", [P, 2, T])
        expo = sb("expo", [P, 2, T])
        expo_left = sb("expo_left", [P, 2, T])
        pause = sb("pause", [P, 2, 3])
        s_ps = [ctx.enter_context(nc.psum_tensor(f"{name}_s_ps{k}", [P, 2 * BANK], F32)) for k in range(2)]
        t_ps = [ctx.enter_context(nc.psum_tensor(f"{name}_t_ps{k}", [P, BANK], F32)) for k in range(2)]
        u_ps = ctx.enter_context(nc.psum_tensor(f"{name}_u_ps", [P, BANK], F32))

        const_loaded = sem("const_loaded")
        qkv_loaded = [sem(f"qkv_loaded{k}") for k in range(2)]
        s_ready = sem("s_ready")
        max_ready = sem("max_ready")
        exp_done = sem("exp_done")
        t_ready = [sem(f"t_ready{k}") for k in range(2)]
        t_copied = [sem(f"t_copied{k}") for k in range(2)]
        u_ready = sem("u_ready")
        u_copied = sem("u_copied")
        o_stored = [sem(f"o_stored{k}") for k in range(2)]
        first_done = sem("first_done")
        negmax_done = sem("negmax_done")
        second_done = sem("second_done")
        left_done = sem("left_done")
        exp_left_done = sem("exp_left_done")
        sel_done = sem("sel_done")

        TPU = QUAD * TILES

        def put_stack(sp, k, u):
            for parts, src, dst in ((Q_PARTS, q_parts, q_sb), (K_PARTS, k_parts, k_sb)):
                for slot, part in enumerate(parts):
                    sp.dma_start(dst[slot * HD:(slot + 1) * HD, k],
                                 src[bass.ds(u, 1), part].rearrange("o (h r) t -> r (o h) t", r=HD)
                                 ).then_inc(qkv_loaded[k], 16)
            sp.dma_start(v_sb[:, k, 0:TILES - 1], v_aug[bass.ds(u, 1), 0:(TILES - 1) * P].rearrange("o (c p) n -> p (o c) n", p=P)
                         ).then_inc(qkv_loaded[k], 16)
            sp.dma_start(v_sb[0:K_SIZE[-1], k, TILES - 1], v_aug[bass.ds(u, 1), (TILES - 1) * P:T].rearrange("o p n -> (o p) n")
                         ).then_inc(qkv_loaded[k], 16)
        LOADS = 16 * (2 * len(Q_PARTS) + 2)

        def put_out(sp, k, u):
            for h in range(QUAD):
                for row, out in ((2 * HD * h, o_out), (2 * HD * h + HD, sum_out)):
                    sp.dma_start(out[bass.ds(u, 1), h * HD:(h + 1) * HD].rearrange("o r t -> (o r) t"),
                                 u_sb[row:row + HD, k]).then_inc(o_stored[k], 16)
        STORES = 16 * 2 * QUAD

        start_from_one(nc, (o_stored,))
        block = ctx.enter_context(nc.Block())
        pairs = units // 2

        @block.sync
        def _(sp):
            sp.dma_start(id_sb[:], ident).then_inc(const_loaded, 16)
            for k in range(2):
                put_stack(sp, k, k)
            with sp.Fori(0, pairs - 1) as i:
                for k in range(2):
                    sp.wait_ge(u_ready, TILES * (2 * i + k + 1))
                    put_stack(sp, k, 2 * i + 2 + k)
                    sp.wait_ge(u_copied, TILES * (2 * i + k + 1))
                    put_out(sp, k, 2 * i + k)
            for k in range(2):
                sp.wait_ge(u_copied, TILES * (units - 2 + k + 1))
                put_out(sp, k, units - 2 + k)
            for k in range(2):
                sp.wait_ge(o_stored[k], STORES * pairs + 1)

        @block.tensor
        def _(pe):
            pe.wait_ge(const_loaded, 16)
            with pe.Fori(0, pairs) as i:
                N = 2 * TPU
                base, ubase = i * N, i * (2 * TILES)

                def logits(n):
                    k, (t, h) = n // TPU, divmod(n % TPU, QUAD)
                    if n % TPU == 0:
                        pe.wait_ge(qkv_loaded[k], LOADS * i + LOADS)
                    if n >= 2:
                        pe.wait_ge(exp_done, base + n - 1)
                    for a, b in ((0, BANK), (BANK, T)):
                        mm = nc.tensor.matmul(s_ps[n % 2][:, a:b], q_sb[:, k, h, Q_START[t]:Q_START[t] + P],
                                              k_sb[:, k, h, a:b], start=True, stop=True)
                    mm.then_inc(s_ready, 1)

                def turn(n):
                    pe.wait_ge(sel_done, base + n + 1)
                    for half in range(2):
                        if n >= 1:
                            pe.wait_ge(t_copied[half], base + n)
                        for c in range(3 * half, 3 * half + 3):
                            mm = nc.tensor.transpose(t_ps[half][0:K_SIZE[c], (c - 3 * half) * P:(c - 3 * half + 1) * P],
                                                     prob[:, n % 2, c * P:c * P + K_SIZE[c]], id_sb[:])
                        mm.then_inc(t_ready[half], 1)

                def weigh(m):
                    k, t = divmod(m, TILES)
                    for half in range(2):
                        pe.wait_ge(t_copied[half], base + QUAD * (m + 1))
                    if m >= 1:
                        pe.wait_ge(u_copied, ubase + m)
                    for c in range(TILES):
                        for h in range(QUAD):
                            mm = nc.tensor.matmul(u_ps[32 * h:32 * h + 32, (m % 4) * P:(m % 4 + 1) * P],
                                                  v_sb[0:K_SIZE[c], k, c, 32 * h:32 * h + 32],
                                                  probT[0:K_SIZE[c], m % 2, h, c], start=(c == 0), stop=(c == TILES - 1))
                    mm.then_inc(u_ready, 1)

                logits(0)
                logits(1)
                logits(2)
                for n in range(N):
                    if n + 3 < N:
                        logits(n + 3)
                    turn(n)
                    if n % QUAD == 1 and n > QUAD:
                        weigh(n // QUAD - 1)
                weigh(2 * TILES - 1)
                pe.wait_ge(exp_done, base + N)
                for half in range(2):
                    pe.wait_ge(t_copied[half], base + N)
                pe.wait_ge(u_copied, ubase + 2 * TILES)

        @block.gpsimd
        def _(pool):
            with pool.Fori(0, pairs) as i:
                N = 2 * TPU
                base = i * N
                for n in range(N):
                    pool.wait_ge(exp_left_done, base + n + 1)
                    pool.wait_ge(exp_done, base + n + 1)
                    if n >= 2:
                        for half in range(2):
                            pool.wait_ge(t_ready[half], base + n - 1)
                    nc.gpsimd.tensor_tensor(prob[:, n % 2], expo[:, n % 2], expo_left[:, n % 2], ALU.subtract).then_inc(sel_done, 1)

        @block.scalar
        def _(act):
            with act.Fori(0, pairs) as i:
                N = 2 * TPU
                base, ubase = i * N, i * (2 * TILES)

                def copy_halves(n):
                    t, h = divmod(n, QUAD)
                    act.wait_ge(t_ready[0], base + n + 1)
                    if t >= 2:
                        act.wait_ge(u_ready, ubase + t - 1)
                    nc.scalar.activation(probT[:, t % 2, h, 0:3].rearrange("p c q -> p (c q)"), t_ps[0][:, 0:HALF],
                                         ACT.Copy).then_inc(t_copied[0], 1)
                    act.wait_ge(t_ready[1], base + n + 1)
                    nc.scalar.activation(probT[:, t % 2, h, 3:5].rearrange("p c q -> p (c q)"), t_ps[1][:, 0:2 * P], ACT.Copy)
                    nc.scalar.activation(probT[0:K_SIZE[5], t % 2, h, 5], t_ps[1][0:K_SIZE[5], 2 * P:3 * P], ACT.Copy
                                         ).then_inc(t_copied[1], 1)

                def exp_left(n):
                    act.wait_ge(left_done, base + n + 1)
                    if n >= 2:
                        act.wait_ge(sel_done, base + n - 1)
                    nc.scalar.activation(expo_left[:, n % 2, :], left[:, n % 2, :], ACT.Exp, bias=negmax[:, n % 2:n % 2 + 1]
                                         ).then_inc(exp_left_done, 1)

                for n in range(N):
                    act.wait_ge(s_ready, base + n + 1)
                    act.wait_ge(max_ready, base + n + 1)
                    act.wait_ge(negmax_done, base + n + 1)
                    if n >= 2:
                        act.wait_ge(sel_done, base + n - 1)
                    nc.scalar.activation(expo[:, n % 2, :], s_ps[n % 2][:, 0:T], ACT.Exp, bias=negmax[:, n % 2:n % 2 + 1]
                                         ).then_inc(exp_done, 1)
                    exp_left(n)
                    if n >= 1:
                        copy_halves(n - 1)
                copy_halves(N - 1)

        @block.vector
        def _(dve):
            with dve.Fori(0, pairs) as i:
                N = 2 * TPU
                base, ubase = i * N, i * (2 * TILES)

                def copy_sums(m):
                    k, t = divmod(m, TILES)
                    dve.wait_ge(u_ready, ubase + m + 1)
                    if t == 0:
                        dve.wait_ge(o_stored[k], STORES * i + 1)
                    nc.vector.tensor_copy(u_sb[:, k, Q_START[t]:Q_START[t] + P], u_ps[:, (m % 4) * P:(m % 4 + 1) * P]
                                          ).then_inc(u_copied, 1)

                def first_eight(n):
                    dve.wait_ge(s_ready, base + n + 1)
                    nc.vector.memset(pause[:, n % 2, 0:1], 0.0)
                    nc.vector.max(best[:, n % 2, 0], s_ps[n % 2][:, 0:T]).then_inc(first_done, 1)

                def minus_maximum(n):
                    dve.wait_ge(first_done, base + n + 1)
                    if n >= 2:
                        dve.wait_ge(exp_left_done, base + n - 1)
                    nc.vector.tensor_scalar(negmax[:, n % 2:n % 2 + 1], best[:, n % 2, 0, 0:1], -1.0, None, ALU.mult
                                            ).then_inc(negmax_done, 1)

                first_eight(0)
                minus_maximum(0)
                for n in range(N):
                    nc.vector.match_replace(left[:, n % 2], best[:, n % 2, 0], s_ps[n % 2][:, 0:T], TAKEN
                                            ).then_inc(max_ready, 1)
                    if n + 1 < N:
                        first_eight(n + 1)
                    if n % QUAD == 0 and n > QUAD:
                        copy_sums(n // QUAD - 2)
                    dve.wait_ge(max_ready, base + n + 1)
                    nc.vector.memset(pause[:, n % 2, 1:2], 0.0)
                    nc.vector.max(best[:, n % 2, 1], left[:, n % 2]).then_inc(second_done, 1)
                    if n + 1 < N:
                        minus_maximum(n + 1)
                    dve.wait_ge(second_done, base + n + 1)
                    nc.vector.memset(pause[:, n % 2, 2:3], 0.0)
                    nc.vector.match_replace(left[:, n % 2], best[:, n % 2, 1], left[:, n % 2], TAKEN
                                            ).then_inc(left_done, 1)
                copy_sums(2 * TILES - 2)
                copy_sums(2 * TILES - 1)


def stage_lstm(nc, wh, xw, mem, trips=T // S):
    with ExitStack() as ctx:
        sems = []
        ctx.callback(end_stage, nc, sems)
        sb = lambda name, shape, dt=F32: ctx.enter_context(nc.sbuf_tensor(name, shape, dt))

        def sem(name):
            sems.append(nc.alloc_semaphore(name))
            return sems[-1]

        w_raw = sb("lstm_w_raw", [P, 2 * E, 2, 1024])
        w_hi = sb("lstm_w_hi", [P, 2, E, 2, 1024], F16)
        w_lo = sb("lstm_w_lo", [P, 2, E, 2, 1024], F16)
        w_peak = sb("lstm_w_peak", [P, 2 * E])
        w_max = sb("lstm_w_max", [P, 1])
        w_allmax = sb("lstm_w_allmax", [P, 1])
        w_scale = sb("lstm_w_scale", [P, 1])
        w_inv = sb("lstm_w_inv", [P, 1])
        xw_sb = sb("lstm_xw", [P, 2, E, S, GC])
        hist = sb("lstm_hist", [P, 2, E * 2, S, B])
        h_parts = sb("lstm_h_parts", [P, 2, E, 2, 2, B], F16)
        part_sum = sb("lstm_part_sum", [P, 2, E * GC])
        z_sb = sb("lstm_z", [P, 2, E, GC])
        gate_sb = sb("lstm_gates", [P, 2, E, GC])
        c_sb = sb("lstm_c", [P, 2, E * 8])
        fc_sb = sb("lstm_fc", [P, 2, E * 8])
        ig_sb = sb("lstm_ig", [P, 2, E * 8])
        tc_sb = sb("lstm_tc", [P, 2, E * 8])
        z_ps = [ctx.enter_context(nc.psum_tensor(f"lstm_z_ps{d}", [P, E, 8, 2, B], F32)) for d in range(2)]

        w_loaded = [sem(f"lstm_w_loaded{n}") for n in range(2 * E)]
        w_read = sem("lstm_w_read")
        peak_done = sem("lstm_peak_done")
        allmax_done = sem("lstm_allmax_done")
        scale_step = sem("lstm_scale_step")
        hi_done = sem("lstm_hi_done")
        split_done = sem("lstm_split_done")
        D = 2
        xw_loaded = [[sem(f"lstm_xw_loaded{d}_{k}") for k in range(len(PIECES))] for d in range(D)]
        hist_stored = [[sem(f"lstm_hist_stored{d}_{k}") for k in range(len(PIECES))] for d in range(D)]
        z_ready = [sem(f"lstm_z_ready{d}") for d in range(D)]
        sum_done = [sem(f"lstm_sum_done{d}") for d in range(D)]
        z_done = [sem(f"lstm_z_done{d}") for d in range(D)]
        sig_done = [sem(f"lstm_sig_done{d}") for d in range(D)]
        tanh_done = [sem(f"lstm_tanh_done{d}") for d in range(D)]
        fc_done = [sem(f"lstm_fc_done{d}") for d in range(D)]
        ig_done = [sem(f"lstm_ig_done{d}") for d in range(D)]
        c_done = [sem(f"lstm_c_done{d}") for d in range(D)]
        tc_done = [sem(f"lstm_tc_done{d}") for d in range(D)]
        h_done = [sem(f"lstm_h_done{d}") for d in range(D)]
        h_hi_done = [sem(f"lstm_h_hi_done{d}") for d in range(D)]
        h_lo_done = [sem(f"lstm_h_lo_done{d}") for d in range(D)]
        zero_done = sem("lstm_zero_done")


        def slot(d, j):
            return j if d == 0 else S - 1 - j

        def slots(d, k):
            a, b = PIECES[k]
            return (a, b) if d == 0 else (S - b, S - a)

        def xw_move(eng, d, k, i):
            a, b = slots(d, k)
            start = i * S + a if d == 0 else i * -S + (T - S + a)
            return eng.dma_start(xw_sb[:, d, :, a:b, :],
                                 xw[d].rearrange("e p t g -> p e t g")[:, :, bass.ds(start, b - a), :])

        def hist_move(eng, d, k, i):
            a, b = slots(d, k)
            start = i * S + a if d == 0 else i * -S + (T - S + a)
            return eng.dma_start(mem[d].rearrange("e c p t b -> p (e c) t b")[:, :, bass.ds(start, b - a), :],
                                 hist[:, d, :, a:b, :])

        start_from_one(nc, (hist_stored,))
        block = ctx.enter_context(nc.Block())

        @block.sync
        def _(sp):
            for n in range(2 * E):
                sp.dma_start(w_raw[:, n], wh[n // E][n % E].rearrange("(k p) n -> p k n", p=P)).then_inc(w_loaded[n], 16)
            for d in range(D):
                for k in range(len(PIECES)):
                    xw_move(sp, d, k, 0).then_inc(xw_loaded[d][k], 16)
            with sp.Fori(0, trips - 1) as i:
                for k, (_, last) in enumerate(PIECES):
                    for d in range(D):
                        sp.wait_ge(sum_done[d], i * S + last)
                        xw_move(sp, d, k, i + 1).then_inc(xw_loaded[d][k], 16)
                        sp.wait_ge(h_lo_done[d], i * S + last + 1)
                        hist_move(sp, d, k, i).then_inc(hist_stored[d][k], 16)
            for k, (_, last) in enumerate(PIECES):
                for d in range(D):
                    sp.wait_ge(h_lo_done[d], (trips - 1) * S + last + 1)
                    hist_move(sp, d, k, trips - 1).then_inc(hist_stored[d][k], 16)
            for k in range(len(PIECES)):
                for d in range(D):
                    sp.wait_ge(hist_stored[d][k], 16 * trips + 1)

        @block.gpsimd
        def _(pool):
            pool.wait_ge(peak_done, 1)
            nc.gpsimd.partition_all_reduce(w_allmax[:], w_max[:], P, bass.bass_isa.ReduceOp.max).then_inc(allmax_done, 1)

        @block.tensor
        def _(pe):
            pe.wait_ge(split_done, 2 * E)
            with pe.Fori(0, trips) as i:
                for j in range(S):
                    for d in range(D):
                        pe.wait_ge(h_lo_done[d], i * S + j + 1)
                        for e in range(E):
                            for m in range(8):
                                for n, (k, w) in enumerate(((0, w_hi), (0, w_lo), (1, w_hi), (1, w_lo))):
                                    mm = nc.tensor.matmul(
                                        z_ps[d][:, e, m].rearrange("p q b -> p (q b)"), w[:, d, e, k, COLS[m] * P:(COLS[m] + 1) * P],
                                        h_parts[:, d, e, k].rearrange("p q b -> p (q b)"), start=(n == 0), stop=(n == 3))
                        mm.then_inc(z_ready[d], 1)

        @block.scalar
        def _(act):
            for n in range(2 * E):
                d, e = n // E, n % E
                act.wait_ge(scale_step, 4)
                act.wait_ge(w_loaded[n], 16)
                nc.scalar.activation(w_hi[:, d, e], w_raw[:, n], ACT.Copy, scale=w_inv[:, 0:1]).then_inc(hi_done, 1)
            with act.Fori(0, trips) as i:
                for j in range(S):
                    for d in range(D):
                        step = i * S + j + 1
                        act.wait_ge(z_done[d], step)
                        nc.scalar.activation(gate_sb[:, d, :, 0:24], z_sb[:, d, :, 0:24], ACT.Sigmoid).then_inc(sig_done[d], 1)
                        nc.scalar.activation(gate_sb[:, d, :, 24:32], z_sb[:, d, :, 24:32], ACT.Tanh).then_inc(tanh_done[d], 1)
                        act.wait_ge(c_done[d], step)
                        nc.scalar.activation(tc_sb[:, d], c_sb[:, d], ACT.Tanh).then_inc(tc_done[d], 1)

        @block.vector
        def _(dve):
            for n in range(2 * E):
                dve.wait_ge(w_loaded[n], 16)
                nc.vector.tensor_reduce(w_peak[:, n:n + 1], w_raw[:, n].rearrange("p k n -> p (k n)"), AX, ALU.max,
                                        apply_absolute_value=True).then_inc(w_read, 1)
            dve.wait_ge(w_read, 2 * E)
            nc.vector.tensor_reduce(w_max[:], w_peak[:], AX, ALU.max).then_inc(peak_done, 1)
            dve.wait_ge(allmax_done, 1)
            nc.vector.tensor_scalar(w_scale[:], w_allmax[:], 1e-30, None, ALU.max).then_inc(scale_step, 1)
            dve.wait_ge(scale_step, 1)
            nc.vector.tensor_scalar(w_scale[:].bitcast(mybir.dt.uint32), w_scale[:].bitcast(mybir.dt.uint32), 0x7f800000, None, ALU.bitwise_and).then_inc(scale_step, 1)
            dve.wait_ge(scale_step, 2)
            nc.vector.reciprocal(w_inv[:], w_scale[:]).then_inc(scale_step, 1)
            nc.vector.memset(c_sb[:], 0.0).then_inc(scale_step, 1)
            dve.wait_ge(scale_step, 4)
            for n in range(2 * E):
                d, e = n // E, n % E
                dve.wait_ge(hi_done, n + 1)
                nc.vector.scalar_tensor_tensor(w_lo[:, d, e], w_raw[:, n], w_inv[:, 0:1], w_hi[:, d, e], ALU.mult, ALU.subtract).then_inc(split_done, 1)
            for d in range(D):
                nc.vector.memset(h_parts[:, d], 0.0).then_inc(h_lo_done[d], 1)
            with dve.Fori(0, trips) as i:
                for j in range(S):
                    k = 0 if j < PIECES[0][1] else 1
                    for d in range(D):
                        step = i * S + j + 1
                        s = slot(d, j)
                        hi = h_parts[:, d, :, :, 0].rearrange("p e c b -> p (e c) b")
                        lo = h_parts[:, d, :, :, 1].rearrange("p e c b -> p (e c) b")
                        o_gate = gate_sb[:, d, :, 16:24].rearrange("p e (c b) -> p e c b", c=2)
                        if j == PIECES[k][0]:
                            dve.wait_ge(xw_loaded[d][k], i * 16 + 16)
                            dve.wait_ge(hist_stored[d][k], i * 16 + 1)
                        dve.wait_ge(z_ready[d], step)
                        nc.vector.scalar_tensor_tensor(
                            part_sum[:, d].rearrange("p (e g b) -> p e g b", e=E, g=8), z_ps[d][:, :, :, 0], w_scale[:, 0:1],
                            xw_sb[:, d, :, s].rearrange("p e (g b) -> p e g b", g=8), ALU.mult, ALU.add).then_inc(sum_done[d], 1)
                        dve.wait_ge(sum_done[d], step)
                        nc.vector.scalar_tensor_tensor(
                            z_sb[:, d].rearrange("p e (g b) -> p (e g) b", g=8), z_ps[d][:, :, :, 1].rearrange("p e g b -> p (e g) b"),
                            w_scale[:, 0:1], part_sum[:, d].rearrange("p (n b) -> p n b", b=B), ALU.mult, ALU.add).then_inc(z_done[d], 1)
                        dve.wait_ge(sig_done[d], step)
                        nc.vector.tensor_tensor(fc_sb[:, d].rearrange("p (e x) -> p e x", e=E), gate_sb[:, d, :, 8:16],
                                                c_sb[:, d].rearrange("p (e x) -> p e x", e=E), ALU.mult).then_inc(fc_done[d], 1)
                        dve.wait_ge(tanh_done[d], step)
                        nc.vector.tensor_tensor(ig_sb[:, d].rearrange("p (e x) -> p e x", e=E), gate_sb[:, d, :, 0:8],
                                                gate_sb[:, d, :, 24:32], ALU.mult).then_inc(ig_done[d], 1)
                        dve.wait_ge(ig_done[d], step)
                        nc.vector.tensor_tensor(c_sb[:, d], fc_sb[:, d], ig_sb[:, d], ALU.add).then_inc(c_done[d], 1)
                        dve.wait_ge(tc_done[d], step)
                        h_now = hist[:, d, :, s]
                        tc = tc_sb[:, d].rearrange("p (e c b) -> p e c b", e=E, c=2)
                        nc.vector.tensor_tensor(h_parts[:, d, :, :, 0], o_gate, tc, ALU.mult).then_inc(h_hi_done[d], 1)
                        nc.vector.tensor_tensor(h_now.rearrange("p (e c) b -> p e c b", e=E), o_gate, tc, ALU.mult).then_inc(h_done[d], 1)
                        dve.wait_ge(h_done[d], step)
                        nc.vector.tensor_tensor(lo, h_now, hi, ALU.subtract).then_inc(h_lo_done[d], 1)


def audio_tower(nc, a, out):
    def scratch(name, shape, dt=F32):
        return nc.dram_tensor(f"scratch_{name}", list(shape), dt, kind="Internal").ap()

    def attention(name, src, w, cols, v_bias, experts, heads, scale, top_k=False):
        units = experts * B * heads // QUAD
        q = scratch(f"{name}_q", (units, 3, QUAD * HD, T), BF16)
        k = scratch(f"{name}_k", (units, 3, QUAD * HD, T), BF16)
        v = scratch(f"{name}_v", (units, T, P))
        o = scratch(f"{name}_o", (units, QUAD * HD, T))
        sums = scratch(f"{name}_sums", (units, QUAD * HD, T))
        stage_qkv(nc, f"{name}p", src, w, cols, v_bias, q, k, v, experts, heads, scale)
        if top_k:
            stage_topk_attention(nc, name, q, k, v, o, sums, a["ident"], units)
        else:
            stage_softmax_attention(nc, name, q, k, v, o, sums, units)
        return o, sums

    h0, h1, h2, h3 = (scratch(f"h{n}", (P, B, T)) for n in range(4))
    n0, n1, n2, n3 = (scratch(f"n{n}", (P, B, T)) for n in range(4))
    as_source = lambda n: n.rearrange("(e k p) b t -> e k p b t", e=1, k=1)
    by_batch = lambda pair: [o.rearrange("(b g) r t -> b (g r) t", b=B) for o in pair]
    by_expert = lambda pair: [o.rearrange("(e b g) r t -> e b (g r) t", e=E, b=B) for o in pair]

    stage_tok(nc, a["x"], a["w_tok"], a["b_tok"], h0)
    stage_norm(nc, "norm0", h0, n0)
    o0 = attention("att0", as_source(n0), a["w_qkv0"], a["cols_qkv0"], a["bv0"], 1, 8, 1.0 / 4.0)
    stage_norm(nc, "norm1", h0, n1, *by_batch(o0), a["wo0"], a["cols_o0"], h1)

    enc = scratch("enc", (E, 2, P, B, T))
    stage_encode(nc, n1, a["enc_w1"], a["enc_w2"], a["cols_enc"], enc)
    oe = attention("atte", enc, a["attn_in_w"], a["cols_qkve"], a["bve"], E, 16, 1.0 / 4.0)
    xw = scratch("xw", (2, E, P, T, GC))
    mem = scratch("mem", (2, E, 2, P, T, B))
    stage_lstm_inputs(nc, *by_expert(oe), a["attn_out_w"], (a["wi_f"], a["wi_b"]),
                      a["cols_xw"], xw)
    stage_lstm(nc, (a["wh_f"], a["wh_b"]), xw, mem)
    stage_decode(nc, mem, n1, h1, a["sig_w1"], a["sig_w2"], a["tan_w1"], a["tan_w2"], a["dec_w1"], a["dec_w2"],
                 a["router_w"], a["cols_dec"], h2)

    stage_norm(nc, "norm2", h2, n2)
    stage_retention(nc, n2, h2, a["w_q1"], a["w_k1"], a["w_v1"], a["decay"], h3)
    stage_norm(nc, "norm3", h3, n3, cols=a["cols_o1"], conv=True)
    o1 = attention("att1", as_source(n3), a["w_qkv1"], a["cols_qkv1"], a["bv1"], 1, 8, float(P) ** -0.5, top_k=True)
    stage_norm(nc, "norm4", h3, None, *by_batch(o1), a["wo1"], a["cols_o1"], out)


def kernel(**inputs):
    import numpy as np
    import concourse.bacc as bacc
    from concourse.bass_utils import run_bass_kernel_spmd as run

    g = {k: np.asarray(v) for k, v in inputs.items()}
    ffn = lambda n: g["L0_ffn_" + n]
    columns = lambda v: v.reshape(-1, P).T
    ecolumns = lambda v: v.reshape(E, -1, P).transpose(0, 2, 1)
    zero = np.zeros((P, 1), np.float32)

    off = P * (TILES - 1)
    distance = np.abs(np.arange(P)[:, None] - np.arange(off + T)[None] + off)
    decay = (0.96875 ** distance).astype(np.float32)

    taps = ("L0_tok_W_z", "L0_tok_W_f", "L0_tok_W_o")
    arrays = {
        "x": g["x"].transpose(2, 0, 1),
        "w_tok": np.stack([g[n].transpose(1, 2, 0) for n in taps], axis=1),
        "b_tok": np.stack([g["L0_tok_b_z"], g["L0_tok_b_f"], g["L0_tok_b_o"]], axis=1),
        "w_qkv0": np.concatenate([g["L0_attn_Wqk"], g["L0_attn_Wv"]], axis=1)[None],
        "cols_qkv0": columns(g["L0_attn_bqk"])[None],
        "bv0": g["L0_attn_bv"][None],
        "wo0": g["L0_attn_Wo"],
        "cols_o0": np.concatenate([columns(g["L0_attn_bo"])] + [zero] * 4, axis=1),
        "enc_w1": ffn("enc_w1"), "enc_w2": ffn("enc_w2"),
        "cols_enc": np.concatenate([ecolumns(ffn(n)) for n in ("enc_b1", "enc_b2", "enc_g", "enc_beta")], axis=2),
        "attn_in_w": ffn("attn_in_w"),
        "cols_qkve": ecolumns(ffn("attn_in_b")[:, :2 * D_EXPERT]),
        "bve": ffn("attn_in_b")[:, 2 * D_EXPERT:],
        "attn_out_w": ffn("attn_out_w"),
        "wi_f": ffn("lstm_wi_f"), "wi_b": ffn("lstm_wi_b"), "wh_f": ffn("lstm_wh_f"), "wh_b": ffn("lstm_wh_b"),
        "cols_xw": np.concatenate([ecolumns(ffn(n)) for n in ("attn_out_b", "lstm_b_f", "lstm_b_b")], axis=2),
        "sig_w1": ffn("sig_w1"), "sig_w2": ffn("sig_w2"), "tan_w1": ffn("tan_w1"), "tan_w2": ffn("tan_w2"),
        "dec_w1": ffn("dec_w1"), "dec_w2": ffn("dec_w2"),
        "router_w": ffn("router_w"),
        "cols_dec": np.concatenate(
            [ecolumns(ffn(n)) for n in ("sig_b1", "sig_b2", "tan_b1", "tan_b2", "dec_b1", "dec_b2", "dec_g", "dec_beta")]
            + [np.broadcast_to(ffn("router_b")[:, None, None], (E, P, 1))], axis=2),
        "w_q1": g["L1_attn_W_Q"], "w_k1": g["L1_attn_W_K"], "w_v1": g["L1_attn_W_V"],
        "decay": decay,
        "cols_o1": np.concatenate([columns(g["L1_ffn_wo_b"]), columns(g["L1_ffn_pos_b"]), g["L1_ffn_pos_w"][:, 0]], axis=1),
        "w_qkv1": g["L1_ffn_qkv_w"].T[None],
        "cols_qkv1": columns(g["L1_ffn_qkv_b"][:2 * P])[None],
        "bv1": g["L1_ffn_qkv_b"][None, 2 * P:],
        "wo1": g["L1_ffn_wo_w"].T,
        "ident": np.eye(P, dtype=np.float32),
    }
    nc = bacc.Bacc("TRN2", target_bir_lowering=False, num_devices=1)
    feed, a = {}, {}
    for name, array in arrays.items():
        feed[f"in_{name}"] = np.ascontiguousarray(array)
        a[name] = nc.dram_tensor(f"in_{name}", list(array.shape), mybir.dt.from_np(array.dtype), kind="ExternalInput").ap()
    out = nc.dram_tensor("out", [P, B, T], F32, kind="ExternalOutput").ap()
    audio_tower(nc, a, out)
    r = run(nc, [feed], core_ids=[0])
    return r.results[0]["out"].transpose(1, 2, 0)
```
